# Optimizing a Trainium2 kernel written in Bass

```python
import numpy as np
import jax
import jax.numpy as jnp

def _softmax(x, axis=-1):
    return jax.nn.softmax(x, axis=axis)

def _gelu(x):
    return jax.nn.gelu(x, approximate=True)

def _silu(x):
    return jax.nn.silu(x)

def _sigmoid(x):
    return jax.nn.sigmoid(x)

def _layernorm(x, axis=-1, eps=1e-05):
    m = jnp.mean(x, axis=axis, keepdims=True)
    v = jnp.var(x, axis=axis, keepdims=True)
    return (x - m) / jnp.sqrt(v + eps)

def _scatter_add(tgt, idx, src, axis=0):
    return tgt.at[idx].add(src)

def _segment_sum(src, seg, n):
    return jax.ops.segment_sum(src, seg, n)
kernel_name = 'mk_gnn_preln_d2_gnn_r32_3143df'

def setup_inputs(seed: int=0):
    np.random.seed(seed)
    _w = jnp.asarray

    def _rec_inputs():
        import jax
        import jax.numpy as jnp
        _gk = jax.random.key(seed)
        x = -0.0005121 + 1.001 * jax.random.normal(jax.random.fold_in(_gk, 1), (3125, 64), jnp.float32)
        _s = jax.random.randint(jax.random.fold_in(_gk, 2), (50000,), 0, 3125, jnp.int32)
        _d = jax.random.randint(jax.random.fold_in(_gk, 3), (50000,), 0, 3125, jnp.int32)
        _loop = jnp.arange(3125, dtype=jnp.int32)
        src = jnp.concatenate([_s, _d, _loop])
        dst = jnp.concatenate([_d, _s, _loop])
        _o = jnp.argsort(dst, stable=True)
        src = src[_o]
        dst = dst[_o]
        edge_attr_64 = 1.36993e-05 + 0.999972 * jax.random.normal(jax.random.fold_in(_gk, 12), (103125, 64), jnp.float32)
        edge_attr_9 = 0.000739051 + 0.999958 * jax.random.normal(jax.random.fold_in(_gk, 13), (103125, 9), jnp.float32)
        return (x, src, dst, edge_attr_64, edge_attr_9)
    x, src, dst, edge_attr_64, edge_attr_9 = _rec_inputs()

    def _L0_gnn_setup():
        import jax, jax.numpy as jnp
        import numpy as np
        N = 50000
        E = 25000
        IN = 64
        H = 4
        D = 16
        OH = H * D
        SCALE = float(np.sqrt(IN))
        LN_EPS = 1e-05
        key = jax.random.key(seed)
        ks = jax.random.split(key, 16)
        w = 0.05
        return {'feats': jax.random.normal(ks[0], (N, IN), jnp.float32), 'Wq': jax.random.normal(ks[1], (IN, OH), jnp.float32) * w, 'bq': jnp.zeros((OH,), jnp.float32), 'Wk': jax.random.normal(ks[2], (IN, OH), jnp.float32) * w, 'bk': jnp.zeros((OH,), jnp.float32), 'Wv': jax.random.normal(ks[3], (IN, OH), jnp.float32) * w, 'bv': jnp.zeros((OH,), jnp.float32), 'Wo': jax.random.normal(ks[4], (OH, OH), jnp.float32) * w, 'bo': jnp.zeros((OH,), jnp.float32), 'Wf': jax.random.normal(ks[5], (IN, OH), jnp.float32) * w, 'bf': jnp.zeros((OH,), jnp.float32), 'gamma': jnp.ones((OH,), jnp.float32), 'beta': jnp.zeros((OH,), jnp.float32), 'src': jax.random.randint(ks[6], (E,), 0, N, jnp.int32), 'dst': jax.random.randint(ks[7], (E,), 0, N, jnp.int32)}
    _L0_gnn_all = _L0_gnn_setup()
    _L0_gnn_in = {k: v for k, v in _L0_gnn_all.items() if k in ('Wq', 'bq', 'Wk', 'bk', 'Wv', 'bv', 'Wo', 'bo', 'Wf', 'bf', 'gamma', 'beta')}
    del _L0_gnn_all

    def _L1_gnn_setup():
        import jax, jax.numpy as jnp
        import numpy as np
        N, E = (10000, 10000)
        D, S, HE = (64, 9, 64)
        H, DQK, DV = (8, 16, 16)
        OK, OV = (H * DQK, H * DV)
        EPS_BN = 1e-05

        def tensor_product(x_e, sh, w, C):
            acc = sh[:, 0:1] * (x_e @ C[:, 0, :])
            for s in range(1, S):
                acc = acc + sh[:, s:s + 1] * (x_e @ C[:, s, :])
            return acc * w

        def mlp2(x, w1, b1, w2, b2):
            return jax.nn.relu(x @ w1 + b1) @ w2 + b2
        key = jax.random.key(seed)
        ks = jax.random.split(key, 20)
        g = lambda k, shape, fan: jax.random.normal(k, shape, jnp.float32) / np.float32(np.sqrt(fan))
        return {'tfn_features': jax.random.normal(ks[0], (N, D), jnp.float32), 'edge_features': jax.random.normal(ks[1], (E, HE), jnp.float32), 'edge_sh': jax.random.normal(ks[2], (E, S), jnp.float32), 'Wq': g(ks[3], (D, OK), D), 'Cqk': g(ks[4], (D, S, OK), D * S), 'Cv': g(ks[5], (D, S, OV), D * S), 'k_w1': g(ks[6], (HE, HE), HE), 'k_b1': jnp.zeros((HE,), jnp.float32), 'k_w2': g(ks[7], (HE, OK), HE), 'k_b2': jnp.zeros((OK,), jnp.float32), 'v_w1': g(ks[8], (HE, HE), HE), 'v_b1': jnp.zeros((HE,), jnp.float32), 'v_w2': g(ks[9], (HE, OV), HE), 'v_b2': jnp.zeros((OV,), jnp.float32), 'W_out': g(ks[10], (OV, D), OV), 'W_self': g(ks[11], (D, D), D), 'gamma': jnp.ones((D,), jnp.float32), 'beta': jnp.zeros((D,), jnp.float32), 'edge_index': jax.random.randint(ks[12], (2, E), 0, N, dtype=jnp.int32)}
    _L1_gnn_all = _L1_gnn_setup()
    _L1_gnn_in = {k: v for k, v in _L1_gnn_all.items() if k in ('Wq', 'Cqk', 'Cv', 'k_w1', 'k_b1', 'k_w2', 'k_b2', 'v_w1', 'v_b1', 'v_w2', 'v_b2', 'W_out', 'W_self', 'gamma', 'beta')}
    del _L1_gnn_all
    return {'x': x, 'src': src, 'dst': dst, 'edge_attr_64': edge_attr_64, 'edge_attr_9': edge_attr_9, 'L0_gnn_Wq': _L0_gnn_in['Wq'], 'L0_gnn_bq': _L0_gnn_in['bq'], 'L0_gnn_Wk': _L0_gnn_in['Wk'], 'L0_gnn_bk': _L0_gnn_in['bk'], 'L0_gnn_Wv': _L0_gnn_in['Wv'], 'L0_gnn_bv': _L0_gnn_in['bv'], 'L0_gnn_Wo': _L0_gnn_in['Wo'], 'L0_gnn_bo': _L0_gnn_in['bo'], 'L0_gnn_Wf': _L0_gnn_in['Wf'], 'L0_gnn_bf': _L0_gnn_in['bf'], 'L0_gnn_gamma': _L0_gnn_in['gamma'], 'L0_gnn_beta': _L0_gnn_in['beta'], 'L1_gnn_Wq': _L1_gnn_in['Wq'], 'L1_gnn_Cqk': _L1_gnn_in['Cqk'], 'L1_gnn_Cv': _L1_gnn_in['Cv'], 'L1_gnn_k_w1': _L1_gnn_in['k_w1'], 'L1_gnn_k_b1': _L1_gnn_in['k_b1'], 'L1_gnn_k_w2': _L1_gnn_in['k_w2'], 'L1_gnn_k_b2': _L1_gnn_in['k_b2'], 'L1_gnn_v_w1': _L1_gnn_in['v_w1'], 'L1_gnn_v_b1': _L1_gnn_in['v_b1'], 'L1_gnn_v_w2': _L1_gnn_in['v_w2'], 'L1_gnn_v_b2': _L1_gnn_in['v_b2'], 'L1_gnn_W_out': _L1_gnn_in['W_out'], 'L1_gnn_W_self': _L1_gnn_in['W_self'], 'L1_gnn_gamma': _L1_gnn_in['gamma'], 'L1_gnn_beta': _L1_gnn_in['beta']}

def reference(x, src, dst, edge_attr_64, edge_attr_9, L0_gnn_Wq, L0_gnn_bq, L0_gnn_Wk, L0_gnn_bk, L0_gnn_Wv, L0_gnn_bv, L0_gnn_Wo, L0_gnn_bo, L0_gnn_Wf, L0_gnn_bf, L0_gnn_gamma, L0_gnn_beta, L1_gnn_Wq, L1_gnn_Cqk, L1_gnn_Cv, L1_gnn_k_w1, L1_gnn_k_b1, L1_gnn_k_w2, L1_gnn_k_b2, L1_gnn_v_w1, L1_gnn_v_b1, L1_gnn_v_w2, L1_gnn_v_b2, L1_gnn_W_out, L1_gnn_W_self, L1_gnn_gamma, L1_gnn_beta):
    import jax
    import jax.numpy as jnp

    def _L0_gnn_ref(feats, Wq, bq, Wk, bk, Wv, bv, Wo, bo, Wf, bf, gamma, beta, src, dst):
        import jax, jax.numpy as jnp
        import numpy as np
        N = 50000
        E = 25000
        IN = 64
        H = 4
        D = 16
        OH = H * D
        SCALE = float(np.sqrt(IN))
        LN_EPS = 1e-05
        n = feats.shape[0]
        q = (feats @ Wq + bq).reshape(n, H, D)
        k = (feats @ Wk + bk).reshape(n, H, D)
        v = (feats @ Wv + bv).reshape(n, H, D)
        score = jnp.sum(k[src] * q[dst], axis=-1)
        score = jnp.exp(jnp.clip(score / SCALE, -5.0, 5.0))
        wv = jax.ops.segment_sum(v[src] * score[..., None], dst, num_segments=n)
        z = jax.ops.segment_sum(score, dst, num_segments=n)
        wv = wv / (z[..., None] + 1.0)
        o = wv.reshape(n, OH) @ Wo + bo
        h = feats @ Wf + bf + o
        mu = jnp.mean(h, axis=-1, keepdims=True)
        var = jnp.var(h, axis=-1, keepdims=True)
        ln = (h - mu) * jax.lax.rsqrt(var + LN_EPS) * gamma + beta
        return h + ln

    def _L1_gnn_ref(tfn_features, edge_features, edge_sh, Wq, Cqk, Cv, k_w1, k_b1, k_w2, k_b2, v_w1, v_b1, v_w2, v_b2, W_out, W_self, gamma, beta, edge_index):
        import jax, jax.numpy as jnp
        import numpy as np
        N, E = (10000, 10000)
        D, S, HE = (64, 9, 64)
        H, DQK, DV = (8, 16, 16)
        OK, OV = (H * DQK, H * DV)
        EPS_BN = 1e-05

        def tensor_product(x_e, sh, w, C):
            acc = sh[:, 0:1] * (x_e @ C[:, 0, :])
            for s in range(1, S):
                acc = acc + sh[:, s:s + 1] * (x_e @ C[:, s, :])
            return acc * w

        def mlp2(x, w1, b1, w2, b2):
            return jax.nn.relu(x @ w1 + b1) @ w2 + b2
        edge_dst, edge_src = (edge_index[0], edge_index[1])
        n = tfn_features.shape[0]
        q = (tfn_features @ Wq).reshape(n, H, DQK)
        x_dst = tfn_features[edge_dst]
        wk = mlp2(edge_features, k_w1, k_b1, k_w2, k_b2)
        wv = mlp2(edge_features, v_w1, v_b1, v_w2, v_b2)
        k = tensor_product(x_dst, edge_sh, wk, Cqk).reshape(-1, H, DQK)
        v = tensor_product(x_dst, edge_sh, wv, Cv).reshape(-1, H, DV)
        attn = jnp.einsum('ehd,ehd->eh', q[edge_src], k)
        amax = jax.ops.segment_max(attn, edge_src, num_segments=n)
        ex = jnp.exp(attn - amax[edge_src])
        denom = jax.ops.segment_sum(ex, edge_src, num_segments=n)
        alpha = ex / (denom[edge_src] + 1e-16)
        upd = jax.ops.segment_sum(v * alpha[..., None], edge_src, num_segments=n)
        upd = upd.reshape(n, OV) @ W_out
        out = tfn_features @ W_self + upd
        mu = out.mean(axis=0)
        var = out.var(axis=0)
        return (out - mu) * jax.lax.rsqrt(var + EPS_BN) * gamma + beta
    edge_index = jnp.stack([src, dst])
    h = jnp.maximum(_layernorm(x, axis=-1), 0.0)
    x = x + _L0_gnn_ref(h, L0_gnn_Wq, L0_gnn_bq, L0_gnn_Wk, L0_gnn_bk, L0_gnn_Wv, L0_gnn_bv, L0_gnn_Wo, L0_gnn_bo, L0_gnn_Wf, L0_gnn_bf, L0_gnn_gamma, L0_gnn_beta, src, dst)
    h = jnp.maximum(_layernorm(x, axis=-1), 0.0)
    x = x + _L1_gnn_ref(h, edge_attr_64, edge_attr_9, L1_gnn_Wq, L1_gnn_Cqk, L1_gnn_Cv, L1_gnn_k_w1, L1_gnn_k_b1, L1_gnn_k_w2, L1_gnn_k_b2, L1_gnn_v_w1, L1_gnn_v_b1, L1_gnn_v_w2, L1_gnn_v_b2, L1_gnn_W_out, L1_gnn_W_self, L1_gnn_gamma, L1_gnn_beta, edge_index)
    return x

_drawn_inputs = setup_inputs


def setup_inputs(seed=0):
    import zlib

    import numpy as np

    out = dict(_drawn_inputs(seed))
    spreads = {'L0_gnn_bq': (0.0, 0.8),
     'L0_gnn_bk': (0.0, 0.8),
     'L0_gnn_bv': (0.0, 0.1),
     'L0_gnn_bo': (0.0, 0.1),
     'L0_gnn_bf': (0.0, 0.1),
     'L0_gnn_gamma': (1.0, 0.2),
     'L0_gnn_beta': (0.0, 0.1),
     'L1_gnn_k_b1': (0.0, 0.294),
     'L1_gnn_k_b2': (0.0, 0.1),
     'L1_gnn_v_b1': (0.0, 0.37),
     'L1_gnn_v_b2': (0.0, 0.1),
     'L1_gnn_gamma': (1.0, 0.2),
     'L1_gnn_beta': (0.0, 0.1)}
    factors = {'L0_gnn_Wq': 8.0, 'L0_gnn_Wk': 8.0}
    for name, (base, spread) in spreads.items():
        noise = np.random.default_rng([zlib.crc32(name.encode()), seed]).standard_normal(out[name].shape)
        drawn = base * np.exp(spread * noise) if base else spread * noise
        out[name] = jnp.asarray(drawn.astype(out[name].dtype))
    for name, factor in factors.items():
        out[name] = (out[name] * factor).astype(out[name].dtype)
    return out
```

```python
from contextlib import ExitStack

import concourse.bass as bass
from concourse import mybir
from concourse.alu_op_type import AluOpType as ALU

F32 = mybir.dt.float32
BF16 = mybir.dt.bfloat16
I32 = mybir.dt.int32
ACT = mybir.ActivationFunctionType
AX = mybir.AxisListType

P = 128
N = 3125
D = 64
E = 103125
S = 9
H0, DH = 4, 16
H1 = 8
O1 = H1 * DH
NP, NJ = 125, 25
Q = 4
ST = Q * P
NST = -(-E // ST)
CH = 16
TC = 51
NT = CH * TC
EP = NT * P
U = TC * P
PAD = N
ACCW = 26 * P
BIG = 1.5e38
LN_EPS = BN_EPS = 1e-5
SCALE0, CLIP = 1.0 / 8.0, 5.0
F0 = D + H0 + 1


def need(eng, sem, n):
    if not isinstance(n, int) or n > 0:
        eng.wait_ge(sem, n)


def supertile_loop(eng, body):
    for b in range(2):
        body(0, b, b)
    with eng.Fori(1, NST // 2) as it:
        for b in range(2):
            body(it, it * 2 + b, b)


def pipelined_loop(eng, ahead, body):
    ahead(0, 0, 0)
    for b in range(2):
        ahead((b + 1) // 2, b + 1, (b + 1) % 2)
        body(0, b, b)
    with eng.Fori(1, NST // 2 - 1) as it:
        for b in range(2):
            ahead(it + b, it * 2 + b + 1, (b + 1) % 2)
            body(it, it * 2 + b, b)
    it = NST // 2 - 1
    ahead(it, NST - 1, 1)
    body(it, NST - 2, 0)
    body(it, NST - 1, 1)


class Chain:

    def __init__(self, eng, sem):
        self.eng, self.sem, self.n = eng, sem, 0

    def __call__(self, ins):
        ins.then_inc(self.sem, 1)
        self.n += 1
        self.eng.wait_ge(self.sem, self.n)


def bcast(ap, axis, n):
    ap = ap.unsqueeze(axis)
    shape = list(ap.shape)
    shape[axis] = n
    return ap.broadcast_to(shape)


def gnn(nc, x, src, dst, ea64, ea9, Wq0, bq0, Wk0, bk0, Wv0, bv0, Wo0, bo0, Wf0, bf0, g0, be0,
        Wq1, Cqk, Cv, kw1, kb1, kw2, kb2, vw1, vb1, vw2, vb2, Wout, Wself, g1, be1, out):
    ctx = ExitStack()

    def sb(name, shape, dt=F32, where=None):
        return (where or ctx).enter_context(nc.sbuf_tensor(name, shape, dt))

    def sem(name):
        return ctx.enter_context(nc.semaphore(name))

    def dram(name, shape, dt=F32):
        return nc.dram_tensor(name, shape, dt, kind="Internal").ap()

    with ctx:
        dst_lin = dram("dst_lin", (1 + EP + 1,), I32)
        src_lin = dram("src_lin", (EP,), I32)
        kv0_tab = dram("kv0_tab", (N, 2 * D))
        q0_tab = dram("q0_tab", (N + 1, D))
        wv0_tab = dram("wv0_tab", (N, D))
        h1_tab = dram("h1_tab", (N, D))
        q1_tab = dram("q1_tab", (N + 1, O1))
        upd_tab = dram("upd_tab", (N, D))
        v1_edge = dram("v1_edge", (NST, P, Q * O1))

        bank = [ctx.enter_context(nc.psum_tensor(f"bank{k}", [P, 512], F32)) for k in range(8)]

        ident = sb("ident", [P, P])
        iota_r = sb("iota_r", [P, P])
        W0 = sb("W0", [D + 1, 3 * D])
        WfA = sb("WfA", [D + 1, D])
        WoA = sb("WoA", [D + 1, D])
        Wq1s = sb("Wq1s", [D, O1])
        Wselfs = sb("Wselfs", [D, D])
        Wouts = sb("Wouts", [O1, D])
        W1 = sb("W1", [D, O1])
        b1 = sb("b1", [O1, 1])
        W2 = sb("W2", [O1, 2 * O1])
        b2 = sb("b2", [P, 2 * O1])
        C = sb("C", [P, 5, 2 * O1])
        g0b = sb("g0b", [NP, D])
        be0b = sb("be0b", [NP, D])
        g1b = sb("g1b", [NP, D])
        be1b = sb("be1b", [NP, D])
        src_i = sb("src_i", [P, NT], I32)
        dst_i = sb("dst_i", [P, NT], I32)
        rrel = sb("rrel", [P, NT])
        fdst = sb("fdst", [P, NT])
        base_i = sb("base_i", [1, NT], I32)
        node_i = sb("node_i", [P, NJ], I32)
        xs = sb("xs", [NP, NJ, D])
        hT = sb("hT", [D + 1, NJ * NP])
        acc = sb("acc", [P, ACCW])

        W_SEM = sem("weights_loaded")

        def layer_norm(dve, step, src_ap, cen, sq, st, var_ready, std_ready, k):
            step(dve.tensor_reduce(st[:, 0, :], src_ap, AX.X, ALU.add))
            step(dve.tensor_scalar(st[:, 0, :], st[:, 0, :], 1.0 / D, None, ALU.mult))
            step(dve.tensor_tensor(cen, src_ap, bcast(st[:, 0, :], 2, D), ALU.subtract))
            step(dve.tensor_tensor(sq, cen, cen, ALU.mult))
            step(dve.tensor_reduce(st[:, 1, :], sq, AX.X, ALU.add))
            dve.tensor_scalar(st[:, 1, :], st[:, 1, :], 1.0 / D, LN_EPS, ALU.mult, ALU.add)\
               .then_inc(var_ready, 1)
            dve.wait_ge(std_ready, k)
            step(dve.reciprocal(st[:, 3, :], st[:, 2, :]))
            step(dve.tensor_tensor(cen, cen, bcast(st[:, 3, :], 2, D), ALU.mult))

        def roots(act, st, var_ready, std_ready, k):
            act.wait_ge(var_ready, k)
            nc.scalar.activation(st[:, 2, :], st[:, 1, :], ACT.Sqrt).then_inc(std_ready, 1)

        ph = ExitStack()
        with ph:
            def tsb(name, shape, dt=F32):
                return sb(name, shape, dt, ph)

            upper = tsb("upper", [P, P])
            ones = tsb("ones", [P, P])
            row0 = tsb("row0", [P, P])
            padv = tsb("padv", [1, EP - E + 1], I32)
            zrow = tsb("zrow", [NP, NJ, D])
            dst_r = tsb("dst_r", [P, 7, P], I32)
            prev_r = tsb("prev_r", [P, 7, P], I32)
            src_r = tsb("src_r", [P, 7, P], I32)
            rows_f = tsb("rows_f", [P, 3, 7 * P])
            dst_e = tsb("dst_e", [P, NT])
            prev_e = tsb("prev_e", [P, NT])
            first = tsb("first", [P, NT])
            total = tsb("total", [P, NT])
            cum = tsb("cum", [P, NT])
            onesr = tsb("onesr", [P, NT])
            cen = tsb("cen", [NP, NJ, D])
            sq = tsb("sq", [NP, NJ, D])
            st = tsb("st", [NP, 4, NJ])
            kvq = tsb("kvq", [NP, NJ, 3 * D])
            padi = tsb("padi", [1, EP - E + 1], I32)

            x_in, fills, lin, rows_in = sem("x_in"), sem("fills"), sem("lin"), sem("rows_in")
            consts, poolc, dstep, rows_cast = sem("consts"), sem("poolc"), sem("dstep1"), sem("rows_cast")
            tpose, tpose_out, count_mm = sem("tpose"), sem("tpose_out"), sem("count_mm")
            var1, std1, h_ready = sem("var1"), sem("std1"), sem("h_ready")
            hT_mm, hT_out, proj_mm, proj_out, tabs = (sem("hT_mm"), sem("hT_out"), sem("proj_mm"),
                                                      sem("proj_out"), sem("tabs"))
            pad_sem, w2z, first_ready = sem("pad_sem"), sem("w2z"), sem("first_ready")
            hT_groups = [(a, min(a + 4, NJ)) for a in range(0, NJ, 4)]
            pj_groups = [(a, min(a + 2, NJ)) for a in range(0, NJ, 2)]
            n_weights = 0

            with nc.Block() as block:
                @block.sync
                def _(sp):
                    nonlocal n_weights
                    sp.dma_start(xs[:, :, :], x.rearrange("(p j) d -> p j d", j=NJ)).then_inc(x_in, 16)
                    sp.dma_start(dst_lin[1:1 + E].unsqueeze(0), dst.unsqueeze(0)).then_inc(lin, 16)
                    sp.dma_start(src_lin[0:E].unsqueeze(0), src.unsqueeze(0)).then_inc(lin, 16)
                    sp.wait_ge(pad_sem, 4)
                    sp.dma_start(dst_lin[0:1].unsqueeze(0), padv[:, 0:1]).then_inc(lin, 16)
                    sp.dma_start(dst_lin[1 + E:2 + EP].unsqueeze(0), padi[:, :]).then_inc(lin, 16)
                    sp.dma_start(src_lin[E:EP].unsqueeze(0), padv[:, 1:1 + EP - E]).then_inc(lin, 16)
                    sp.wait_ge(lin, 80)
                    for n, (rows, lo, tab) in enumerate(((dst_r, 1, dst_lin), (prev_r, 0, dst_lin),
                                                         (src_r, 0, src_lin))):
                        t6 = 6 * P * P
                        sp.dma_start(rows[:, 0:6, :], tab[lo:lo + t6].rearrange(
                            "(g t p) -> t g p", g=6, t=P)).then_inc(rows_in, 16)
                        sp.dma_start(rows[0:NT - 6 * P, 6, :], tab[lo + t6:lo + EP].rearrange(
                            "(t p) -> t p", p=P)).then_inc(rows_in, 16)
                    sp.wait_ge(fills, 1)
                    sp.dma_start(q0_tab[N:N + 1, :], zrow[0:1, 0, :]).then_inc(tabs, 16)
                    sp.dma_start(q1_tab[N:N + 1, :], zrow[0:1, 0:2, :].rearrange("p a d -> p (a d)"))\
                      .then_inc(tabs, 16)
                    sp.dma_start(wv0_tab.rearrange("(p j) d -> p j d", j=NJ), zrow[:, :, :]).then_inc(tabs, 16)
                    sp.dma_start(upd_tab.rearrange("(p j) d -> p j d", j=NJ), zrow[:, :, :]).then_inc(tabs, 16)
                    sp.wait_ge(proj_out, len(pj_groups))
                    sp.dma_start(kv0_tab.rearrange("(p j) d -> p j d", j=NJ), kvq[:, :, 0:2 * D]).then_inc(tabs, 16)
                    sp.dma_start(q0_tab[0:N, :].rearrange("(p j) d -> p j d", j=NJ),
                                 kvq[:, :, 2 * D:3 * D]).then_inc(tabs, 16)
                    sp.wait_ge(tabs, 96)
                    sp.wait_ge(rows_in, 96)

                @block.scalar
                def _(act):
                    nonlocal n_weights
                    act.wait_ge(w2z, 1)
                    loads = [(W0[0:D, 0:D], Wk0), (W0[0:D, D:2 * D], Wv0), (W0[0:D, 2 * D:3 * D], Wq0),
                             (W0[D:D + 1, 0:D], bk0.unsqueeze(0)), (W0[D:D + 1, D:2 * D], bv0.unsqueeze(0)),
                             (W0[D:D + 1, 2 * D:3 * D], bq0.unsqueeze(0)),
                             (WfA[0:D, :], Wf0), (WfA[D:D + 1, :], bf0.unsqueeze(0)),
                             (WoA[0:D, :], Wo0), (WoA[D:D + 1, :], bo0.unsqueeze(0)),
                             (Wq1s[:, :], Wq1), (Wselfs[:, :], Wself), (Wouts[:, :], Wout),
                             (W1[:, 0:D], kw1), (W1[:, D:O1], vw1),
                             (b1[0:D, :], kb1.unsqueeze(1)), (b1[D:O1, :], vb1.unsqueeze(1)),
                             (W2[0:D, 0:O1], kw2), (W2[D:O1, O1:2 * O1], vw2),
                             (b2[:, 0:O1], kb2.unsqueeze(0).broadcast_to([P, O1])),
                             (b2[:, O1:2 * O1], vb2.unsqueeze(0).broadcast_to([P, O1]))]
                    for s in range(S):
                        r = D * (s % 2)
                        loads += [(C[r:r + D, s // 2, 0:O1], Cqk[:, s, :]),
                                  (C[r:r + D, s // 2, O1:2 * O1], Cv[:, s, :])]
                    for dst_t, v in ((g0b, g0), (be0b, be0), (g1b, g1), (be1b, be1)):
                        loads.append((dst_t[:, :], v.unsqueeze(0).broadcast_to([NP, D])))
                    for a, b in loads:
                        act.dma_start(a, b).then_inc(W_SEM, 16)
                    n_weights = 16 * len(loads)
                    roots(act, st, var1, std1, 1)
                    for n in range(3):
                        for half in range(2):
                            act.wait_ge(tpose, 2 * n + half + 1)
                            w = 512 if half == 0 else NT - 512
                            dest = (dst_e, prev_e, src_i)[n]
                            nc.scalar.activation(dest[:, 512 * half:512 * half + w],
                                                 bank[2 * (n % 2) + half][:, 0:w], ACT.Copy).then_inc(tpose_out, 1)
                    for g, (a, b) in enumerate(hT_groups):
                        act.wait_ge(hT_mm, g + 1)
                        nc.scalar.activation(hT[0:D, a * NP:b * NP], bank[4 + g % 2][0:D, 0:(b - a) * NP],
                                             ACT.Copy).then_inc(hT_out, 1)
                    for g, (a, b) in enumerate(pj_groups):
                        act.wait_ge(proj_mm, g + 1)
                        nc.scalar.activation(kvq[:, a:b, :].rearrange("p a d -> p (a d)"),
                                             bank[6 + g % 2][0:NP, 0:(b - a) * 3 * D], ACT.Copy).then_inc(proj_out, 1)
                    act.wait_ge(W_SEM, n_weights)

                @block.gpsimd
                def _(pool):
                    pool.memset(padv[:, 1:], 0).then_inc(pad_sem, 1)
                    pool.memset(padv[:, 0:1], -1).then_inc(pad_sem, 1)
                    pool.memset(padi[:, 0:EP - E], PAD).then_inc(pad_sem, 1)
                    pool.memset(padi[:, EP - E:], PAD + 1).then_inc(pad_sem, 1)
                    pool.memset(zrow[:, :, :], 0.0).then_inc(fills, 1)
                    pool.memset(W2[:, :], 0.0).then_inc(w2z, 1)
                    pool.memset(ident[:, :], 0.0).then_inc(poolc, 1)
                    pool.memset(upper[:, :], 1.0).then_inc(poolc, 1)
                    pool.memset(row0[:, :], 0.0).then_inc(poolc, 1)
                    pool.wait_ge(poolc, 3)
                    pool.affine_select(out=ident[:, :], in_=ident[:, :], compare_op=ALU.not_equal, fill=1.0,
                                       base=0, pattern=[[-1, P]], channel_multiplier=1).then_inc(consts, 1)
                    pool.affine_select(out=upper[:, :], in_=upper[:, :], compare_op=ALU.is_ge, fill=0.0,
                                       base=0, pattern=[[1, P]], channel_multiplier=-1).then_inc(consts, 1)
                    pool.memset(row0[0:1, :], 1.0).then_inc(consts, 1)
                    pool.memset(ones[:, :], 1.0).then_inc(consts, 1)
                    pool.iota(iota_r[:, :], [[1, P]], base=0, channel_multiplier=0,
                              allow_small_or_imprecise_dtypes=True).then_inc(consts, 1)
                    pool.wait_ge(consts, 5)
                    pool.memset(hT[D:D + 1, :], 1.0).then_inc(consts, 1)
                    pool.wait_ge(consts, 6)
                    pool.memset(acc[:, :], 0.0).then_inc(consts, 1)
                    pool.memset(onesr[:, :], 1.0).then_inc(consts, 1)

                @block.vector
                def _(dve):
                    step = Chain(dve, dstep)
                    dve.wait_ge(x_in, 16)
                    layer_norm(dve, step, xs[:, :, :], cen[:, :, :], sq[:, :, :], st, var1, std1, 1)
                    dve.tensor_scalar(cen[:, :, :], cen[:, :, :], 0.0, None, ALU.max).then_inc(h_ready, 1)
                    dve.wait_ge(rows_in, 96)
                    for n, rows in enumerate((dst_r, prev_r, src_r)):
                        dve.tensor_copy(rows_f[:, n, 0:6 * P], rows[:, 0:6, :].rearrange("t g p -> t (g p)"))\
                           .then_inc(rows_cast, 1)
                        dve.tensor_copy(rows_f[0:NT - 6 * P, n, 6 * P:7 * P], rows[0:NT - 6 * P, 6, :])\
                           .then_inc(rows_cast, 1)
                    dve.wait_ge(tpose_out, 4)
                    dve.wait_ge(consts, 8)
                    step(dve.tensor_tensor(first[:, :], dst_e[:, :], prev_e[:, :], ALU.not_equal))
                    dve.tensor_copy(dst_i[:, :], dst_e[:, :]).then_inc(first_ready, 1)
                    step(dve.tensor_scalar(dst_e[:, :], dst_e[:, :], 1.0, None, ALU.add))
                    step(dve.tensor_tensor(fdst[:, :], dst_e[:, :], first[:, :], ALU.mult))
                    dve.wait_ge(count_mm, 6)
                    for half in range(2):
                        w = 512 if half == 0 else NT - 512
                        c = slice(512 * half, 512 * half + w)
                        step(dve.tensor_copy(prev_e[:, c], bank[4 + half][:, 0:w]))
                        step(dve.tensor_tensor(rrel[:, c], bank[half][:, 0:w], prev_e[:, c], ALU.subtract))
                        step(dve.tensor_copy(total[:, c], bank[2 + half][:, 0:w]))
                    step(dve.tensor_tensor_scan(cum[:, :], onesr[:, :], total[:, :], -1.0, ALU.mult, ALU.add))
                    step(dve.tensor_tensor(cum[:, :], cum[:, :], total[:, :], ALU.subtract))
                    step(dve.tensor_tensor(cum[:, :], cum[:, :], prev_e[:, :], ALU.add))
                    step(dve.tensor_copy(base_i[0:1, :], cum[0:1, :]))

                @block.tensor
                def _(pe):
                    pe.wait_ge(consts, 8)
                    for n in range(3):
                        pe.wait_ge(rows_cast, 2 * n + 2)
                        if n == 2:
                            pe.wait_ge(tpose_out, 2)
                        for g in range(7):
                            rows = P if g < 6 else NT - 6 * P
                            b = bank[2 * (n % 2) + g // 4]
                            ins = nc.tensor.transpose(b[:, (g % 4) * P:(g % 4) * P + rows],
                                                      rows_f[0:rows, n, g * P:(g + 1) * P], ident[0:rows, 0:rows])
                            if g in (3, 6):
                                ins.then_inc(tpose, 1)
                    pe.wait_ge(h_ready, 1)
                    for g, (a, b) in enumerate(hT_groups):
                        if g >= 2:
                            pe.wait_ge(hT_out, g - 1)
                        for j in range(a, b):
                            ins = nc.tensor.transpose(bank[4 + g % 2][0:D, (j - a) * NP:(j - a + 1) * NP],
                                                      cen[:, j, :], ident[0:NP, 0:NP])
                        ins.then_inc(hT_mm, 1)
                    pe.wait_ge(hT_out, len(hT_groups))
                    pe.wait_ge(W_SEM, n_weights)
                    for g, (a, b) in enumerate(pj_groups):
                        if g >= 2:
                            pe.wait_ge(proj_out, g - 1)
                        for j in range(a, b):
                            ins = nc.tensor.matmul(bank[6 + g % 2][0:NP, (j - a) * 3 * D:(j - a + 1) * 3 * D],
                                                   hT[:, j * NP:(j + 1) * NP], W0[:, :], start=True, stop=True)
                        ins.then_inc(proj_mm, 1)
                    pe.wait_ge(first_ready, 1)
                    pe.wait_ge(tpose_out, 6)
                    for n, w_t in enumerate((upper, ones, row0)):
                        for half in range(2):
                            w = 512 if half == 0 else NT - 512
                            nc.tensor.matmul(bank[2 * n + half][:, 0:w], w_t[:, :],
                                             first[:, 512 * half:512 * half + w], start=True, stop=True)\
                                     .then_inc(count_mm, 1)

        ph = ExitStack()
        with ph:
            kv = [sb(f"kv{b}", [P, Q, 2 * D], F32, ph) for b in range(2)]
            qd = [sb(f"qd{b}", [P, Q, D], F32, ph) for b in range(2)]
            idx = [sb(f"idx{b}", [P, 2, Q], I32, ph) for b in range(2)]
            prod = sb("prod", [P, Q * D], F32, ph)
            sc = sb("sc", [P, Q, H0], F32, ph)
            feat = [sb(f"feat{b}", [P, Q, F0], F32, ph) for b in range(2)]
            hot = [sb(f"hot{b}", [P, Q, P], F32, ph) for b in range(2)]
            idx_copied, idx_turn = sem("idx_copied"), sem("idx_turn")
            rows_got = [sem(f"rows_got{b}") for b in range(2)]
            score_ready, exp_done = sem("score_ready"), sem("exp_done")
            feat_ready, win_ready, col_added, d2 = (sem("feat_ready"), sem("win_ready"), sem("col_added"),
                                                    sem("dstep2"))
            K2 = 5

            with nc.Block() as block:
                @block.gpsimd
                def _(pool):
                    def body(it, i, b):
                        need(pool, feat_ready, i - 1)
                        pool.tensor_copy(idx[b][:, 0, :], src_i[:, bass.ds(i * Q, Q)]).then_inc(idx_copied, 1)
                        pool.tensor_copy(idx[b][:, 1, :], dst_i[:, bass.ds(i * Q, Q)]).then_inc(idx_copied, 1)
                        pool.wait_ge(idx_copied, i * 2 + 2)
                        pool.sem_inc(idx_turn, 1)
                        for q in range(Q):
                            for t, tab, k in ((kv[b], kv0_tab, 0), (qd[b], q0_tab, 1)):
                                pool.indirect_dma_start(
                                    t[:, q, :], None, tab,
                                    bass.IndirectOffsetOnAxis(ap=idx[b][:, k, q:q + 1], axis=0))\
                                    .then_inc(rows_got[b], 16)
                    supertile_loop(pool, body)

                @block.scalar
                def _(act):
                    def body(it, i, b):
                        act.wait_ge(score_ready, i + 1)
                        need(act, win_ready, i - 1)
                        nc.scalar.activation(feat[b][:, :, D:D + H0], sc[:, :, :], ACT.Exp).then_inc(exp_done, 1)
                    supertile_loop(act, body)

                @block.vector
                def _(dve):
                    def body(it, i, b):
                        n = i * K2
                        bases = [dve.value_load(base_i[0:1, bass.ds(i * Q + q, 1)], min_val=0, max_val=N)
                                 for q in range(Q)]
                        need(dve, win_ready, i - 1)
                        dve.tensor_tensor(hot[b][:, :, :], bcast(iota_r[:, :], 1, Q),
                                          bcast(rrel[:, bass.ds(i * Q, Q)], 2, P), ALU.is_equal).then_inc(d2, 1)
                        dve.tensor_copy(feat[b][:, :, D + H0:F0], fdst[:, bass.ds(i * Q, Q)].unsqueeze(2))\
                           .then_inc(d2, 1)
                        dve.wait_ge(rows_got[b], it * (2 * Q * 16) + 2 * Q * 16)
                        dve.tensor_tensor(prod[:, :].rearrange("p (q d) -> p q d", q=Q), kv[b][:, :, 0:D],
                                          qd[b][:, :, :], ALU.mult).then_inc(d2, 1)
                        dve.wait_ge(d2, n + 3)
                        need(dve, exp_done, i)
                        dve.tensor_reduce(sc[:, :, :].rearrange("p q h -> p (q h)"),
                                          prod[:, :].rearrange("p (g d) -> p g d", d=DH), AX.X, ALU.add)\
                           .then_inc(d2, 1)
                        dve.wait_ge(d2, n + 4)
                        dve.tensor_scalar(sc[:, :, :], sc[:, :, :], SCALE0, -CLIP, ALU.mult, ALU.max).then_inc(d2, 1)
                        dve.wait_ge(d2, n + 5)
                        dve.tensor_scalar(sc[:, :, :], sc[:, :, :], CLIP, None, ALU.min).then_inc(score_ready, 1)
                        dve.wait_ge(exp_done, i + 1)
                        dve.tensor_tensor(
                            feat[b][:, :, 0:D].rearrange("p q (h d) -> p q h d", d=DH),
                            kv[b][:, :, D:2 * D].rearrange("p q (h d) -> p q h d", d=DH),
                            bcast(feat[b][:, :, D:D + H0], 3, DH), ALU.mult).then_inc(feat_ready, 1)
                        dve.wait_ge(win_ready, i + 1)
                        for q in range(Q):
                            need(dve, col_added, i * Q + q)
                            a = acc[0:F0, bass.ds(bases[q], P)]
                            dve.tensor_tensor(a, a, bank[b][0:F0, q * P:(q + 1) * P], ALU.add).then_inc(col_added, 1)
                    supertile_loop(dve, body)

                @block.tensor
                def _(pe):
                    def body(it, i, b):
                        pe.wait_ge(feat_ready, i + 1)
                        need(pe, col_added, (i - 1) * Q)
                        for q in range(Q):
                            ins = nc.tensor.matmul(bank[b][0:F0, q * P:(q + 1) * P], feat[b][:, q, :],
                                                   hot[b][:, q, :], start=True, stop=True)
                        ins.then_inc(win_ready, 1)
                    supertile_loop(pe, body)

        ph = ExitStack()
        with ph:
            cols = sb("cols", [P, NJ, F0], F32, ph)
            wvn = sb("wvn", [P, NJ, D], F32, ph)
            zr = sb("zr", [P, NJ, H0], F32, ph)
            nf = sb("nf", [P, 2, NJ], F32, ph)
            wv = sb("wv", [NP, NJ, D], F32, ph)
            wvT = sb("wvT", [D + 1, NJ * NP], F32, ph)
            hp = sb("hp", [NP, NJ, D], F32, ph)
            cen = sb("cen3", [NP, NJ, D], F32, ph)
            sq = sb("sq3", [NP, NJ, D], F32, ph)
            st = sb("st3", [NP, 4, NJ], F32, ph)
            q1n = sb("q1n", [NP, NJ, O1], F32, ph)
            d3, c_mm, c_out, scat, scat_ready = sem("dstep3"), sem("c_mm"), sem("c_out"), sem("scat"), sem("scat_ready")
            wv_in, t_mm, t_out, o_mm, o_out = sem("wv_in"), sem("t3_mm"), sem("t3_out"), sem("o_mm"), sem("o_out")
            var3, std3, h1_ready, u_mm, u_out = sem("var3"), sem("std3"), sem("h1_ready"), sem("u_mm"), sem("u_out")
            q_mm, q_out, tab3, onesw = sem("q_mm"), sem("q_out"), sem("tab3"), sem("onesw")
            groups4 = [(a, min(a + 4, NJ)) for a in range(0, NJ, 4)]

            with nc.Block() as block:
                @block.gpsimd
                def _(pool):
                    pool.memset(wvT[D:D + 1, :], 1.0).then_inc(onesw, 1)
                    pool.wait_ge(scat_ready, 1)
                    for c in range(NJ):
                        pool.indirect_dma_start(
                            wv0_tab, bass.IndirectOffsetOnAxis(ap=node_i[:, c:c + 1], axis=0), wvn[:, c, :], None,
                            bounds_check=N - 1, oob_is_err=False).then_inc(scat, 16)
                    pool.wait_ge(scat, 16 * NJ)

                @block.sync
                def _(sp):
                    sp.wait_ge(scat, 16 * NJ)
                    sp.dma_start(wv[:, :, :], wv0_tab.rearrange("(p j) d -> p j d", j=NJ)).then_inc(wv_in, 16)
                    sp.wait_ge(h1_ready, 1)
                    sp.dma_start(h1_tab.rearrange("(p j) d -> p j d", j=NJ), cen[:, :, :]).then_inc(tab3, 16)
                    sp.wait_ge(q_out, len(groups4))
                    sp.dma_start(q1_tab[0:N, :].rearrange("(p j) d -> p j d", j=NJ), q1n[:, :, :]).then_inc(tab3, 16)
                    sp.wait_ge(tab3, 32)

                @block.tensor
                def _(pe):
                    for c in range(NJ):
                        g = c // 4
                        if g >= 2 and c % 4 == 0:
                            pe.wait_ge(c_out, g - 1)
                        ins = nc.tensor.transpose(bank[g % 2][:, (c % 4) * F0:(c % 4 + 1) * F0],
                                                  acc[0:F0, c * P:(c + 1) * P], ident[0:F0, 0:F0])
                        if c % 4 == 3 or c == NJ - 1:
                            ins.then_inc(c_mm, 1)
                    pe.wait_ge(wv_in, 16)
                    pe.wait_ge(onesw, 1)
                    for g, (a, b) in enumerate(groups4):
                        if g >= 2:
                            pe.wait_ge(t_out, g - 1)
                        for j in range(a, b):
                            ins = nc.tensor.transpose(bank[2 + g % 2][0:D, (j - a) * NP:(j - a + 1) * NP],
                                                      wv[:, j, :], ident[0:NP, 0:NP])
                        ins.then_inc(t_mm, 1)
                    pe.wait_ge(t_out, len(groups4))
                    for g, (a, b) in enumerate(groups4):
                        if g >= 2:
                            pe.wait_ge(o_out, g - 1)
                        for j in range(a, b):
                            o = bank[4 + g % 2][0:NP, (j - a) * D:(j - a + 1) * D]
                            nc.tensor.matmul(o, hT[:, j * NP:(j + 1) * NP], WfA[:, :], start=True, stop=False)
                            ins = nc.tensor.matmul(o, wvT[:, j * NP:(j + 1) * NP], WoA[:, :], start=False, stop=True)
                        ins.then_inc(o_mm, 1)
                    pe.wait_ge(h1_ready, 1)
                    for g, (a, b) in enumerate(groups4):
                        if g >= 2:
                            pe.wait_ge(u_out, g - 1)
                        for j in range(a, b):
                            ins = nc.tensor.transpose(bank[6 + g % 2][0:D, (j - a) * NP:(j - a + 1) * NP],
                                                      cen[:, j, :], ident[0:NP, 0:NP])
                        ins.then_inc(u_mm, 1)
                    pe.wait_ge(u_out, len(groups4))
                    for g, (a, b) in enumerate(groups4):
                        if g >= 2:
                            pe.wait_ge(q_out, g - 1)
                        for j in range(a, b):
                            ins = nc.tensor.matmul(bank[g % 2][0:NP, (j - a) * O1:(j - a + 1) * O1],
                                                   hT[0:D, j * NP:(j + 1) * NP], Wq1s[:, :], start=True, stop=True)
                        ins.then_inc(q_mm, 1)

                @block.scalar
                def _(act):
                    for g, (a, b) in enumerate(groups4):
                        act.wait_ge(c_mm, g + 1)
                        nc.scalar.activation(cols[:, a:b, :].rearrange("p a f -> p (a f)"),
                                             bank[g % 2][:, 0:(b - a) * F0], ACT.Copy).then_inc(c_out, 1)
                    for g, (a, b) in enumerate(groups4):
                        act.wait_ge(t_mm, g + 1)
                        nc.scalar.activation(wvT[0:D, a * NP:b * NP], bank[2 + g % 2][0:D, 0:(b - a) * NP],
                                             ACT.Copy).then_inc(t_out, 1)
                    for g, (a, b) in enumerate(groups4):
                        act.wait_ge(o_mm, g + 1)
                        nc.scalar.activation(hp[:, a:b, :].rearrange("p a d -> p (a d)"),
                                             bank[4 + g % 2][0:NP, 0:(b - a) * D], ACT.Copy).then_inc(o_out, 1)
                    roots(act, st, var3, std3, 1)
                    roots(act, st, var3, std3, 2)
                    for g, (a, b) in enumerate(groups4):
                        act.wait_ge(u_mm, g + 1)
                        nc.scalar.activation(hT[0:D, a * NP:b * NP], bank[6 + g % 2][0:D, 0:(b - a) * NP],
                                             ACT.Copy).then_inc(u_out, 1)
                    for g, (a, b) in enumerate(groups4):
                        act.wait_ge(q_mm, g + 1)
                        nc.scalar.activation(q1n[:, a:b, :].rearrange("p a d -> p (a d)"),
                                             bank[g % 2][0:NP, 0:(b - a) * O1], ACT.Copy).then_inc(q_out, 1)

                @block.vector
                def _(dve):
                    step = Chain(dve, d3)
                    dve.wait_ge(c_out, len(groups4))
                    step(dve.tensor_scalar(zr[:, :, :], cols[:, :, D:D + H0], 1.0, None, ALU.add))
                    step(dve.reciprocal(zr[:, :, :], zr[:, :, :]))
                    for h in range(H0):
                        step(dve.tensor_tensor(wvn[:, :, h * DH:(h + 1) * DH], cols[:, :, h * DH:(h + 1) * DH],
                                               zr[:, :, h:h + 1].broadcast_to([P, NJ, DH]), ALU.mult))
                    num = cols[:, :, D + H0]
                    step(dve.tensor_scalar(nf[:, 0, :], num, 0.0, float(2 * N), ALU.is_equal, ALU.mult))
                    step(dve.tensor_tensor(nf[:, 1, :], nf[:, 0, :], num, ALU.add))
                    step(dve.tensor_scalar(node_i[:, :], nf[:, 1, :], -1.0, None, ALU.add))
                    dve.sem_inc(scat_ready, 1)
                    step(dve.memset(acc[:, :], 0.0))
                    dve.wait_ge(o_out, len(groups4))
                    layer_norm(dve, step, hp[:, :, :], cen[:, :, :], sq[:, :, :], st, var3, std3, 1)
                    step(dve.tensor_tensor(cen[:, :, :], cen[:, :, :], bcast(g0b[:, :], 1, NJ), ALU.mult))
                    step(dve.tensor_tensor(cen[:, :, :], cen[:, :, :], bcast(be0b[:, :], 1, NJ), ALU.add))
                    step(dve.tensor_tensor(hp[:, :, :], hp[:, :, :], cen[:, :, :], ALU.add))
                    step(dve.tensor_tensor(xs[:, :, :], xs[:, :, :], hp[:, :, :], ALU.add))
                    layer_norm(dve, step, xs[:, :, :], cen[:, :, :], sq[:, :, :], st, var3, std3, 2)
                    dve.tensor_scalar(cen[:, :, :], cen[:, :, :], 0.0, None, ALU.max).then_inc(h1_ready, 1)

        attn = sb("attn", [P, NT * H1])
        ph = ExitStack()
        with ph:
            ef = [sb(f"ef{b}", [P, Q, D], F32, ph) for b in range(2)]
            sh = [sb(f"sh{b}", [P, Q, S], F32, ph) for b in range(2)]
            xg = [sb(f"xg{b}", [P, Q, D], F32, ph) for b in range(2)]
            qg = [sb(f"qg{b}", [P, Q, O1], F32, ph) for b in range(2)]
            idx_x = [sb(f"idx_x{b}", [P, Q], I32, ph) for b in range(2)]
            idx_q = [sb(f"idx_q{b}", [P, Q], I32, ph) for b in range(2)]
            z = [sb(f"z{b}", [P, Q, S * D], F32, ph) for b in range(2)]
            zT = [sb(f"zT{b}", [P, 5, Q * P], F32, ph) for b in range(2)]
            efT = sb("efT", [D, Q * P], F32, ph)
            hid = sb("hid", [O1, Q * P], F32, ph)
            wsb = sb("wsb", [P, Q, 2 * O1], F32, ph)
            kvs = [sb(f"kvs{b}", [P, Q, 2 * O1], F32, ph) for b in range(2)]
            kq = sb("kq", [P, Q * O1], F32, ph)
            ef_in = [sem(f"ef_in{b}") for b in range(2)]
            sh_in = [sem(f"sh_in{b}") for b in range(2)]
            x_got = [sem(f"x_got{b}") for b in range(2)]
            q_got = [sem(f"q_got{b}") for b in range(2)]
            v_out = [sem(f"v_out{b}") for b in range(2)]
            idx_x_set, idx_q_set, idy_turn = sem("idx_x_set"), sem("idx_q_set"), sem("idy_turn")
            z_ready, efT_mm, efT_out, hid_mm, hid_out = (sem("z_ready"), sem("efT_mm"), sem("efT_out"),
                                                         sem("hid_mm"), sem("hid_out"))
            zT_mm, zT_out, w_mm, w_out = sem("zT_mm"), sem("zT_out"), sem("w_mm"), sem("w_out")
            a_mm, kv_ready, kq_ready, attn_ready = sem("a_mm"), sem("kv_ready"), sem("kq_ready"), sem("attn_ready")
            pe_turn = sem("pe_turn")
            ROWS = [P] * 4 + [D]
            TAIL = E - (NST - 1) * ST

            with nc.Block() as block:
                @block.sync
                def _(sp):
                    def loads(i, b):
                        need(sp, z_ready, i - 1)
                        need(sp, efT_mm, i - 1)
                        pairs = ((ef[b], ea64, ef_in[b]), (sh[b], ea9, sh_in[b]))
                        if not isinstance(i, int) or i < NST - 1:
                            for t, a, s in pairs:
                                sp.dma_start(t[:, :, :], a[bass.ds(i * ST, ST), :].rearrange(
                                    "(q p) d -> p q d", p=P)).then_inc(s, 16)
                            return
                        lo, q, n = i * ST, TAIL // P, TAIL % P
                        for t, a, s in pairs:
                            sp.dma_start(t[:, 0:q, :], a[lo:lo + q * P, :].rearrange(
                                "(q p) d -> p q d", p=P)).then_inc(s, 16)
                            sp.dma_start(t[0:n, q, :], a[lo + q * P:E, :]).then_inc(s, 16)

                    def store(i, b):
                        sp.wait_ge(kv_ready, i * 2 + 2)
                        sp.dma_start(v1_edge[bass.ds(i, 1)].rearrange("a p (q o) -> p (a q) o", q=Q),
                                     kvs[b][:, :, O1:2 * O1]).then_inc(v_out[b], 16)

                    loads(0, 0)
                    loads(1, 1)
                    for b in range(2):
                        loads(2 + b, b)
                        store(b, b)
                    with sp.Fori(1, NST // 2 - 2) as it:
                        for b in range(2):
                            loads(it * 2 + 2 + b, b)
                            store(it * 2 + b, b)
                    for b in range(2):
                        loads(NST - 2 + b, b)
                        store(NST - 4 + b, b)
                    for b in range(2):
                        store(NST - 2 + b, b)
                    for b in range(2):
                        sp.wait_ge(v_out[b], 16 * (NST // 2))

                @block.gpsimd
                def _(pool):
                    def gather_x(it, i, b):
                        need(pool, z_ready, i - 1)
                        pool.tensor_copy(idx_x[b][:, :], src_i[:, bass.ds(i * Q, Q)]).then_inc(idx_x_set, 1)
                        pool.wait_ge(idx_x_set, i + 1)
                        pool.sem_inc(idy_turn, 1)
                        for q in range(Q):
                            pool.indirect_dma_start(
                                xg[b][:, q, :], None, h1_tab,
                                bass.IndirectOffsetOnAxis(ap=idx_x[b][:, q:q + 1], axis=0)).then_inc(x_got[b], 16)

                    def gather_q(it, i, b):
                        need(pool, kq_ready, i - 1)
                        pool.tensor_copy(idx_q[b][:, :], dst_i[:, bass.ds(i * Q, Q)]).then_inc(idx_q_set, 1)
                        pool.wait_ge(idx_q_set, i + 1)
                        pool.sem_inc(idy_turn, 1)
                        for q in range(Q):
                            pool.indirect_dma_start(
                                qg[b][:, q, :], None, q1_tab,
                                bass.IndirectOffsetOnAxis(ap=idx_q[b][:, q:q + 1], axis=0)).then_inc(q_got[b], 16)

                    pipelined_loop(pool, gather_x, gather_q)

                @block.tensor
                def _(pe):
                    def t_ef(it, i, b):
                        n = 16 * (it + 1)
                        if isinstance(i, int) and i == NST - 1:
                            n += 16
                        pe.wait_ge(ef_in[b], n)
                        need(pe, efT_out, i)
                        pe.sem_inc(pe_turn, 1)
                        for q in range(Q):
                            ins = nc.tensor.transpose(bank[2][0:D, q * P:(q + 1) * P], ef[b][:, q, :], ident[:, :])
                        ins.then_inc(efT_mm, 1)

                    def t_z(i, b, c):
                        if c == 0:
                            pe.wait_ge(z_ready, i + 1)
                        need(pe, zT_out, i * 5 + c - 1)
                        if c == 4:
                            pe.sem_inc(pe_turn, 1)
                        for q in range(Q):
                            ins = nc.tensor.transpose(bank[(c + b) % 2][0:ROWS[c], q * P:(q + 1) * P],
                                                      z[b][:, q, c * P:c * P + ROWS[c]], ident[:, :])
                        ins.then_inc(zT_mm, 1)

                    def m_hid(i):
                        pe.wait_ge(efT_out, i + 1)
                        need(pe, hid_out, i)
                        nc.tensor.matmul(bank[3][:, :], W1[:, :], efT[:, :], start=True, stop=True).then_inc(hid_mm, 1)

                    def m_w(i, half):
                        pe.wait_ge(hid_out, i + 1)
                        need(pe, w_out, i * 2 + half - 1)
                        for r in range(2):
                            q = 2 * half + r
                            ins = nc.tensor.matmul(bank[4 + half][:, r * 2 * O1:(r + 1) * 2 * O1],
                                                   hid[:, q * P:(q + 1) * P], W2[:, :], start=True, stop=True)
                        ins.then_inc(w_mm, 1)

                    def m_acc(i, b, q):
                        pe.wait_ge(zT_out, i * 5 + 5)
                        need(pe, kv_ready, i * 2 + q // 2 - 1)
                        for c in range(5):
                            ins = nc.tensor.matmul(bank[6 + q // 2][:, (q % 2) * 2 * O1:(q % 2 + 1) * 2 * O1],
                                                   zT[b][0:ROWS[c], c, q * P:(q + 1) * P], C[0:ROWS[c], c, :],
                                                   start=(c == 0), stop=(c == 4))
                        if q % 2:
                            ins.then_inc(a_mm, 1)

                    def step(i, b, nit, ni):
                        nb = 1 - b
                        if ni is not None:
                            t_ef(nit, ni, nb)
                            t_z(ni, nb, 0)
                        m_w(i, 0)
                        if ni is not None:
                            t_z(ni, nb, 1)
                        m_w(i, 1)
                        for q in range(Q):
                            if ni is not None and 0 < q:
                                t_z(ni, nb, q + 1)
                            if ni is not None and q == 3:
                                m_hid(ni)
                            m_acc(i, b, q)

                    t_ef(0, 0, 0)
                    for c in range(5):
                        t_z(0, 0, c)
                    m_hid(0)
                    step(0, 0, 0, 1)
                    step(1, 1, 1, 2)
                    with pe.Fori(1, NST // 2 - 1) as it:
                        step(it * 2, 0, it, it * 2 + 1)
                        step(it * 2 + 1, 1, it + 1, it * 2 + 2)
                    step(NST - 2, 0, NST // 2 - 1, NST - 1)
                    step(NST - 1, 1, None, None)

                @block.scalar
                def _(act):
                    def body(it, i, b):
                        act.wait_ge(efT_mm, i + 1)
                        need(act, hid_mm, i)
                        nc.scalar.activation(efT[:, :], bank[2][0:D, :], ACT.Copy).then_inc(efT_out, 1)
                        need(act, a_mm, i * 2 - 2)
                        for c in range(5):
                            act.wait_ge(zT_mm, i * 5 + c + 1)
                            nc.scalar.activation(zT[b][0:ROWS[c], c, :], bank[(c + b) % 2][0:ROWS[c], :], ACT.Copy)\
                                     .then_inc(zT_out, 1)
                        act.wait_ge(hid_mm, i + 1)
                        need(act, w_mm, i * 2)
                        nc.scalar.activation(hid[:, :], bank[3][:, :], ACT.Relu, bias=b1[:, 0:1]).then_inc(hid_out, 1)
                    supertile_loop(act, body)

                @block.vector
                def _(dve):
                    dve.memset(attn[:, NST * Q * H1:], 0.0).then_inc(attn_ready, 1)

                    def outer(it, i, b):
                        dve.wait_ge(x_got[b], 16 * Q * (it + 1))
                        dve.wait_ge(sh_in[b], 16 * (it + 1) + (16 if isinstance(i, int) and i == NST - 1 else 0))
                        need(dve, zT_mm, i * 5 - 5)
                        dve.tensor_tensor(z[b][:, :, :].rearrange("p q (s d) -> p q s d", d=D),
                                          bcast(xg[b][:, :, :], 2, S), bcast(sh[b][:, :, :], 3, D), ALU.mult)\
                           .then_inc(z_ready, 1)

                    def body(it, i, b):
                        for half in range(2):
                            dve.wait_ge(w_mm, i * 2 + half + 1)
                            need(dve, kv_ready, i * 2 + half - 1)
                            dve.tensor_tensor(wsb[:, 2 * half:2 * half + 2, :],
                                              bank[4 + half][:, :].rearrange("p (q o) -> p q o", q=2),
                                              bcast(b2[:, :], 1, 2), ALU.add).then_inc(w_out, 1)
                        need(dve, v_out[b], it * 16)
                        for half in range(2):
                            dve.wait_ge(a_mm, i * 2 + half + 1)
                            dve.wait_ge(w_out, i * 2 + half + 1)
                            dve.tensor_tensor(kvs[b][:, 2 * half:2 * half + 2, :], wsb[:, 2 * half:2 * half + 2, :],
                                              bank[6 + half][:, :].rearrange("p (q o) -> p q o", q=2), ALU.mult)\
                               .then_inc(kv_ready, 1)
                        dve.wait_ge(q_got[b], 16 * Q * (it + 1))
                        dve.wait_ge(kv_ready, i * 2 + 2)
                        dve.wait_ge(attn_ready, i + 1)
                        dve.tensor_tensor(kq[:, :].rearrange("p (q o) -> p q o", q=Q), kvs[b][:, :, 0:O1],
                                          qg[b][:, :, :], ALU.mult).then_inc(kq_ready, 1)
                        dve.wait_ge(kq_ready, i + 1)
                        dve.tensor_reduce(attn[:, bass.ds(i * (Q * H1), Q * H1)],
                                          kq[:, :].rearrange("p (g d) -> p g d", d=DH), AX.X, ALU.add)\
                           .then_inc(attn_ready, 1)

                    pipelined_loop(dve, outer, body)

        ph = ExitStack()
        with ph:
            A = sb("A", [P, U], F32, ph)
            Fs = sb("Fs", [P, U], F32, ph)
            X = sb("X", [P, U + 2], F32, ph)
            NE = sb("NE", [P, U + 1], BF16, ph)
            CT = sb("CT", [P, U + 1], BF16, ph)
            sel8 = sb("sel8", [P, H1], F32, ph)
            selT = sb("selT", [H1, P], F32, ph)
            chm = sb("chm", [P, CH], F32, ph)
            sums = sb("sums", [P, 2], F32, ph)
            spread = sb("spread", [P, 2, CH], F32, ph)
            per_head = sb("per_head", [H1, 2, CH], F32, ph)
            run = sb("run", [H1, CH], F32, ph)
            carry = sb("carry", [H1, CH], F32, ph)
            back = sb("back", [P, CH], F32, ph)
            cin = sb("cin", [P, 1], F32, ph)
            starts = sb("starts", [P, 2], F32, ph)
            d5, dst_in, a_tr, a_cp = sem("dstep5"), sem("dst_in"), sem("a_tr"), sem("a_cp")
            sel_ready, selT_mm, spr_ready, head_mm, car_ready, back_mm = (
                sem("sel_ready"), sem("selT_mm"), sem("spr_ready"), sem("head_mm"), sem("car_ready"), sem("back_mm"))
            sub_ready, ex_ready, alpha_ready, b_tr, b_cp = (sem("sub_ready"), sem("ex_ready"), sem("alpha_ready"),
                                                            sem("b_tr"), sem("b_cp"))
            perm_ready = sem("perm_ready")
            groups = [(a, min(a + 4, TC)) for a in range(0, TC, 4)]
            attn_v = attn[:, :].rearrange("p (j c h) -> p c j h", j=CH, h=H1)

            with nc.Block() as block:
                @block.sync
                def _(sp):
                    for j in range(CH):
                        sp.dma_start(X[j * H1:(j + 1) * H1, :].bitcast(I32),
                                     dst_lin[j * U:j * U + U + 2].unsqueeze(0).broadcast_to([H1, U + 2]))\
                          .then_inc(dst_in, 16)
                    sp.wait_ge(dst_in, 16 * CH)

                @block.tensor
                def _(pe):
                    pe.wait_ge(perm_ready, 1)
                    for g, (a, b) in enumerate(groups):
                        need(pe, a_cp, g - 1)
                        for c in range(a, b):
                            ins = nc.tensor.transpose(bank[g % 2][:, (c - a) * P:(c - a + 1) * P],
                                                      Fs[:, c * P:(c + 1) * P], ident[:, :])
                        ins.then_inc(a_tr, 1)
                    pe.wait_ge(sel_ready, 1)
                    nc.tensor.transpose(bank[2][0:H1, 0:P], sel8[:, :], ident[:, :]).then_inc(selT_mm, 1)
                    for k in range(4):
                        pe.wait_ge(spr_ready, k + 1)
                        nc.tensor.matmul(bank[3][0:H1, 0:2 * CH], sel8[:, :],
                                         spread[:, :, :].rearrange("p a c -> p (a c)"), start=True, stop=True)\
                                 .then_inc(head_mm, 1)
                        pe.wait_ge(car_ready, k + 1)
                        nc.tensor.matmul(bank[4][:, 0:CH], selT[:, :], carry[:, :], start=True, stop=True)\
                                 .then_inc(back_mm, 1)
                    pe.wait_ge(alpha_ready, 1)
                    for g, (a, b) in enumerate(groups):
                        need(pe, b_cp, g - 1)
                        for c in range(a, b):
                            ins = nc.tensor.transpose(bank[5 + g % 2][:, (c - a) * P:(c - a + 1) * P],
                                                      A[:, c * P:(c + 1) * P], ident[:, :])
                        ins.then_inc(b_tr, 1)

                @block.scalar
                def _(act):
                    nc.scalar.activation(Fs[:, :].rearrange("p (c j h) -> p c j h", c=TC, h=H1), attn_v[:, :],
                                         ACT.Copy).then_inc(perm_ready, 1)
                    for g, (a, b) in enumerate(groups):
                        act.wait_ge(a_tr, g + 1)
                        nc.scalar.activation(A[:, a * P:b * P], bank[g % 2][:, 0:(b - a) * P], ACT.Copy)\
                                 .then_inc(a_cp, 1)
                    act.wait_ge(sub_ready, 1)
                    nc.scalar.activation(A[:, :], A[:, :], ACT.Exp).then_inc(ex_ready, 1)
                    for g, (a, b) in enumerate(groups):
                        act.wait_ge(b_tr, g + 1)
                        nc.scalar.activation(attn_v[:, a:b], bank[5 + g % 2][:, 0:(b - a) * P].rearrange(
                            "p (c j h) -> p c j h", c=b - a, h=H1), ACT.Copy).then_inc(b_cp, 1)

                @block.vector
                def _(dve):
                    step = Chain(dve, d5)
                    rev = slice(None, None, -1)
                    carries = [0]

                    def carry_in(last, flag, forward, largest):
                        carries[0] += 1
                        step(dve.tensor_scalar(spread[:, 0, :], chm[:, :], last, None, ALU.mult))
                        step(dve.tensor_scalar(spread[:, 1, :], chm[:, :], flag, None, ALU.mult))
                        dve.sem_inc(spr_ready, 1)
                        dve.wait_ge(head_mm, carries[0])
                        step(dve.tensor_copy(per_head[:, :, :].rearrange("p a c -> p (a c)"),
                                             bank[3][0:H1, 0:2 * CH]))
                        if largest:
                            step(dve.tensor_scalar(per_head[:, 1, :], per_head[:, 1, :], -BIG, None, ALU.mult))
                            step(dve.tensor_tensor_scan(run[:, :], per_head[:, 1, :], per_head[:, 0, :], -BIG,
                                                        ALU.add, ALU.max))
                        else:
                            step(dve.tensor_scalar(per_head[:, 1, :], per_head[:, 1, :], -1.0, 1.0, ALU.mult, ALU.add))
                            r = slice(None) if forward else rev
                            step(dve.tensor_tensor_scan(run[:, r], per_head[:, 1, r], per_head[:, 0, r], 0.0,
                                                        ALU.mult, ALU.add))
                        if forward:
                            step(dve.memset(carry[:, 0:1], -BIG if largest else 0.0))
                            step(dve.tensor_copy(carry[:, 1:], run[:, 0:CH - 1]))
                        else:
                            step(dve.memset(carry[:, CH - 1:], 0.0))
                            step(dve.tensor_copy(carry[:, 0:CH - 1], run[:, 1:]))
                        dve.sem_inc(car_ready, 1)
                        dve.wait_ge(back_mm, carries[0])
                        step(dve.tensor_tensor(back[:, :], bank[4][:, 0:CH], chm[:, :], ALU.mult))
                        step(dve.tensor_reduce(cin[:, :], back[:, :], AX.X, ALU.add))

                    def spread_back():
                        step(dve.tensor_tensor(X[:, 0:U], Fs[:, :], NE[:, 1:U + 1], ALU.mult))

                        def scan(init):
                            step(dve.tensor_tensor_scan(Fs[:, rev], CT[:, 1:U + 1][:, rev], X[:, 0:U][:, rev], init,
                                                        ALU.mult, ALU.add))
                        scan(0.0)
                        carry_in(Fs[:, 0:1], starts[:, 1:2], False, False)
                        scan(cin[:, 0:1])

                    step(dve.tensor_reduce(sel8[:, :], ident[:, :].rearrange("p (j h) -> p h j", h=H1), AX.X, ALU.add))
                    dve.sem_inc(sel_ready, 1)
                    step(dve.tensor_reduce(chm[:, :], ident[:, :].rearrange("p (j h) -> p j h", h=H1), AX.X, ALU.add))
                    dve.wait_ge(selT_mm, 1)
                    step(dve.tensor_copy(selT[:, :], bank[2][0:H1, 0:P]))
                    dve.wait_ge(dst_in, 16 * CH)
                    Xi = X[:, :].bitcast(I32)
                    step(dve.tensor_tensor(NE[:, :], Xi[:, 1:], Xi[:, 0:U + 1], ALU.not_equal))
                    step(dve.tensor_scalar(CT[:, :], NE[:, :], -1.0, 1.0, ALU.mult, ALU.add))
                    step(dve.tensor_reduce(starts[:, 0:1], NE[:, 0:U], AX.X, ALU.max))
                    step(dve.tensor_reduce(starts[:, 1:2], NE[:, 1:U + 1], AX.X, ALU.max))
                    step(dve.tensor_scalar(X[:, 0:U], NE[:, 0:U], -BIG, None, ALU.mult))
                    dve.wait_ge(a_cp, len(groups))

                    def scan_max(init):
                        step(dve.tensor_tensor_scan(Fs[:, :], X[:, 0:U], A[:, :], init, ALU.add, ALU.max))
                    scan_max(-BIG)
                    carry_in(Fs[:, U - 1:U], starts[:, 0:1], True, True)
                    scan_max(cin[:, 0:1])
                    spread_back()
                    step(dve.tensor_tensor(A[:, :], A[:, :], Fs[:, :], ALU.subtract))
                    dve.sem_inc(sub_ready, 1)
                    dve.wait_ge(ex_ready, 1)

                    def scan_sum(init):
                        step(dve.tensor_tensor_scan(Fs[:, :], CT[:, 0:U], A[:, :], init, ALU.mult, ALU.add))
                    scan_sum(0.0)
                    carry_in(Fs[:, U - 1:U], starts[:, 0:1], True, False)
                    scan_sum(cin[:, 0:1])
                    spread_back()
                    step(dve.tensor_scalar(Fs[:, :], Fs[:, :], 1e-16, None, ALU.add))
                    step(dve.reciprocal(X[:, 0:U], Fs[:, :]))
                    step(dve.tensor_tensor(A[:, :], A[:, :], X[:, 0:U], ALU.mult))
                    dve.sem_inc(alpha_ready, 1)

        ph = ExitStack()
        with ph:
            vin = [sb(f"vin{b}", [P, Q * O1], F32, ph) for b in range(2)]
            va = [sb(f"va{b}", [P, Q * O1], F32, ph) for b in range(2)]
            hot = [sb(f"hov{b}", [P, Q, P], F32, ph) for b in range(2)]
            rr = [sb(f"rr{b}", [P, Q], F32, ph) for b in range(2)]
            v_in = [sem(f"v_in{b}") for b in range(2)]
            rr_set, rr_turn = sem("rr_set"), sem("rr_turn")
            hot_ready, va_ready, sum_mm, col6 = sem("hot_ready"), sem("va_ready"), sem("sum_mm"), sem("col_added6")

            with nc.Block() as block:
                @block.sync
                def _(sp):
                    def body(it, i, b):
                        need(sp, va_ready, i - 1)
                        sp.dma_start(vin[b][:, :], v1_edge[bass.ds(i, 1)].rearrange("a p o -> p (a o)"))\
                          .then_inc(v_in[b], 16)
                    supertile_loop(sp, body)

                @block.gpsimd
                def _(pool):
                    def body(it, i, b):
                        need(pool, sum_mm, i - 1)
                        pool.tensor_copy(rr[b][:, :], rrel[:, bass.ds(i * Q, Q)]).then_inc(rr_set, 1)
                        pool.wait_ge(rr_set, i + 1)
                        pool.sem_inc(rr_turn, 1)
                        for q in range(Q):
                            ins = pool.tensor_scalar(hot[b][:, q, :], iota_r[:, :], rr[b][:, q:q + 1], None,
                                                     ALU.is_equal)
                            ins.then_inc(hot_ready, 1)
                    supertile_loop(pool, body)

                @block.vector
                def _(dve):
                    def body(it, i, b):
                        bases = [dve.value_load(base_i[0:1, bass.ds(i * Q + q, 1)], min_val=0, max_val=N)
                                 for q in range(Q)]
                        dve.wait_ge(v_in[b], 16 * (it + 1))
                        need(dve, sum_mm, i - 1)
                        dve.tensor_tensor(va[b][:, :].rearrange("p (g d) -> p g d", d=DH),
                                          vin[b][:, :].rearrange("p (g d) -> p g d", d=DH),
                                          bcast(attn[:, bass.ds(i * (Q * H1), Q * H1)], 2, DH), ALU.mult)\
                           .then_inc(va_ready, 1)
                        dve.wait_ge(sum_mm, i + 1)
                        for q in range(Q):
                            need(dve, col6, i * Q + q)
                            a = acc[:, bass.ds(bases[q], P)]
                            dve.tensor_tensor(a, a, bank[b][:, q * P:(q + 1) * P], ALU.add).then_inc(col6, 1)
                    supertile_loop(dve, body)

                @block.tensor
                def _(pe):
                    def body(it, i, b):
                        pe.wait_ge(va_ready, i + 1)
                        pe.wait_ge(hot_ready, i * Q + Q)
                        need(pe, col6, (i - 1) * Q)
                        for q in range(Q):
                            ins = nc.tensor.matmul(bank[b][:, q * P:(q + 1) * P], va[b][:, q * O1:(q + 1) * O1],
                                                   hot[b][:, q, :], start=True, stop=True)
                        ins.then_inc(sum_mm, 1)
                    supertile_loop(pe, body)

        ph = ExitStack()
        with ph:
            up = sb("up", [P, NJ, D], F32, ph)
            upn = sb("upn", [NP, NJ, D], F32, ph)
            o = sb("o", [NP, NJ, D], F32, ph)
            sq = sb("sq7", [NP, NJ, D], F32, ph)
            stat = sb("stat", [NP, 4, D], F32, ph)
            onesn = sb("onesn", [NP, NP], F32, ph)
            d7, up_mm, up_out, scat7, upd_in = sem("dstep7"), sem("up_mm"), sem("up_out"), sem("scat7"), sem("upd_in")
            self_mm, self_out, ones7, part_ready, part_mm = (sem("self_mm"), sem("self_out"), sem("ones7"),
                                                             sem("part_ready"), sem("part_mm"))
            var7, std7, x_ready, out_sem = sem("var7"), sem("std7"), sem("x_ready"), sem("out_sem")
            groups8 = [(a, min(a + 8, NJ)) for a in range(0, NJ, 8)]

            with nc.Block() as block:
                @block.gpsimd
                def _(pool):
                    pool.memset(onesn[:, :], 1.0).then_inc(ones7, 1)
                    pool.wait_ge(up_out, len(groups8))
                    for c in range(NJ):
                        pool.indirect_dma_start(
                            upd_tab, bass.IndirectOffsetOnAxis(ap=node_i[:, c:c + 1], axis=0), up[:, c, :], None,
                            bounds_check=N - 1, oob_is_err=False).then_inc(scat7, 16)
                    pool.wait_ge(scat7, 16 * NJ)

                @block.sync
                def _(sp):
                    sp.wait_ge(scat7, 16 * NJ)
                    sp.dma_start(upn[:, :, :], upd_tab.rearrange("(p j) d -> p j d", j=NJ)).then_inc(upd_in, 16)
                    sp.wait_ge(x_ready, 1)
                    sp.dma_start(out.rearrange("(p j) d -> p j d", j=NJ), xs[:, :, :]).then_inc(out_sem, 16)
                    sp.wait_ge(out_sem, 16)

                @block.tensor
                def _(pe):
                    for g, (a, b) in enumerate(groups8):
                        need(pe, up_out, g - 1)
                        for c in range(a, b):
                            ins = nc.tensor.matmul(bank[g % 2][:, (c - a) * D:(c - a + 1) * D],
                                                   acc[:, c * P:(c + 1) * P], Wouts[:, :], start=True, stop=True)
                        ins.then_inc(up_mm, 1)
                    for g, (a, b) in enumerate(groups8):
                        need(pe, self_out, g - 1)
                        for j in range(a, b):
                            ins = nc.tensor.matmul(bank[2 + g % 2][0:NP, (j - a) * D:(j - a + 1) * D],
                                                   hT[0:D, j * NP:(j + 1) * NP], Wselfs[:, :], start=True, stop=True)
                        ins.then_inc(self_mm, 1)
                    pe.wait_ge(ones7, 1)
                    for k in range(2):
                        pe.wait_ge(part_ready, k + 1)
                        nc.tensor.matmul(bank[4 + k][0:NP, 0:D], onesn[:, :], stat[:, k, :], start=True, stop=True)\
                                 .then_inc(part_mm, 1)

                @block.scalar
                def _(act):
                    for g, (a, b) in enumerate(groups8):
                        act.wait_ge(up_mm, g + 1)
                        nc.scalar.activation(up[:, a:b, :].rearrange("p a d -> p (a d)"),
                                             bank[g % 2][:, 0:(b - a) * D], ACT.Copy).then_inc(up_out, 1)
                    for g, (a, b) in enumerate(groups8):
                        act.wait_ge(self_mm, g + 1)
                        nc.scalar.activation(o[:, a:b, :].rearrange("p a d -> p (a d)"),
                                             bank[2 + g % 2][0:NP, 0:(b - a) * D], ACT.Copy).then_inc(self_out, 1)
                    act.wait_ge(var7, 1)
                    nc.scalar.activation(stat[:, 3, :], stat[:, 2, :], ACT.Sqrt).then_inc(std7, 1)

                @block.vector
                def _(dve):
                    step = Chain(dve, d7)
                    dve.wait_ge(self_out, len(groups8))
                    dve.wait_ge(upd_in, 16)
                    step(dve.tensor_tensor(o[:, :, :], o[:, :, :], upn[:, :, :], ALU.add))
                    dve.tensor_reduce(stat[:, 0, :], o[:, :, :].rearrange("p j d -> p d j"), AX.X, ALU.add)\
                       .then_inc(part_ready, 1)
                    dve.wait_ge(part_mm, 1)
                    step(dve.tensor_scalar(stat[:, 2, :], bank[4][0:NP, 0:D], 1.0 / N, None, ALU.mult))
                    step(dve.tensor_tensor(o[:, :, :], o[:, :, :], bcast(stat[:, 2, :], 1, NJ), ALU.subtract))
                    step(dve.tensor_tensor(sq[:, :, :], o[:, :, :], o[:, :, :], ALU.mult))
                    dve.tensor_reduce(stat[:, 1, :], sq[:, :, :].rearrange("p j d -> p d j"), AX.X, ALU.add)\
                       .then_inc(part_ready, 1)
                    dve.wait_ge(part_mm, 2)
                    dve.tensor_scalar(stat[:, 2, :], bank[5][0:NP, 0:D], 1.0 / N, BN_EPS, ALU.mult, ALU.add)\
                       .then_inc(var7, 1)
                    dve.wait_ge(std7, 1)
                    step(dve.reciprocal(stat[:, 2, :], stat[:, 3, :]))
                    step(dve.tensor_tensor(stat[:, 2, :], stat[:, 2, :], g1b[:, :], ALU.mult))
                    step(dve.tensor_tensor(o[:, :, :], o[:, :, :], bcast(stat[:, 2, :], 1, NJ), ALU.mult))
                    step(dve.tensor_tensor(o[:, :, :], o[:, :, :], bcast(be1b[:, :], 1, NJ), ALU.add))
                    dve.tensor_tensor(xs[:, :, :], xs[:, :, :], o[:, :, :], ALU.add).then_inc(x_ready, 1)


_INS = ["x", "src", "dst", "edge_attr_64", "edge_attr_9", "L0_gnn_Wq", "L0_gnn_bq", "L0_gnn_Wk", "L0_gnn_bk",
        "L0_gnn_Wv", "L0_gnn_bv", "L0_gnn_Wo", "L0_gnn_bo", "L0_gnn_Wf", "L0_gnn_bf", "L0_gnn_gamma",
        "L0_gnn_beta", "L1_gnn_Wq", "L1_gnn_Cqk", "L1_gnn_Cv", "L1_gnn_k_w1", "L1_gnn_k_b1", "L1_gnn_k_w2",
        "L1_gnn_k_b2", "L1_gnn_v_w1", "L1_gnn_v_b1", "L1_gnn_v_w2", "L1_gnn_v_b2", "L1_gnn_W_out",
        "L1_gnn_W_self", "L1_gnn_gamma", "L1_gnn_beta"]


def kernel(**inputs):
    import numpy as np
    import concourse.bacc as bacc
    from concourse.bass_utils import run_bass_kernel_spmd

    nc = bacc.Bacc("TRN2", target_bir_lowering=False, num_devices=1)
    arrays, args = {}, []
    for name in _INS:
        a = np.ascontiguousarray(inputs[name])
        arrays[f"in_{name}"] = a
        args.append(nc.dram_tensor(f"in_{name}", a.shape, mybir.dt.from_np(a.dtype), kind="ExternalInput").ap())
    out = nc.dram_tensor("out", (N, D), F32, kind="ExternalOutput").ap()
    gnn(nc, *args, out)
    return run_bass_kernel_spmd(nc, [arrays], core_ids=[0]).results[0]["out"]
```

```python
from contextlib import ExitStack

import concourse.bass as bass
from concourse import mybir
from concourse.alu_op_type import AluOpType as ALU

F32 = mybir.dt.float32
F32R = mybir.dt.float32r
BF16 = mybir.dt.bfloat16
I32 = mybir.dt.int32
ACT = mybir.ActivationFunctionType
AX = mybir.AxisListType

P = 128
N = 3125
D = 64
E = 103125
S = 9
H0, DH = 4, 16
H1 = 8
O1 = H1 * DH
NP, NJ = 125, 25
Q = 4
ST = Q * P
NST = -(-E // ST)
CH = 16
TC = 51
NT = CH * TC
EP = NT * P
U = TC * P
PAD = N
NTR = NST * Q
BIG = 1.5e38
LN_EPS = BN_EPS = 1e-5
SCALE0, CLIP = 1.0 / 8.0, 5.0
F0 = D + H0


def need(eng, sem, n):
    if not isinstance(n, int) or n > 0:
        eng.wait_ge(sem, n)


def pipelined(eng, stages):
    most, least = max(a for _, a in stages), min(a for _, a in stages)

    def step(it, i, b):
        for f, a in stages:
            if not isinstance(i, int) or 0 <= i + a < NST:
                f(it + (b + a) // 2, i + a, (b + a) % 2)

    first = max(1, (2 - least) // 2)
    end = (NST - 1 - max(most, 0)) // 2
    for i in range(-max(most, 0), 2 * first):
        step(i // 2, i, i % 2)
    with eng.Fori(first, end) as it:
        for b in range(2):
            step(it, it * 2 + b, b)
    for i in range(2 * end, NST - least):
        step(i // 2, i, i % 2)


class Chain:

    def __init__(self, eng, sem):
        self.eng, self.sem, self.n = eng, sem, 0

    def __call__(self, ins):
        ins.then_inc(self.sem, 1)
        self.n += 1
        self.eng.wait_ge(self.sem, self.n)


def bcast(ap, axis, n):
    ap = ap.unsqueeze(axis)
    shape = list(ap.shape)
    shape[axis] = n
    return ap.broadcast_to(shape)


def gnn(nc, x, src, dst, ea64, ea9, Wq0, bq0, Wk0, bk0, Wv0, bv0, Wo0, bo0, Wf0, bf0, g0, be0,
        Wq1, Cqk, Cv, kw1, kb1, kw2, kb2, vw1, vb1, vw2, vb2, Wout, Wself, g1, be1, out):
    ctx = ExitStack()

    def sb(name, shape, dt=F32, where=None):
        return (where or ctx).enter_context(nc.sbuf_tensor(name, shape, dt))

    def sem(name):
        return ctx.enter_context(nc.semaphore(name))

    def dram(name, shape, dt=F32):
        return nc.dram_tensor(name, shape, dt, kind="Internal").ap()

    with ctx:
        dst_tab = dram("dst_tab", (NT + 1, P), I32)
        src_tab = dram("src_tab", (NT, P), I32)
        kv0_tab = dram("kv0_tab", (N, 2 * D))
        q0_tab = dram("q0_tab", (N + 1, D))
        q0_edge = dram("q0_edge", (NTR * P, D))
        sum0_edge = dram("sum0_edge", (NTR * P, F0))
        carry0_tab = dram("carry0_tab", (NTR, F0))
        h1_tab = dram("h1_tab", (N, D))
        q1_tab = dram("q1_tab", (N + 1, O1))
        v1_edge = dram("v1_edge", (NST, P, Q * O1))
        sum1_edge = dram("sum1_edge", (NTR * P, O1))
        carry1_tab = dram("carry1_tab", (NTR, O1))

        bank = [ctx.enter_context(nc.psum_tensor(f"bank{k}", [P, 512], F32)) for k in range(8)]

        ident = sb("ident", [P, P])
        W0 = sb("W0", [D + 1, 3 * D])
        WfA = sb("WfA", [D + 1, D])
        WoA = sb("WoA", [D + 1, D])
        Wq1s = sb("Wq1s", [D, O1])
        Wselfs = sb("Wselfs", [D, D])
        Wouts = sb("Wouts", [O1, D])
        W1_hi = sb("W1_hi", [P, O1], F32R)
        W1_lo = sb("W1_lo", [P, O1], F32R)
        b1 = sb("b1", [O1, 1])
        W2_hi = sb("W2_hi", [O1, 2 * O1], F32R)
        W2_lo = sb("W2_lo", [O1, 2 * O1], F32R)
        b2 = sb("b2", [P, 2 * O1])
        C_hi = sb("C_hi", [P, 5, 2 * O1], F32R)
        C_lo = sb("C_lo", [P, 5, 2 * O1], F32R)
        g0b = sb("g0b", [NP, D])
        be0b = sb("be0b", [NP, D])
        g1b = sb("g1b", [NP, D])
        be1b = sb("be1b", [NP, D])
        src_i = sb("src_i", [P, NT], I32)
        dst_i = sb("dst_i", [P, NT], I32)
        dst_e = sb("dst_e", [P, NT])
        cont = sb("cont", [P, NTR])
        last_i = sb("last_i", [NP, NJ], I32)
        tile_i = sb("tile_i", [NP, NJ], I32)
        has = sb("has", [NP, NJ])
        over = sb("over", [NP, NJ])
        xs = sb("xs", [NP, NJ, D])
        hT = sb("hT", [D + 1, NJ * NP])

        W_SEM = sem("weights_loaded")

        def layer_norm(dve, step, src_ap, cen, sq, st, var_ready, std_ready, k):
            step(dve.tensor_reduce(st[:, 0, :], src_ap, AX.X, ALU.add))
            step(dve.tensor_scalar(st[:, 0, :], st[:, 0, :], 1.0 / D, None, ALU.mult))
            step(dve.tensor_tensor(cen, src_ap, bcast(st[:, 0, :], 2, D), ALU.subtract))
            step(dve.tensor_tensor(sq, cen, cen, ALU.mult))
            step(dve.tensor_reduce(st[:, 1, :], sq, AX.X, ALU.add))
            dve.tensor_scalar(st[:, 1, :], st[:, 1, :], 1.0 / D, LN_EPS, ALU.mult, ALU.add)\
               .then_inc(var_ready, 1)
            dve.wait_ge(std_ready, k)
            step(dve.reciprocal(st[:, 3, :], st[:, 2, :]))
            step(dve.tensor_tensor(cen, cen, bcast(st[:, 3, :], 2, D), ALU.mult))

        def roots(act, st, var_ready, std_ready, k):
            act.wait_ge(var_ready, k)
            nc.scalar.activation(st[:, 2, :], st[:, 1, :], ACT.Sqrt).then_inc(std_ready, 1)

        ph = ExitStack()
        with ph:
            def tsb(name, shape, dt=F32):
                return sb(name, shape, dt, ph)

            ones = tsb("ones", [P, P])
            row_l = tsb("row_l", [P, P])
            C = tsb("C", [P, 5, 2 * O1])
            W1 = tsb("W1", [P, O1])
            W2 = tsb("W2", [O1, 2 * O1])
            padi = tsb("padi", [1, EP - E + P], I32)
            zrow = tsb("zrow", [P, 101, D])
            dst_r = tsb("dst_r", [P, 7, P], I32)
            src_r = tsb("src_r", [P, 7, P], I32)
            first_i = tsb("first_i", [P, 7], I32)
            qfirst = tsb("qfirst", [P, 7, D])
            rows_f = tsb("rows_f", [P, 2, 7 * P])
            lastrow = tsb("lastrow", [P, NT])
            junk = tsb("junk", [P, NT])
            node_n = tsb("node_n", [NP, NJ + 1])
            tiles_n = tsb("tiles_n", [NP, NJ + 1])
            tiles_i = tsb("tiles_i", [NP, NJ + 1], I32)
            inner_n = tsb("inner_n", [NP, NJ + 1])
            upto = tsb("upto", [NP, NJ + 1])
            tile_rows = tsb("tile_rows", [NP, NJ + 1, P], I32)
            start_n = tsb("start_n", [NP, NJ])
            start_i = tsb("start_i", [NP, NJ], I32)
            tf = tsb("tf", [NP, 3, NJ])
            cen = tsb("cen", [NP, NJ, D])
            sq = tsb("sq", [NP, NJ, D])
            st = tsb("st", [NP, 4, NJ])
            kvq = tsb("kvq", [NP, NJ, 3 * D])
            qn = tsb("qn", [NP, NJ, D])

            x_in, lin, rows_in, pad_set, zero_set = sem("x_in"), sem("lin"), sem("rows_in"), sem("pad_set"), sem("zero_set")
            consts, poolc, dstep, rows_cast = sem("consts"), sem("poolc"), sem("dstep1"), sem("rows_cast")
            tpose, tpose_out, last_mm = sem("tpose"), sem("tpose_out"), sem("last_mm")
            var1, std1, h_ready, w2z = sem("var1"), sem("std1"), sem("h_ready"), sem("w2z")
            hT_mm, hT_out, proj_mm, proj_out, tabs = (sem("hT_mm"), sem("hT_out"), sem("proj_mm"),
                                                      sem("proj_out"), sem("tabs"))
            filled, tiles_ready, tiles_got, start_ready = (sem("filled"), sem("tiles_ready"), sem("tiles_got"),
                                                           sem("start_ready"))
            q_scat, first_set, first_got, first_put = sem("q_scat"), sem("first_set"), sem("first_got"), sem("first_put")
            ranges_ready = sem("ranges_ready")
            hT_groups = [(a, min(a + 4, NJ)) for a in range(0, NJ, 4)]
            pj_groups = [(a, min(a + 2, NJ)) for a in range(0, NJ, 2)]
            dst_flat = dst_tab.rearrange("t p -> (t p)")
            src_flat = src_tab.rearrange("t p -> (t p)")

            loads = [(W0[0:D, 0:D], Wk0), (W0[0:D, D:2 * D], Wv0), (W0[0:D, 2 * D:3 * D], Wq0),
                     (W0[D:D + 1, 0:D], bk0.unsqueeze(0)), (W0[D:D + 1, D:2 * D], bv0.unsqueeze(0)),
                     (W0[D:D + 1, 2 * D:3 * D], bq0.unsqueeze(0)),
                     (WfA[0:D, :], Wf0), (WfA[D:D + 1, :], bf0.unsqueeze(0)),
                     (WoA[0:D, :], Wo0), (WoA[D:D + 1, :], bo0.unsqueeze(0)),
                     (Wq1s[:, :], Wq1), (Wselfs[:, :], Wself), (Wouts[:, :], Wout),
                     (W1[D:2 * D, 0:D], kw1), (W1[D:2 * D, D:O1], vw1),
                     (b1[0:D, :], kb1.unsqueeze(1)), (b1[D:O1, :], vb1.unsqueeze(1)),
                     (W2[0:D, 0:O1], kw2), (W2[D:O1, O1:2 * O1], vw2),
                     (b2[:, 0:O1], kb2.unsqueeze(0).broadcast_to([P, O1])),
                     (b2[:, O1:2 * O1], vb2.unsqueeze(0).broadcast_to([P, O1]))]
            for s in range(S):
                r = D * (s % 2)
                loads += [(C[r:r + D, s // 2, 0:O1], Cqk[:, s, :]),
                          (C[r:r + D, s // 2, O1:2 * O1], Cv[:, s, :])]
            for dst_t, v in ((g0b, g0), (be0b, be0), (g1b, g1), (be1b, be1)):
                loads.append((dst_t[:, :], v.unsqueeze(0).broadcast_to([NP, D])))
            n_weights = 16 * len(loads)

            with nc.Block() as block:
                @block.sync
                def _(sp):
                    sp.dma_start(dst_flat[0:E].unsqueeze(0), dst.unsqueeze(0)).then_inc(lin, 16)
                    sp.dma_start(src_flat[0:E].unsqueeze(0), src.unsqueeze(0)).then_inc(lin, 16)
                    sp.dma_start(xs[:, :, :], x.rearrange("(p j) d -> p j d", j=NJ)).then_inc(x_in, 16)
                    sp.wait_ge(pad_set, 3)
                    sp.dma_start(dst_flat[E:EP + P].unsqueeze(0), padi[:, :]).then_inc(lin, 16)
                    sp.dma_start(src_flat[E:EP].unsqueeze(0), zrow[0:1, :, :].bitcast(I32).rearrange(
                        "p a d -> p (a d)")[:, 0:EP - E]).then_inc(lin, 16)
                    sp.wait_ge(lin, 64)
                    for rows, tab in ((dst_r, dst_tab), (src_r, src_tab)):
                        sp.dma_start(rows[:, 0:6, :], tab[0:6 * P, :].rearrange("(g t) p -> t g p", g=6))\
                          .then_inc(rows_in, 16)
                        sp.dma_start(rows[0:NT - 6 * P, 6, :], tab[6 * P:NT, :]).then_inc(rows_in, 16)
                    sp.dma_start(q0_tab[N:N + 1, :], zrow[0:1, 0, :]).then_inc(tabs, 16)
                    sp.dma_start(q1_tab[N:N + 1, :], zrow[0:1, 0:2, :].rearrange("p a d -> p (a d)"))\
                      .then_inc(tabs, 16)
                    q0_fill = q0_edge.rearrange("(a p n) d -> a p n d", p=P, n=101)
                    for a in range(NTR // 101):
                        sp.dma_start(q0_fill[a], zrow[:, :, :]).then_inc(filled, 16)
                    sp.wait_ge(proj_out, len(pj_groups))
                    sp.dma_start(kv0_tab.rearrange("(p j) d -> p j d", j=NJ), kvq[:, :, 0:2 * D]).then_inc(tabs, 16)
                    sp.dma_start(q0_tab[0:N, :].rearrange("(p j) d -> p j d", j=NJ),
                                 kvq[:, :, 2 * D:3 * D]).then_inc(tabs, 16)
                    sp.wait_ge(tabs, 64)
                    sp.wait_ge(first_got, 16 * 7)
                    sp.wait_ge(q_scat, 16 * NJ)
                    rows_of = q0_edge.rearrange("(t p) d -> t p d", p=P)
                    for g in range(7):
                        n = P if g < 6 else NTR - 6 * P
                        sp.dma_start(rows_of[g * P:g * P + n, 0, :], qfirst[0:n, g, :]).then_inc(first_put, 16)
                    sp.wait_ge(first_put, 16 * 7)

                @block.scalar
                def _(act):
                    act.wait_ge(w2z, 1)
                    for a, b in loads:
                        act.dma_start(a, b).then_inc(W_SEM, 16)
                    roots(act, st, var1, std1, 1)
                    for n in range(2):
                        for half in range(2):
                            act.wait_ge(tpose, 2 * n + half + 1)
                            w = 512 if half == 0 else NT - 512
                            dest = (dst_e, src_i)[n]
                            nc.scalar.activation(dest[:, 512 * half:512 * half + w],
                                                 bank[2 * n + half][:, 0:w], ACT.Copy).then_inc(tpose_out, 1)
                    for half in range(2):
                        act.wait_ge(last_mm, half + 1)
                        w = 512 if half == 0 else NT - 512
                        nc.scalar.activation(lastrow[:, 512 * half:512 * half + w], bank[half][:, 0:w],
                                             ACT.Copy).then_inc(tpose_out, 1)
                    for g, (a, b) in enumerate(hT_groups):
                        act.wait_ge(hT_mm, g + 1)
                        nc.scalar.activation(hT[0:D, a * NP:b * NP], bank[4 + g % 2][0:D, 0:(b - a) * NP],
                                             ACT.Copy).then_inc(hT_out, 1)
                    for g, (a, b) in enumerate(pj_groups):
                        act.wait_ge(proj_mm, g + 1)
                        nc.scalar.activation(kvq[:, a:b, :].rearrange("p a d -> p (a d)"),
                                             bank[6 + g % 2][0:NP, 0:(b - a) * 3 * D], ACT.Copy).then_inc(proj_out, 1)
                    act.wait_ge(W_SEM, n_weights)

                @block.gpsimd
                def _(pool):
                    pool.memset(padi[:, 0:EP - E], PAD).then_inc(pad_set, 1)
                    pool.memset(padi[:, EP - E:], PAD + 1).then_inc(pad_set, 1)
                    pool.memset(zrow[:, :, :], 0.0).then_inc(pad_set, 1)
                    pool.memset(W2[:, :], 0.0).then_inc(w2z, 1)
                    pool.memset(ident[:, :], 0.0).then_inc(poolc, 1)
                    pool.memset(row_l[:, :], 0.0).then_inc(poolc, 1)
                    pool.wait_ge(poolc, 2)
                    pool.affine_select(out=ident[:, :], in_=ident[:, :], compare_op=ALU.not_equal, fill=1.0,
                                       base=0, pattern=[[-1, P]], channel_multiplier=1).then_inc(consts, 1)
                    pool.affine_select(out=row_l[:, :], in_=row_l[:, :], compare_op=ALU.not_equal, fill=1.0,
                                       base=1 - P, pattern=[[0, P]], channel_multiplier=1).then_inc(consts, 1)
                    pool.iota(node_n[:, :], [[1, NJ + 1]], base=-1, channel_multiplier=NJ,
                              allow_small_or_imprecise_dtypes=True).then_inc(consts, 1)
                    pool.wait_ge(consts, 3)
                    pool.memset(hT[D:D + 1, :], 1.0).then_inc(consts, 1)
                    pool.wait_ge(consts, 4)
                    pool.wait_ge(tiles_ready, 1)
                    for j in range(NJ + 1):
                        pool.indirect_dma_start(
                            tile_rows[:, j, :], None, dst_tab,
                            bass.IndirectOffsetOnAxis(ap=tiles_i[:, j:j + 1], axis=0)).then_inc(tiles_got, 16)
                    pool.wait_ge(tabs, 64)
                    pool.wait_ge(first_set, 2)
                    for g in range(7):
                        n = P if g < 6 else NTR - 6 * P
                        pool.indirect_dma_start(
                            qfirst[0:n, g, :], None, q0_tab,
                            bass.IndirectOffsetOnAxis(ap=first_i[0:n, g:g + 1], axis=0)).then_inc(first_got, 16)
                    pool.wait_ge(start_ready, 2)
                    pool.wait_ge(filled, 16 * (NTR // 101))
                    for j in range(NJ):
                        pool.indirect_dma_start(
                            q0_edge, bass.IndirectOffsetOnAxis(ap=start_i[:, j:j + 1], axis=0), qn[:, j, :], None,
                            bounds_check=NTR * P - 1, oob_is_err=False).then_inc(q_scat, 16)

                @block.vector
                def _(dve):
                    step = Chain(dve, dstep)
                    dve.wait_ge(x_in, 16)
                    layer_norm(dve, step, xs[:, :, :], cen[:, :, :], sq[:, :, :], st, var1, std1, 1)
                    dve.tensor_scalar(cen[:, :, :], cen[:, :, :], 0.0, None, ALU.max).then_inc(h_ready, 1)
                    dve.wait_ge(rows_in, 64)
                    for n, rows in enumerate((dst_r, src_r)):
                        dve.tensor_copy(rows_f[:, n, 0:6 * P], rows[:, 0:6, :].rearrange("t g p -> t (g p)"))\
                           .then_inc(rows_cast, 1)
                        dve.tensor_copy(rows_f[0:NT - 6 * P, n, 6 * P:7 * P], rows[0:NT - 6 * P, 6, :])\
                           .then_inc(rows_cast, 1)
                    dve.tensor_copy(first_i[:, 0:6], dst_r[:, 0:6, 0]).then_inc(first_set, 1)
                    dve.tensor_copy(first_i[0:NT - 6 * P, 6:7], dst_r[0:NT - 6 * P, 6, 0:1]).then_inc(first_set, 1)
                    dve.wait_ge(tpose_out, 6)
                    dve.wait_ge(consts, 4)
                    for j in range(NJ + 1):
                        step(dve.tensor_scalar(junk[0:NP, :], lastrow[0:NP, :], node_n[:, j:j + 1], 0.0, ALU.is_le,
                                               ALU.add, accum_out=tiles_n[:, j:j + 1]))
                    step(dve.tensor_copy(tiles_i[:, :], tiles_n[:, :]))
                    dve.sem_inc(tiles_ready, 1)
                    dve.tensor_copy(dst_i[:, :], dst_e[:, :]).then_inc(ranges_ready, 1)
                    step(dve.tensor_scalar(cont[:, 0:1], dst_e[:, 0:1], 0.0, None, ALU.mult))
                    step(dve.tensor_tensor(cont[:, 1:], lastrow[:, 1:NTR], lastrow[:, 0:NTR - 1], ALU.is_equal))
                    dve.wait_ge(tiles_got, 16 * (NJ + 1))
                    for j in range(NJ + 1):
                        step(dve.tensor_scalar(junk[0:NP, 0:P], tile_rows[:, j, :], node_n[:, j:j + 1], 0.0, ALU.is_le,
                                               ALU.add, accum_out=inner_n[:, j:j + 1]))
                    step(dve.scalar_tensor_tensor(upto[:, :], tiles_n[:, :], float(P), inner_n[:, :], ALU.mult,
                                                  ALU.add))
                    lo, hi = upto[:, 0:NJ], upto[:, 1:NJ + 1]
                    step(dve.tensor_tensor(has[:, :], hi, lo, ALU.is_gt))
                    step(dve.tensor_scalar(tf[:, 0, :], has[:, :], -4.0 * E, 4.0 * E, ALU.mult, ALU.add))
                    step(dve.tensor_tensor(start_n[:, :], lo, tf[:, 0, :], ALU.add))
                    dve.tensor_copy(start_i[:, :], start_n[:, :]).then_inc(start_ready, 1)
                    dve.wait_ge(proj_out, len(pj_groups))
                    dve.tensor_copy(qn[:, :, :], kvq[:, :, 2 * D:3 * D]).then_inc(start_ready, 1)
                    step(dve.tensor_scalar(tf[:, 1, :], hi, -1.0, 0.0, ALU.add, ALU.max))
                    step(dve.tensor_copy(last_i[:, :], tf[:, 1, :]))
                    step(dve.tensor_scalar(tf[:, 2, :], inner_n[:, 1:NJ + 1], 0.0, None, ALU.is_equal))
                    step(dve.tensor_tensor(tf[:, 2, :], tiles_n[:, 1:NJ + 1], tf[:, 2, :], ALU.subtract))
                    step(dve.tensor_scalar(tf[:, 2, :], tf[:, 2, :], 0.0, None, ALU.max))
                    step(dve.tensor_copy(tile_i[:, :], tf[:, 2, :]))
                    step(dve.scalar_tensor_tensor(tf[:, 0, :], tf[:, 2, :], float(P), lo, ALU.mult, ALU.is_gt))
                    step(dve.tensor_tensor(over[:, :], tf[:, 0, :], has[:, :], ALU.mult))
                    dve.wait_ge(W_SEM, n_weights)
                    parts = [(C[:, 0:4, :], C_hi[:, 0:4, :], C_lo[:, 0:4, :]),
                             (C[0:D, 4, :], C_hi[0:D, 4, :], C_lo[0:D, 4, :]),
                             (W1[D:2 * D, :], W1_hi[D:2 * D, :], W1_lo[D:2 * D, :]),
                             (W2[:, :], W2_hi[:, :], W2_lo[:, :])]
                    for whole, hi, lo in parts:
                        step(dve.tensor_copy(hi, whole))
                        step(dve.tensor_tensor(lo, whole, hi.bitcast(F32), ALU.subtract))

                @block.tensor
                def _(pe):
                    pe.wait_ge(consts, 4)
                    for n in range(2):
                        pe.wait_ge(rows_cast, 2 * n + 2)
                        for g in range(7):
                            rows = P if g < 6 else NT - 6 * P
                            b = bank[2 * n + g // 4]
                            ins = nc.tensor.transpose(b[:, (g % 4) * P:(g % 4) * P + rows],
                                                      rows_f[0:rows, n, g * P:(g + 1) * P], ident[0:rows, 0:rows])
                            if g in (3, 6):
                                ins.then_inc(tpose, 1)
                    for half in range(2):
                        pe.wait_ge(tpose_out, half + 1)
                        w = 512 if half == 0 else NT - 512
                        nc.tensor.matmul(bank[half][:, 0:w], row_l[:, :], dst_e[:, 512 * half:512 * half + w],
                                         start=True, stop=True).then_inc(last_mm, 1)
                    pe.wait_ge(h_ready, 1)
                    for g, (a, b) in enumerate(hT_groups):
                        need(pe, hT_out, g - 1)
                        for j in range(a, b):
                            ins = nc.tensor.transpose(bank[4 + g % 2][0:D, (j - a) * NP:(j - a + 1) * NP],
                                                      cen[:, j, :], ident[0:NP, 0:NP])
                        ins.then_inc(hT_mm, 1)
                    pe.wait_ge(hT_out, len(hT_groups))
                    pe.wait_ge(W_SEM, n_weights)
                    for g, (a, b) in enumerate(pj_groups):
                        need(pe, proj_out, g - 1)
                        for j in range(a, b):
                            ins = nc.tensor.matmul(bank[6 + g % 2][0:NP, (j - a) * 3 * D:(j - a + 1) * 3 * D],
                                                   hT[:, j * NP:(j + 1) * NP], W0[:, :], start=True, stop=True)
                        ins.then_inc(proj_mm, 1)

        def dst_rows(i):
            return dst_tab[bass.ds(i * Q, Q), :].rearrange("q p -> (q p)").unsqueeze(0).broadcast_to([P, ST])

        ph = ExitStack()
        with ph:
            kv = [sb(f"kv{b}", [P, Q, 2 * D], F32, ph) for b in range(2)]
            idx = [sb(f"idx{b}", [P, Q], I32, ph) for b in range(2)]
            qs = [sb(f"qs{b}", [P, Q, D], F32, ph) for b in range(2)]
            drow = [sb(f"drow{b}", [P, ST], I32, ph) for b in range(2)]
            prod = sb("prod", [P, Q * D], F32, ph)
            sc = sb("sc", [P, Q, H0], F32, ph)
            feat = [sb(f"feat{b}", [P, Q, F0], F32, ph) for b in range(2)]
            same = [sb(f"same{b}", [P, Q, P], F32, ph) for b in range(2)]
            rows = [sb(f"rows{b}", [P, Q, F0], F32, ph) for b in range(2)]
            idx_copied, idx_turn = sem("idx_copied"), sem("idx_turn")
            kv_got = [sem(f"kv_got{b}") for b in range(2)]
            qs_in = [sem(f"qs_in{b}") for b in range(2)]
            drow_in = [sem(f"drow_in{b}") for b in range(2)]
            rows_out = [sem(f"rows_out{b}") for b in range(2)]
            same_ready, qe_mm, prod_ready, red_ready, clip_ready = (
                sem("same_ready"), sem("qe_mm"), sem("prod_ready"), sem("red_ready"), sem("clip_ready"))
            score_ready, exp_done, feat_ready = sem("score_ready"), sem("exp_done"), sem("feat_ready")
            sum_mm, rows_cp = sem("sum_mm"), sem("rows_cp")

            with nc.Block() as block:
                @block.gpsimd
                def _(pool):
                    def gather(it, i, b):
                        need(pool, feat_ready, i - 1)
                        pool.tensor_copy(idx[b][:, :], src_i[:, bass.ds(i * Q, Q)]).then_inc(idx_copied, 1)
                        pool.wait_ge(idx_copied, i + 1)
                        pool.sem_inc(idx_turn, 1)
                        for q in range(Q):
                            pool.indirect_dma_start(
                                kv[b][:, q, :], None, kv0_tab,
                                bass.IndirectOffsetOnAxis(ap=idx[b][:, q:q + 1], axis=0)).then_inc(kv_got[b], 16)
                    pipelined(pool, [(gather, 0)])

                @block.sync
                def _(sp):
                    def load(it, i, b):
                        need(sp, same_ready, i - 1)
                        sp.dma_start(drow[b][:, :], dst_rows(i)).then_inc(drow_in[b], 16)
                        need(sp, qe_mm, i - 1)
                        sp.dma_start(qs[b][:, :, :], q0_edge[bass.ds(i * ST, ST), :].rearrange(
                            "(q p) d -> p q d", p=P)).then_inc(qs_in[b], 16)

                    def store(it, i, b):
                        sp.wait_ge(rows_cp, i + 1)
                        sp.dma_start(sum0_edge[bass.ds(i * ST, ST), :].rearrange("(q p) d -> p q d", p=P),
                                     rows[b][:, :, :]).then_inc(rows_out[b], 16)
                    pipelined(sp, [(load, 2), (store, 0)])
                    for b in range(2):
                        sp.wait_ge(rows_out[b], 16 * (NST // 2))

                @block.scalar
                def _(act):
                    def score(it, i, b):
                        act.wait_ge(score_ready, i + 1)
                        need(act, sum_mm, i - 1)
                        nc.scalar.activation(feat[b][:, :, D:F0], sc[:, :, :], ACT.Exp).then_inc(exp_done, 1)

                    def sums(it, i, b):
                        act.wait_ge(sum_mm, i + 1)
                        need(act, rows_out[b], it * 16)
                        nc.scalar.activation(rows[b][:, :, :].rearrange("p q f -> p (q f)"),
                                             bank[2 + b][:, 0:Q * F0], ACT.Copy).then_inc(rows_cp, 1)
                    pipelined(act, [(score, 0), (sums, -1)])

                @block.vector
                def _(dve):
                    def build(it, i, b):
                        dve.wait_ge(drow_in[b], 16 * (it + 1))
                        need(dve, sum_mm, i - 1)
                        dve.tensor_tensor(same[b][:, :, :], drow[b][:, :].rearrange("p (q e) -> p q e", q=Q),
                                          bcast(dst_e[:, bass.ds(i * Q, Q)], 2, P), ALU.is_equal)\
                           .then_inc(same_ready, 1)

                    def body(it, i, b):
                        dve.wait_ge(kv_got[b], 16 * Q * (it + 1))
                        dve.wait_ge(qe_mm, i + 1)
                        need(dve, red_ready, i)
                        dve.tensor_tensor(prod[:, :].rearrange("p (q d) -> p q d", q=Q), kv[b][:, :, 0:D],
                                          bank[b][:, 0:Q * D].rearrange("p (q d) -> p q d", q=Q), ALU.mult)\
                           .then_inc(prod_ready, 1)
                        dve.wait_ge(prod_ready, i + 1)
                        need(dve, exp_done, i)
                        dve.tensor_reduce(sc[:, :, :].rearrange("p q h -> p (q h)"),
                                          prod[:, :].rearrange("p (g d) -> p g d", d=DH), AX.X, ALU.add)\
                           .then_inc(red_ready, 1)
                        dve.wait_ge(red_ready, i + 1)
                        dve.tensor_scalar(sc[:, :, :], sc[:, :, :], SCALE0, -CLIP, ALU.mult, ALU.max)\
                           .then_inc(clip_ready, 1)
                        dve.wait_ge(clip_ready, i + 1)
                        dve.tensor_scalar(sc[:, :, :], sc[:, :, :], CLIP, None, ALU.min).then_inc(score_ready, 1)

                    def weigh(it, i, b):
                        dve.wait_ge(exp_done, i + 1)
                        dve.tensor_tensor(
                            feat[b][:, :, 0:D].rearrange("p q (h d) -> p q h d", d=DH),
                            kv[b][:, :, D:2 * D].rearrange("p q (h d) -> p q h d", d=DH),
                            bcast(feat[b][:, :, D:F0], 3, DH), ALU.mult).then_inc(feat_ready, 1)
                    pipelined(dve, [(body, 0), (build, 1), (weigh, 0)])

                @block.tensor
                def _(pe):
                    def spread_q(it, i, b):
                        pe.wait_ge(same_ready, i + 1)
                        pe.wait_ge(qs_in[b], 16 * (it + 1))
                        need(pe, prod_ready, i - 1)
                        for q in range(Q):
                            ins = nc.tensor.matmul(bank[b][:, q * D:(q + 1) * D], same[b][:, q, :], qs[b][:, q, :],
                                                   start=True, stop=True)
                        ins.then_inc(qe_mm, 1)

                    def sums(it, i, b):
                        pe.wait_ge(feat_ready, i + 1)
                        need(pe, rows_cp, i - 1)
                        for q in range(Q):
                            ins = nc.tensor.matmul(bank[2 + b][:, q * F0:(q + 1) * F0], same[b][:, q, :],
                                                   feat[b][:, q, :], start=True, stop=True)
                        ins.then_inc(sum_mm, 1)
                    pipelined(pe, [(spread_q, 1), (sums, 0)])

        c_groups = [(g * P, min((g + 1) * P, NTR)) for g in range(7)]

        def load_last_rows(sp, lrows, sum_edge, got):
            of_tile = sum_edge.rearrange("(t p) f -> t p f", p=P)
            for g, (a, b) in enumerate(c_groups):
                sp.dma_start(lrows[0:b - a, g, :], of_tile[a:b, P - 1, :]).then_inc(got, 16)

        def transpose_last_rows(pe, lrows, F, got, done):
            pe.wait_ge(got, 16 * len(c_groups))
            for g, (a, b) in enumerate(c_groups):
                ins = nc.tensor.transpose(bank[6 + g // 4][0:F, (g % 4) * P:(g % 4) * P + b - a],
                                          lrows[0:b - a, g, :], ident[0:b - a, 0:b - a])
                if g in (3, 6):
                    ins.then_inc(done, 1)

        def copy_last(act, last, F, mm, done):
            for half in range(2):
                act.wait_ge(mm, half + 1)
                w = 512 if half == 0 else NTR - 512
                nc.scalar.activation(last[:, 512 * half:512 * half + w], bank[6 + half][0:F, 0:w],
                                     ACT.Copy).then_inc(done, 1)
        ph = ExitStack()
        with ph:
            lrows = sb("lrows", [P, 7, F0], F32, ph)
            last = sb("last", [F0, NTR], F32, ph)
            full = sb("full", [F0, NTR], F32, ph)
            cshift = sb("cshift", [F0, NTR], F32, ph)
            crows = sb("crows", [P, 7, F0], F32, ph)
            own = sb("own", [NP, NJ, F0], F32, ph)
            car = sb("car", [NP, NJ, F0], F32, ph)
            zr = sb("zr", [NP, NJ, H0], F32, ph)
            wv = sb("wv", [NP, NJ, D], F32, ph)
            wvT = sb("wvT", [D + 1, NJ * NP], F32, ph)
            hp = sb("hp", [NP, NJ, D], F32, ph)
            cen = sb("cen3", [NP, NJ, D], F32, ph)
            sq = sb("sq3", [NP, NJ, D], F32, ph)
            st = sb("st3", [NP, 4, NJ], F32, ph)
            q1n = sb("q1n", [NP, NJ, O1], F32, ph)
            last_got, last_mm, last_out = sem("last3_got"), sem("last3_mm"), sem("last3_out")
            d3, c_mm, c_out, c_put = sem("dstep3"), sem("c_mm"), sem("c_out"), sem("c_put")
            shift_ready, own_got, car_got, wv_ready = sem("shift_ready"), sem("own_got"), sem("car_got"), sem("wv_ready")
            t_mm, t_out, o_mm, o_out = sem("t3_mm"), sem("t3_out"), sem("o_mm"), sem("o_out")
            var3, std3, h1_ready, u_mm, u_out = sem("var3"), sem("std3"), sem("h1_ready"), sem("u_mm"), sem("u_out")
            q_mm, q_out, tab3, onesw = sem("q_mm"), sem("q_out"), sem("tab3"), sem("onesw")
            groups4 = [(a, min(a + 4, NJ)) for a in range(0, NJ, 4)]

            with nc.Block() as block:
                @block.gpsimd
                def _(pool):
                    pool.memset(wvT[D:D + 1, :], 1.0).then_inc(onesw, 1)
                    for j in range(NJ):
                        pool.indirect_dma_start(
                            own[:, j, :], None, sum0_edge,
                            bass.IndirectOffsetOnAxis(ap=last_i[:, j:j + 1], axis=0)).then_inc(own_got, 16)
                    pool.wait_ge(c_put, 16 * 7)
                    for j in range(NJ):
                        pool.indirect_dma_start(
                            car[:, j, :], None, carry0_tab,
                            bass.IndirectOffsetOnAxis(ap=tile_i[:, j:j + 1], axis=0)).then_inc(car_got, 16)

                @block.sync
                def _(sp):
                    load_last_rows(sp, lrows, sum0_edge, last_got)
                    for g, (a, b) in enumerate(c_groups):
                        sp.wait_ge(c_out, g + 1)
                        sp.dma_start(carry0_tab[a:b, :], crows[0:b - a, g, :]).then_inc(c_put, 16)
                    sp.wait_ge(h1_ready, 1)
                    sp.dma_start(h1_tab.rearrange("(p j) d -> p j d", j=NJ), cen[:, :, :]).then_inc(tab3, 16)
                    sp.wait_ge(q_out, len(groups4))
                    sp.dma_start(q1_tab[0:N, :].rearrange("(p j) d -> p j d", j=NJ), q1n[:, :, :]).then_inc(tab3, 16)
                    sp.wait_ge(tab3, 32)
                    sp.wait_ge(c_put, 16 * 7)

                @block.tensor
                def _(pe):
                    transpose_last_rows(pe, lrows, F0, last_got, last_mm)
                    pe.wait_ge(shift_ready, 1)
                    for g, (a, b) in enumerate(c_groups):
                        need(pe, c_out, g - 1)
                        nc.tensor.transpose(bank[g % 2][0:b - a, 0:F0], cshift[:, a:b], ident[0:F0, 0:F0])\
                                 .then_inc(c_mm, 1)
                    pe.wait_ge(wv_ready, 1)
                    pe.wait_ge(onesw, 1)
                    for g, (a, b) in enumerate(groups4):
                        need(pe, t_out, g - 1)
                        for j in range(a, b):
                            ins = nc.tensor.transpose(bank[2 + g % 2][0:D, (j - a) * NP:(j - a + 1) * NP],
                                                      wv[:, j, :], ident[0:NP, 0:NP])
                        ins.then_inc(t_mm, 1)
                    pe.wait_ge(t_out, len(groups4))
                    for g, (a, b) in enumerate(groups4):
                        if g >= 2:
                            pe.wait_ge(o_out, g - 1)
                        for j in range(a, b):
                            o = bank[4 + g % 2][0:NP, (j - a) * D:(j - a + 1) * D]
                            nc.tensor.matmul(o, hT[:, j * NP:(j + 1) * NP], WfA[:, :], start=True, stop=False)
                            ins = nc.tensor.matmul(o, wvT[:, j * NP:(j + 1) * NP], WoA[:, :], start=False, stop=True)
                        ins.then_inc(o_mm, 1)
                    pe.wait_ge(h1_ready, 1)
                    for g, (a, b) in enumerate(groups4):
                        if g >= 2:
                            pe.wait_ge(u_out, g - 1)
                        for j in range(a, b):
                            ins = nc.tensor.transpose(bank[6 + g % 2][0:D, (j - a) * NP:(j - a + 1) * NP],
                                                      cen[:, j, :], ident[0:NP, 0:NP])
                        ins.then_inc(u_mm, 1)
                    pe.wait_ge(u_out, len(groups4))
                    for g, (a, b) in enumerate(groups4):
                        if g >= 2:
                            pe.wait_ge(q_out, g - 1)
                        for j in range(a, b):
                            ins = nc.tensor.matmul(bank[g % 2][0:NP, (j - a) * O1:(j - a + 1) * O1],
                                                   hT[0:D, j * NP:(j + 1) * NP], Wq1s[:, :], start=True, stop=True)
                        ins.then_inc(q_mm, 1)

                @block.scalar
                def _(act):
                    copy_last(act, last, F0, last_mm, last_out)
                    for g, (a, b) in enumerate(c_groups):
                        act.wait_ge(c_mm, g + 1)
                        nc.scalar.activation(crows[0:b - a, g, :], bank[g % 2][0:b - a, 0:F0], ACT.Copy)\
                                 .then_inc(c_out, 1)
                    for g, (a, b) in enumerate(groups4):
                        act.wait_ge(t_mm, g + 1)
                        nc.scalar.activation(wvT[0:D, a * NP:b * NP], bank[2 + g % 2][0:D, 0:(b - a) * NP],
                                             ACT.Copy).then_inc(t_out, 1)
                    for g, (a, b) in enumerate(groups4):
                        act.wait_ge(o_mm, g + 1)
                        nc.scalar.activation(hp[:, a:b, :].rearrange("p a d -> p (a d)"),
                                             bank[4 + g % 2][0:NP, 0:(b - a) * D], ACT.Copy).then_inc(o_out, 1)
                    roots(act, st, var3, std3, 1)
                    roots(act, st, var3, std3, 2)
                    for g, (a, b) in enumerate(groups4):
                        act.wait_ge(u_mm, g + 1)
                        nc.scalar.activation(hT[0:D, a * NP:b * NP], bank[6 + g % 2][0:D, 0:(b - a) * NP],
                                             ACT.Copy).then_inc(u_out, 1)
                    for g, (a, b) in enumerate(groups4):
                        act.wait_ge(q_mm, g + 1)
                        nc.scalar.activation(q1n[:, a:b, :].rearrange("p a d -> p (a d)"),
                                             bank[g % 2][0:NP, 0:(b - a) * O1], ACT.Copy).then_inc(q_out, 1)

                @block.vector
                def _(dve):
                    step = Chain(dve, d3)
                    dve.wait_ge(last_out, 2)
                    step(dve.tensor_tensor_scan(full[:, :], cont[0:F0, :], last[:, :], 0.0, ALU.mult, ALU.add))
                    step(dve.memset(cshift[:, 0:1], 0.0))
                    step(dve.tensor_copy(cshift[:, 1:], full[:, 0:NTR - 1]))
                    dve.sem_inc(shift_ready, 1)
                    dve.wait_ge(own_got, 16 * NJ)
                    dve.wait_ge(car_got, 16 * NJ)
                    step(dve.tensor_tensor(own[:, :, :], own[:, :, :], bcast(has[:, :], 2, F0), ALU.mult))
                    step(dve.tensor_tensor(car[:, :, :], car[:, :, :], bcast(over[:, :], 2, F0), ALU.mult))
                    step(dve.tensor_tensor(own[:, :, :], own[:, :, :], car[:, :, :], ALU.add))
                    step(dve.tensor_scalar(zr[:, :, :], own[:, :, D:F0], 1.0, None, ALU.add))
                    step(dve.reciprocal(zr[:, :, :], zr[:, :, :]))
                    for h in range(H0):
                        step(dve.tensor_tensor(wv[:, :, h * DH:(h + 1) * DH], own[:, :, h * DH:(h + 1) * DH],
                                               zr[:, :, h:h + 1].broadcast_to([NP, NJ, DH]), ALU.mult))
                    dve.sem_inc(wv_ready, 1)
                    dve.wait_ge(o_out, len(groups4))
                    layer_norm(dve, step, hp[:, :, :], cen[:, :, :], sq[:, :, :], st, var3, std3, 1)
                    step(dve.tensor_tensor(cen[:, :, :], cen[:, :, :], bcast(g0b[:, :], 1, NJ), ALU.mult))
                    step(dve.tensor_tensor(cen[:, :, :], cen[:, :, :], bcast(be0b[:, :], 1, NJ), ALU.add))
                    step(dve.tensor_tensor(hp[:, :, :], hp[:, :, :], cen[:, :, :], ALU.add))
                    step(dve.tensor_tensor(xs[:, :, :], xs[:, :, :], hp[:, :, :], ALU.add))
                    layer_norm(dve, step, xs[:, :, :], cen[:, :, :], sq[:, :, :], st, var3, std3, 2)
                    dve.tensor_scalar(cen[:, :, :], cen[:, :, :], 0.0, None, ALU.max).then_inc(h1_ready, 1)

        attn = sb("attn", [P, NT * H1])
        ph = ExitStack()
        with ph:
            sh = [sb(f"sh{b}", [P, Q, S], F32, ph) for b in range(2)]
            xg = [sb(f"xg{b}", [P, Q, D], F32, ph) for b in range(2)]
            qg = [sb(f"qg{b}", [P, Q, O1], F32, ph) for b in range(2)]
            idx_x = [sb(f"idx_x{b}", [P, Q], I32, ph) for b in range(2)]
            idx_q = [sb(f"idx_q{b}", [P, Q], I32, ph) for b in range(2)]
            z = [sb(f"z{b}", [P, Q, (S + 1) * D], F32, ph) for b in range(2)]
            z_hi = [sb(f"z_hi{b}", [P, 5, Q * P], F32R, ph) for b in range(2)]
            z_lo = [sb(f"z_lo{b}", [P, 5, Q * P], F32R, ph) for b in range(2)]
            hid = sb("hid", [O1, Q * P], F32, ph)
            hid_hi = sb("hid_hi", [O1, Q * P], F32R, ph)
            hid_lo = sb("hid_lo", [O1, Q * P], F32R, ph)
            wsb = sb("wsb", [P, Q, 2 * O1], F32, ph)
            kvs = [sb(f"kvs{b}", [P, Q, 2 * O1], F32, ph) for b in range(2)]
            kq = sb("kq", [P, Q * O1], F32, ph)
            ef_in = [sem(f"ef_in{b}") for b in range(2)]
            sh_in = [sem(f"sh_in{b}") for b in range(2)]
            ef_tail, sh_tail = sem("ef_tail"), sem("sh_tail")
            x_got = [sem(f"x_got{b}") for b in range(2)]
            q_got = [sem(f"q_got{b}") for b in range(2)]
            v_out = [sem(f"v_out{b}") for b in range(2)]
            idx_x_set, idx_q_set, idy_turn = sem("idx_x_set"), sem("idx_q_set"), sem("idy_turn")
            z_ready, hid_mm, hid_out, hid_split = sem("z_ready"), sem("hid_mm"), sem("hid_out"), sem("hid_split")
            zT_mm, hi_out, lo_out, w_mm, w_out = sem("zT_mm"), sem("hi_out"), sem("lo_out"), sem("w_mm"), sem("w_out")
            a_mm, kv_ready, kq_ready, attn_ready = sem("a_mm"), sem("kv_ready"), sem("kq_ready"), sem("attn_ready")
            pe_turn = sem("pe_turn")
            KROWS = [P] * 4 + [D]
            CHUNK = [4, 0, 1, 2, 3]
            ZB = [0, 1, 2, 0, 1]
            ZB_BEFORE = [-2, -1, -3, 0, 1]
            TAIL = E - (NST - 1) * ST

            def load_rows(sp, i, t, a, got, got_tail):
                if not isinstance(i, int) or i < NST - 1:
                    sp.dma_start(t, a[bass.ds(i * ST, ST), :].rearrange("(q p) d -> p q d", p=P)).then_inc(got, 16)
                    return
                lo, q, n = i * ST, TAIL // P, TAIL % P
                sp.dma_start(t[:, 0:q, :], a[lo:lo + q * P, :].rearrange("(q p) d -> p q d", p=P)).then_inc(got, 16)
                sp.dma_start(t[0:n, q, :], a[lo + q * P:E, :]).then_inc(got_tail, 16)

            with nc.Block() as block:
                @block.sync
                def _(sp):
                    def load_sh(it, i, b):
                        need(sp, z_ready, i * 2 - 2)
                        load_rows(sp, i, sh[b][:, :, :], ea9, sh_in[b], sh_tail)

                    def load_ef(it, i, b):
                        need(sp, zT_mm, i * 5 - 9)
                        load_rows(sp, i, z[b][:, :, S * D:], ea64, ef_in[b], ef_tail)

                    def store(it, i, b):
                        sp.wait_ge(kv_ready, i * 2 + 2)
                        sp.dma_start(v1_edge[bass.ds(i, 1)].rearrange("a p (q o) -> p (a q) o", q=Q),
                                     kvs[b][:, :, O1:2 * O1]).then_inc(v_out[b], 16)

                    pipelined(sp, [(load_sh, 3), (load_ef, 2), (store, -1)])
                    for b in range(2):
                        sp.wait_ge(v_out[b], 16 * (NST // 2))

                @block.gpsimd
                def _(pool):
                    def gather_x(it, i, b):
                        need(pool, z_ready, i * 2 - 2)
                        pool.tensor_copy(idx_x[b][:, :], src_i[:, bass.ds(i * Q, Q)]).then_inc(idx_x_set, 1)
                        pool.wait_ge(idx_x_set, i + 1)
                        pool.sem_inc(idy_turn, 1)
                        for q in range(Q):
                            pool.indirect_dma_start(
                                xg[b][:, q, :], None, h1_tab,
                                bass.IndirectOffsetOnAxis(ap=idx_x[b][:, q:q + 1], axis=0)).then_inc(x_got[b], 16)

                    def gather_q(it, i, b):
                        need(pool, kq_ready, i - 1)
                        pool.tensor_copy(idx_q[b][:, :], dst_i[:, bass.ds(i * Q, Q)]).then_inc(idx_q_set, 1)
                        pool.wait_ge(idx_q_set, i + 1)
                        pool.sem_inc(idy_turn, 1)
                        for q in range(Q):
                            pool.indirect_dma_start(
                                qg[b][:, q, :], None, q1_tab,
                                bass.IndirectOffsetOnAxis(ap=idx_q[b][:, q:q + 1], axis=0)).then_inc(q_got[b], 16)

                    pipelined(pool, [(gather_x, 3), (gather_q, 1)])

                @block.tensor
                def _(pe):
                    def t_z(k):
                        c = CHUNK[k]

                        def stage(it, i, b):
                            if k == 0:
                                pe.wait_ge(z_ready, i * 2 + 2)
                                pe.wait_ge(ef_in[b], 16 * (it + 1))
                                if isinstance(i, int) and i == NST - 1:
                                    pe.wait_ge(ef_tail, 16)
                            need(pe, lo_out, i * 5 + ZB_BEFORE[k] + 1)
                            for q in range(Q):
                                ins = nc.tensor.transpose(bank[ZB[k]][:, q * P:(q + 1) * P],
                                                          z[b][:, q, c * P:(c + 1) * P], ident[:, :])
                            ins.then_inc(zT_mm, 1)
                        return stage

                    def m_hid(it, i, b):
                        pe.wait_ge(lo_out, i * 5 + 1)
                        need(pe, hid_out, i * 2)
                        parts = [(z_hi, W1_hi), (z_hi, W1_lo), (z_lo, W1_hi)]
                        for n, (zt, wt) in enumerate(parts):
                            ins = nc.tensor.matmul(bank[3][:, :], wt[D:2 * D, :], zt[b][D:2 * D, 4, :],
                                                   start=(n == 0), stop=(n == 2))
                        ins.then_inc(hid_mm, 1)

                    def m_w(half):
                        def stage(it, i, b):
                            pe.wait_ge(hid_split, i + 1)
                            need(pe, w_out, i * 2 + half - 1)
                            parts = [(hid_hi, W2_hi), (hid_hi, W2_lo), (hid_lo, W2_hi)]
                            for r in range(2):
                                q = 2 * half + r
                                for n, (ht, wt) in enumerate(parts):
                                    ins = nc.tensor.matmul(bank[4 + half][:, r * 2 * O1:(r + 1) * 2 * O1],
                                                           ht[:, q * P:(q + 1) * P], wt[:, :],
                                                           start=(n == 0), stop=(n == 2))
                            ins.then_inc(w_mm, 1)
                        return stage

                    def m_acc(q):
                        def stage(it, i, b):
                            pe.wait_ge(lo_out, i * 5 + 5)
                            need(pe, kv_ready, i * 2 + q // 2 - 1)
                            e = slice(q * P, (q + 1) * P)
                            parts = [(z_hi, C_hi), (z_hi, C_lo), (z_lo, C_hi)]
                            for n, (c, (zt, ct)) in enumerate((c, t) for c in range(5) for t in parts):
                                ins = nc.tensor.matmul(bank[6 + q // 2][:, (q % 2) * 2 * O1:(q % 2 + 1) * 2 * O1],
                                                       zt[b][0:KROWS[c], c, e], ct[0:KROWS[c], c, :],
                                                       start=(n == 0), stop=(n == 14))
                            if q % 2:
                                ins.then_inc(a_mm, 1)
                        return stage

                    pipelined(pe, [(t_z(0), 1), (m_acc(0), 0), (m_w(0), 0), (t_z(1), 1), (m_acc(1), 0),
                                   (m_w(1), 0), (t_z(2), 1), (m_acc(2), 0), (t_z(3), 1), (m_hid, 1), (t_z(4), 1),
                                   (m_acc(3), 0)])

                @block.scalar
                def _(act):
                    def hi(k):
                        def stage(it, i, b):
                            act.wait_ge(zT_mm, i * 5 + k + 1)
                            need(act, a_mm, i * 2 - 2)
                            nc.scalar.activation(z_hi[b][:, CHUNK[k], :], bank[ZB[k]][:, :], ACT.Copy).then_inc(hi_out, 1)
                        return stage

                    def hidden(it, i, b):
                        act.wait_ge(hid_mm, i + 1)
                        need(act, hid_split, i)
                        nc.scalar.activation(hid[:, :], bank[3][:, :], ACT.Relu, bias=b1[:, 0:1]).then_inc(hid_out, 1)

                    def hidden_hi(it, i, b):
                        need(act, w_mm, i * 2)
                        nc.scalar.activation(hid_hi[:, :], bank[3][:, :], ACT.Relu, bias=b1[:, 0:1])\
                                 .then_inc(hid_out, 1)
                    pipelined(act, [(hi(0), 1), (hi(1), 1), (hi(2), 1), (hi(3), 1), (hidden, 1), (hi(4), 1),
                                    (hidden_hi, 1)])

                @block.vector
                def _(dve):
                    dve.memset(attn[:, NTR * H1:], 0.0).then_inc(attn_ready, 1)

                    def outer(half):
                        tiles = slice(half * Q // 2, (half + 1) * Q // 2)

                        def stage(it, i, b):
                            if half == 0:
                                dve.wait_ge(x_got[b], 16 * Q * (it + 1))
                                dve.wait_ge(sh_in[b], 16 * (it + 1))
                                if isinstance(i, int) and i == NST - 1:
                                    dve.wait_ge(sh_tail, 16)
                                need(dve, zT_mm, i * 5 - 5)
                            dve.tensor_tensor(z[b][:, tiles, 0:S * D].rearrange("p q (s d) -> p q s d", d=D),
                                              bcast(xg[b][:, tiles, :], 2, S), bcast(sh[b][:, tiles, :], 3, D),
                                              ALU.mult).then_inc(z_ready, 1)
                        return stage

                    def lo(k):
                        def stage(it, i, b):
                            dve.wait_ge(hi_out, i * 5 + k + 1)
                            need(dve, a_mm, i * 2 - 2)
                            c = CHUNK[k]
                            dve.tensor_tensor(z_lo[b][:, c, :], bank[ZB[k]][:, :], z_hi[b][:, c, :].bitcast(F32),
                                              ALU.subtract).then_inc(lo_out, 1)
                        return stage

                    def hidden_lo(it, i, b):
                        dve.wait_ge(hid_out, i * 2 + 2)
                        need(dve, w_mm, i * 2)
                        dve.tensor_tensor(hid_lo[:, :], hid[:, :], hid_hi[:, :].bitcast(F32), ALU.subtract)\
                           .then_inc(hid_split, 1)

                    def bias(half):
                        def stage(it, i, b):
                            dve.wait_ge(w_mm, i * 2 + half + 1)
                            need(dve, kv_ready, i * 2 + half - 1)
                            dve.tensor_tensor(wsb[:, 2 * half:2 * half + 2, :],
                                              bank[4 + half][:, :].rearrange("p (q o) -> p q o", q=2),
                                              bcast(b2[:, :], 1, 2), ALU.add).then_inc(w_out, 1)
                        return stage

                    def product(half):
                        def stage(it, i, b):
                            need(dve, v_out[b], it * 16)
                            dve.wait_ge(a_mm, i * 2 + half + 1)
                            dve.wait_ge(w_out, i * 2 + half + 1)
                            dve.tensor_tensor(kvs[b][:, 2 * half:2 * half + 2, :], wsb[:, 2 * half:2 * half + 2, :],
                                              bank[6 + half][:, :].rearrange("p (q o) -> p q o", q=2), ALU.mult)\
                               .then_inc(kv_ready, 1)
                        return stage

                    def logits(it, i, b):
                        dve.wait_ge(q_got[b], 16 * Q * (it + 1))
                        dve.wait_ge(kv_ready, i * 2 + 2)
                        dve.wait_ge(attn_ready, i + 1)
                        dve.tensor_tensor(kq[:, :].rearrange("p (q o) -> p q o", q=Q), kvs[b][:, :, 0:O1],
                                          qg[b][:, :, :], ALU.mult).then_inc(kq_ready, 1)
                        dve.wait_ge(kq_ready, i + 1)
                        dve.tensor_reduce(attn[:, bass.ds(i * (Q * H1), Q * H1)],
                                          kq[:, :].rearrange("p (g d) -> p g d", d=DH), AX.X, ALU.add)\
                           .then_inc(attn_ready, 1)

                    pipelined(dve, [(product(1), -1), (lo(0), 1), (outer(0), 2), (bias(0), 0), (lo(1), 1),
                                    (logits, -1), (product(0), 0), (bias(1), 0), (lo(2), 1), (outer(1), 2),
                                    (lo(3), 1), (lo(4), 1), (hidden_lo, 1)])

        ph = ExitStack()
        with ph:
            A = sb("A", [P, U], F32, ph)
            Fs = sb("Fs", [P, U], F32, ph)
            X = sb("X", [P, U + 2], F32, ph)
            NE = sb("NE", [P, U + 1], BF16, ph)
            CT = sb("CT", [P, U + 1], BF16, ph)
            sel8 = sb("sel8", [P, H1], F32, ph)
            selT = sb("selT", [H1, P], F32, ph)
            chm = sb("chm", [P, CH], F32, ph)
            sums = sb("sums", [P, 2], F32, ph)
            spread = sb("spread", [P, 2, CH], F32, ph)
            per_head = sb("per_head", [H1, 2, CH], F32, ph)
            run = sb("run", [H1, CH], F32, ph)
            carry = sb("carry", [H1, CH], F32, ph)
            back = sb("back", [P, CH], F32, ph)
            cin = sb("cin", [P, 1], F32, ph)
            starts = sb("starts", [P, 2], F32, ph)
            d5, dst_in, a_tr, a_cp = sem("dstep5"), sem("dst_in"), sem("a_tr"), sem("a_cp")
            sel_ready, selT_mm, spr_ready, head_mm, car_ready, back_mm = (
                sem("sel_ready"), sem("selT_mm"), sem("spr_ready"), sem("head_mm"), sem("car_ready"), sem("back_mm"))
            sub_ready, ex_ready, alpha_ready, b_tr, b_cp = (sem("sub_ready"), sem("ex_ready"), sem("alpha_ready"),
                                                            sem("b_tr"), sem("b_cp"))
            perm_ready, x0_set = sem("perm_ready"), sem("x0_set")
            groups = [(a, min(a + 4, TC)) for a in range(0, TC, 4)]
            attn_v = attn[:, :].rearrange("p (j c h) -> p c j h", j=CH, h=H1)

            with nc.Block() as block:
                @block.sync
                def _(sp):
                    flat = dst_tab.rearrange("t p -> (t p)")
                    for j in range(CH):
                        lo = 1 if j == 0 else 0
                        sp.dma_start(X[j * H1:(j + 1) * H1, lo:].bitcast(I32),
                                     flat[j * U - 1 + lo:j * U + U + 1].unsqueeze(0).broadcast_to([H1, U + 2 - lo]))\
                          .then_inc(dst_in, 16)
                    sp.wait_ge(dst_in, 16 * CH)

                @block.gpsimd
                def _(pool):
                    pool.memset(X[0:H1, 0:1].bitcast(I32), -1).then_inc(x0_set, 1)

                @block.tensor
                def _(pe):
                    pe.wait_ge(perm_ready, 1)
                    for g, (a, b) in enumerate(groups):
                        need(pe, a_cp, g - 1)
                        for c in range(a, b):
                            ins = nc.tensor.transpose(bank[g % 2][:, (c - a) * P:(c - a + 1) * P],
                                                      Fs[:, c * P:(c + 1) * P], ident[:, :])
                        ins.then_inc(a_tr, 1)
                    pe.wait_ge(sel_ready, 1)
                    nc.tensor.transpose(bank[2][0:H1, 0:P], sel8[:, :], ident[:, :]).then_inc(selT_mm, 1)
                    for k in range(4):
                        pe.wait_ge(spr_ready, k + 1)
                        nc.tensor.matmul(bank[3][0:H1, 0:2 * CH], sel8[:, :],
                                         spread[:, :, :].rearrange("p a c -> p (a c)"), start=True, stop=True)\
                                 .then_inc(head_mm, 1)
                        pe.wait_ge(car_ready, k + 1)
                        nc.tensor.matmul(bank[4][:, 0:CH], selT[:, :], carry[:, :], start=True, stop=True)\
                                 .then_inc(back_mm, 1)
                    pe.wait_ge(alpha_ready, 1)
                    for g, (a, b) in enumerate(groups):
                        need(pe, b_cp, g - 1)
                        for c in range(a, b):
                            ins = nc.tensor.transpose(bank[5 + g % 2][:, (c - a) * P:(c - a + 1) * P],
                                                      A[:, c * P:(c + 1) * P], ident[:, :])
                        ins.then_inc(b_tr, 1)

                @block.scalar
                def _(act):
                    nc.scalar.activation(Fs[:, :].rearrange("p (c j h) -> p c j h", c=TC, h=H1), attn_v[:, :],
                                         ACT.Copy).then_inc(perm_ready, 1)
                    for g, (a, b) in enumerate(groups):
                        act.wait_ge(a_tr, g + 1)
                        nc.scalar.activation(A[:, a * P:b * P], bank[g % 2][:, 0:(b - a) * P], ACT.Copy)\
                                 .then_inc(a_cp, 1)
                    act.wait_ge(sub_ready, 1)
                    nc.scalar.activation(A[:, :], A[:, :], ACT.Exp).then_inc(ex_ready, 1)
                    for g, (a, b) in enumerate(groups):
                        act.wait_ge(b_tr, g + 1)
                        nc.scalar.activation(attn_v[:, a:b], bank[5 + g % 2][:, 0:(b - a) * P].rearrange(
                            "p (c j h) -> p c j h", c=b - a, h=H1), ACT.Copy).then_inc(b_cp, 1)

                @block.vector
                def _(dve):
                    step = Chain(dve, d5)
                    rev = slice(None, None, -1)
                    carries = [0]

                    def carry_in(last, flag, forward, largest):
                        carries[0] += 1
                        step(dve.tensor_scalar(spread[:, 0, :], chm[:, :], last, None, ALU.mult))
                        step(dve.tensor_scalar(spread[:, 1, :], chm[:, :], flag, None, ALU.mult))
                        dve.sem_inc(spr_ready, 1)
                        dve.wait_ge(head_mm, carries[0])
                        step(dve.tensor_copy(per_head[:, :, :].rearrange("p a c -> p (a c)"),
                                             bank[3][0:H1, 0:2 * CH]))
                        if largest:
                            step(dve.tensor_scalar(per_head[:, 1, :], per_head[:, 1, :], -BIG, None, ALU.mult))
                            step(dve.tensor_tensor_scan(run[:, :], per_head[:, 1, :], per_head[:, 0, :], -BIG,
                                                        ALU.add, ALU.max))
                        else:
                            step(dve.tensor_scalar(per_head[:, 1, :], per_head[:, 1, :], -1.0, 1.0, ALU.mult, ALU.add))
                            r = slice(None) if forward else rev
                            step(dve.tensor_tensor_scan(run[:, r], per_head[:, 1, r], per_head[:, 0, r], 0.0,
                                                        ALU.mult, ALU.add))
                        if forward:
                            step(dve.memset(carry[:, 0:1], -BIG if largest else 0.0))
                            step(dve.tensor_copy(carry[:, 1:], run[:, 0:CH - 1]))
                        else:
                            step(dve.memset(carry[:, CH - 1:], 0.0))
                            step(dve.tensor_copy(carry[:, 0:CH - 1], run[:, 1:]))
                        dve.sem_inc(car_ready, 1)
                        dve.wait_ge(back_mm, carries[0])
                        step(dve.tensor_tensor(back[:, :], bank[4][:, 0:CH], chm[:, :], ALU.mult))
                        step(dve.tensor_reduce(cin[:, :], back[:, :], AX.X, ALU.add))

                    def spread_back():
                        step(dve.tensor_tensor(X[:, 0:U], Fs[:, :], NE[:, 1:U + 1], ALU.mult))

                        def scan(init):
                            step(dve.tensor_tensor_scan(Fs[:, rev], CT[:, 1:U + 1][:, rev], X[:, 0:U][:, rev], init,
                                                        ALU.mult, ALU.add))
                        scan(0.0)
                        carry_in(Fs[:, 0:1], starts[:, 1:2], False, False)
                        scan(cin[:, 0:1])

                    step(dve.tensor_reduce(sel8[:, :], ident[:, :].rearrange("p (j h) -> p h j", h=H1), AX.X, ALU.add))
                    dve.sem_inc(sel_ready, 1)
                    step(dve.tensor_reduce(chm[:, :], ident[:, :].rearrange("p (j h) -> p j h", h=H1), AX.X, ALU.add))
                    dve.wait_ge(selT_mm, 1)
                    step(dve.tensor_copy(selT[:, :], bank[2][0:H1, 0:P]))
                    dve.wait_ge(dst_in, 16 * CH)
                    dve.wait_ge(x0_set, 1)
                    Xi = X[:, :].bitcast(I32)
                    step(dve.tensor_tensor(NE[:, :], Xi[:, 1:], Xi[:, 0:U + 1], ALU.not_equal))
                    step(dve.tensor_scalar(CT[:, :], NE[:, :], -1.0, 1.0, ALU.mult, ALU.add))
                    step(dve.tensor_reduce(starts[:, 0:1], NE[:, 0:U], AX.X, ALU.max))
                    step(dve.tensor_reduce(starts[:, 1:2], NE[:, 1:U + 1], AX.X, ALU.max))
                    step(dve.tensor_scalar(X[:, 0:U], NE[:, 0:U], -BIG, None, ALU.mult))
                    dve.wait_ge(a_cp, len(groups))

                    def scan_max(init):
                        step(dve.tensor_tensor_scan(Fs[:, :], X[:, 0:U], A[:, :], init, ALU.add, ALU.max))
                    scan_max(-BIG)
                    carry_in(Fs[:, U - 1:U], starts[:, 0:1], True, True)
                    scan_max(cin[:, 0:1])
                    spread_back()
                    step(dve.tensor_tensor(A[:, :], A[:, :], Fs[:, :], ALU.subtract))
                    dve.sem_inc(sub_ready, 1)
                    dve.wait_ge(ex_ready, 1)

                    def scan_sum(init):
                        step(dve.tensor_tensor_scan(Fs[:, :], CT[:, 0:U], A[:, :], init, ALU.mult, ALU.add))
                    scan_sum(0.0)
                    carry_in(Fs[:, U - 1:U], starts[:, 0:1], True, False)
                    scan_sum(cin[:, 0:1])
                    spread_back()
                    step(dve.tensor_scalar(Fs[:, :], Fs[:, :], 1e-16, None, ALU.add))
                    step(dve.reciprocal(X[:, 0:U], Fs[:, :]))
                    step(dve.tensor_tensor(A[:, :], A[:, :], X[:, 0:U], ALU.mult))
                    dve.sem_inc(alpha_ready, 1)

        ph = ExitStack()
        with ph:
            vin = [sb(f"vin{b}", [P, Q * O1], F32, ph) for b in range(2)]
            va = [sb(f"va{b}", [P, Q * O1], F32, ph) for b in range(2)]
            drow = [sb(f"dsow{b}", [P, ST], I32, ph) for b in range(2)]
            same = [sb(f"samf{b}", [P, Q, P], F32, ph) for b in range(2)]
            rows = [sb(f"rowt{b}", [P, Q * O1], F32, ph) for b in range(2)]
            v_in = [sem(f"v_in{b}") for b in range(2)]
            drow_in = [sem(f"dsow_in{b}") for b in range(2)]
            rows_out = [sem(f"rowt_out{b}") for b in range(2)]
            same_ready, va_ready, sum_mm, rows_cp = (sem("samf_ready"), sem("va_ready"), sem("sum1_mm"),
                                                     sem("rowt_cp"))

            with nc.Block() as block:
                @block.sync
                def _(sp):
                    def load(it, i, b):
                        need(sp, same_ready, i - 1)
                        sp.dma_start(drow[b][:, :], dst_rows(i)).then_inc(drow_in[b], 16)
                        need(sp, va_ready, i - 1)
                        sp.dma_start(vin[b][:, :], v1_edge[bass.ds(i, 1)].rearrange("a p o -> p (a o)"))\
                          .then_inc(v_in[b], 16)

                    def store(it, i, b):
                        sp.wait_ge(rows_cp, i + 1)
                        sp.dma_start(sum1_edge[bass.ds(i * ST, ST), :].rearrange("(q p) d -> p q d", p=P),
                                     rows[b][:, :].rearrange("p (q o) -> p q o", q=Q)).then_inc(rows_out[b], 16)
                    pipelined(sp, [(load, 2), (store, 0)])
                    for b in range(2):
                        sp.wait_ge(rows_out[b], 16 * (NST // 2))

                @block.vector
                def _(dve):
                    def build(it, i, b):
                        dve.wait_ge(drow_in[b], 16 * (it + 1))
                        need(dve, sum_mm, i - 1)
                        dve.tensor_tensor(same[b][:, :, :], drow[b][:, :].rearrange("p (q e) -> p q e", q=Q),
                                          bcast(dst_e[:, bass.ds(i * Q, Q)], 2, P), ALU.is_equal)\
                           .then_inc(same_ready, 1)

                    def weigh(it, i, b):
                        dve.wait_ge(v_in[b], 16 * (it + 1))
                        need(dve, sum_mm, i - 1)
                        dve.tensor_tensor(va[b][:, :].rearrange("p (g d) -> p g d", d=DH),
                                          vin[b][:, :].rearrange("p (g d) -> p g d", d=DH),
                                          bcast(attn[:, bass.ds(i * (Q * H1), Q * H1)], 2, DH), ALU.mult)\
                           .then_inc(va_ready, 1)
                    pipelined(dve, [(build, 0), (weigh, 0)])

                @block.tensor
                def _(pe):
                    def sums(it, i, b):
                        pe.wait_ge(va_ready, i + 1)
                        pe.wait_ge(same_ready, i + 1)
                        need(pe, rows_cp, i - 1)
                        for q in range(Q):
                            ins = nc.tensor.matmul(bank[b][:, q * O1:(q + 1) * O1], same[b][:, q, :],
                                                   va[b][:, q * O1:(q + 1) * O1], start=True, stop=True)
                        ins.then_inc(sum_mm, 1)
                    pipelined(pe, [(sums, 0)])

                @block.scalar
                def _(act):
                    def sums(it, i, b):
                        act.wait_ge(sum_mm, i + 1)
                        need(act, rows_out[b], it * 16)
                        nc.scalar.activation(rows[b][:, :], bank[b][:, :], ACT.Copy).then_inc(rows_cp, 1)
                    pipelined(act, [(sums, 0)])

        ph = ExitStack()
        with ph:
            lrows = sb("lrows7", [P, 7, O1], F32, ph)
            last = sb("last7", [O1, NTR], F32, ph)
            full = sb("full7", [O1, NTR], F32, ph)
            cshift = sb("cshift7", [O1, NTR], F32, ph)
            crows = sb("crows7", [P, 7, O1], F32, ph)
            own = sb("own7", [NP, NJ, O1], F32, ph)
            car = sb("car7", [NP, NJ, O1], F32, ph)
            updT = sb("updT", [O1, NJ * NP], F32, ph)
            o = sb("o", [NP, NJ, D], F32, ph)
            sq = sb("sq7", [NP, NJ, D], F32, ph)
            stat = sb("stat", [NP, 4, D], F32, ph)
            onesn = sb("onesn", [NP, NP], F32, ph)
            last_got, last_mm, last_out = sem("last7_got"), sem("last7_mm"), sem("last7_out")
            d7, c_mm, c_out, c_put = sem("dstep7"), sem("c7_mm"), sem("c7_out"), sem("c7_put")
            shift_ready, own_got, car_got, upd_ready = sem("shift7"), sem("own7_got"), sem("car7_got"), sem("upd_ready")
            t_mm, t_out, o_mm, o_out, ones7, part_ready, part_mm = (
                sem("t7_mm"), sem("t7_out"), sem("o7_mm"), sem("o7_out"), sem("ones7"), sem("part_ready"),
                sem("part_mm"))
            var7, std7, x_ready, out_sem = sem("var7"), sem("std7"), sem("x_ready"), sem("out_sem")
            groups4 = [(a, min(a + 4, NJ)) for a in range(0, NJ, 4)]
            groups8 = [(a, min(a + 8, NJ)) for a in range(0, NJ, 8)]

            with nc.Block() as block:
                @block.gpsimd
                def _(pool):
                    pool.memset(onesn[:, :], 1.0).then_inc(ones7, 1)
                    for j in range(NJ):
                        pool.indirect_dma_start(
                            own[:, j, :], None, sum1_edge,
                            bass.IndirectOffsetOnAxis(ap=last_i[:, j:j + 1], axis=0)).then_inc(own_got, 16)
                    pool.wait_ge(c_put, 16 * 7)
                    for j in range(NJ):
                        pool.indirect_dma_start(
                            car[:, j, :], None, carry1_tab,
                            bass.IndirectOffsetOnAxis(ap=tile_i[:, j:j + 1], axis=0)).then_inc(car_got, 16)

                @block.sync
                def _(sp):
                    load_last_rows(sp, lrows, sum1_edge, last_got)
                    for g, (a, b) in enumerate(c_groups):
                        sp.wait_ge(c_out, g + 1)
                        sp.dma_start(carry1_tab[a:b, :], crows[0:b - a, g, :]).then_inc(c_put, 16)
                    sp.wait_ge(c_put, 16 * 7)
                    sp.wait_ge(x_ready, 1)
                    sp.dma_start(out.rearrange("(p j) d -> p j d", j=NJ), xs[:, :, :]).then_inc(out_sem, 16)
                    sp.wait_ge(out_sem, 16)

                @block.tensor
                def _(pe):
                    transpose_last_rows(pe, lrows, O1, last_got, last_mm)
                    pe.wait_ge(shift_ready, 1)
                    for g, (a, b) in enumerate(c_groups):
                        need(pe, c_out, g - 1)
                        nc.tensor.transpose(bank[g % 2][0:b - a, 0:O1], cshift[:, a:b], ident[:, :]).then_inc(c_mm, 1)
                    pe.wait_ge(upd_ready, 1)
                    for g, (a, b) in enumerate(groups4):
                        need(pe, t_out, g - 1)
                        for j in range(a, b):
                            ins = nc.tensor.transpose(bank[2 + g % 2][:, (j - a) * NP:(j - a + 1) * NP],
                                                      own[:, j, :], ident[0:NP, 0:NP])
                        ins.then_inc(t_mm, 1)
                    pe.wait_ge(t_out, len(groups4))
                    for g, (a, b) in enumerate(groups8):
                        need(pe, o_out, g - 1)
                        for j in range(a, b):
                            r = bank[4 + g % 2][0:NP, (j - a) * D:(j - a + 1) * D]
                            nc.tensor.matmul(r, hT[0:D, j * NP:(j + 1) * NP], Wselfs[:, :], start=True, stop=False)
                            ins = nc.tensor.matmul(r, updT[:, j * NP:(j + 1) * NP], Wouts[:, :], start=False, stop=True)
                        ins.then_inc(o_mm, 1)
                    pe.wait_ge(ones7, 1)
                    for k in range(2):
                        pe.wait_ge(part_ready, k + 1)
                        nc.tensor.matmul(bank[6 + k][0:NP, 0:D], onesn[:, :], stat[:, k, :], start=True, stop=True)\
                                 .then_inc(part_mm, 1)

                @block.scalar
                def _(act):
                    copy_last(act, last, O1, last_mm, last_out)
                    for g, (a, b) in enumerate(c_groups):
                        act.wait_ge(c_mm, g + 1)
                        nc.scalar.activation(crows[0:b - a, g, :], bank[g % 2][0:b - a, 0:O1], ACT.Copy)\
                                 .then_inc(c_out, 1)
                    for g, (a, b) in enumerate(groups4):
                        act.wait_ge(t_mm, g + 1)
                        nc.scalar.activation(updT[:, a * NP:b * NP], bank[2 + g % 2][:, 0:(b - a) * NP],
                                             ACT.Copy).then_inc(t_out, 1)
                    for g, (a, b) in enumerate(groups8):
                        act.wait_ge(o_mm, g + 1)
                        nc.scalar.activation(o[:, a:b, :].rearrange("p a d -> p (a d)"),
                                             bank[4 + g % 2][0:NP, 0:(b - a) * D], ACT.Copy).then_inc(o_out, 1)
                    act.wait_ge(var7, 1)
                    nc.scalar.activation(stat[:, 3, :], stat[:, 2, :], ACT.Sqrt).then_inc(std7, 1)

                @block.vector
                def _(dve):
                    step = Chain(dve, d7)
                    dve.wait_ge(last_out, 2)
                    step(dve.tensor_tensor_scan(full[:, :], cont[:, :], last[:, :], 0.0, ALU.mult, ALU.add))
                    step(dve.memset(cshift[:, 0:1], 0.0))
                    step(dve.tensor_copy(cshift[:, 1:], full[:, 0:NTR - 1]))
                    dve.sem_inc(shift_ready, 1)
                    dve.wait_ge(own_got, 16 * NJ)
                    step(dve.tensor_tensor(own[:, :, :], own[:, :, :], bcast(has[:, :], 2, O1), ALU.mult))
                    dve.wait_ge(car_got, 16 * NJ)
                    step(dve.tensor_tensor(car[:, :, :], car[:, :, :], bcast(over[:, :], 2, O1), ALU.mult))
                    step(dve.tensor_tensor(own[:, :, :], own[:, :, :], car[:, :, :], ALU.add))
                    dve.sem_inc(upd_ready, 1)
                    dve.wait_ge(o_out, len(groups8))
                    dve.tensor_reduce(stat[:, 0, :], o[:, :, :].rearrange("p j d -> p d j"), AX.X, ALU.add)\
                       .then_inc(part_ready, 1)
                    dve.wait_ge(part_mm, 1)
                    step(dve.tensor_scalar(stat[:, 2, :], bank[6][0:NP, 0:D], 1.0 / N, None, ALU.mult))
                    step(dve.tensor_tensor(o[:, :, :], o[:, :, :], bcast(stat[:, 2, :], 1, NJ), ALU.subtract))
                    step(dve.tensor_tensor(sq[:, :, :], o[:, :, :], o[:, :, :], ALU.mult))
                    dve.tensor_reduce(stat[:, 1, :], sq[:, :, :].rearrange("p j d -> p d j"), AX.X, ALU.add)\
                       .then_inc(part_ready, 1)
                    dve.wait_ge(part_mm, 2)
                    dve.tensor_scalar(stat[:, 2, :], bank[7][0:NP, 0:D], 1.0 / N, BN_EPS, ALU.mult, ALU.add)\
                       .then_inc(var7, 1)
                    dve.wait_ge(std7, 1)
                    step(dve.reciprocal(stat[:, 2, :], stat[:, 3, :]))
                    step(dve.tensor_tensor(stat[:, 2, :], stat[:, 2, :], g1b[:, :], ALU.mult))
                    step(dve.tensor_tensor(o[:, :, :], o[:, :, :], bcast(stat[:, 2, :], 1, NJ), ALU.mult))
                    step(dve.tensor_tensor(o[:, :, :], o[:, :, :], bcast(be1b[:, :], 1, NJ), ALU.add))
                    dve.tensor_tensor(xs[:, :, :], xs[:, :, :], o[:, :, :], ALU.add).then_inc(x_ready, 1)


_INS = ["x", "src", "dst", "edge_attr_64", "edge_attr_9", "L0_gnn_Wq", "L0_gnn_bq", "L0_gnn_Wk", "L0_gnn_bk",
        "L0_gnn_Wv", "L0_gnn_bv", "L0_gnn_Wo", "L0_gnn_bo", "L0_gnn_Wf", "L0_gnn_bf", "L0_gnn_gamma",
        "L0_gnn_beta", "L1_gnn_Wq", "L1_gnn_Cqk", "L1_gnn_Cv", "L1_gnn_k_w1", "L1_gnn_k_b1", "L1_gnn_k_w2",
        "L1_gnn_k_b2", "L1_gnn_v_w1", "L1_gnn_v_b1", "L1_gnn_v_w2", "L1_gnn_v_b2", "L1_gnn_W_out",
        "L1_gnn_W_self", "L1_gnn_gamma", "L1_gnn_beta"]


def kernel(**inputs):
    import numpy as np
    import concourse.bacc as bacc
    from concourse.bass_utils import run_bass_kernel_spmd

    nc = bacc.Bacc("TRN2", target_bir_lowering=False, num_devices=1)
    arrays, args = {}, []
    for name in _INS:
        a = np.ascontiguousarray(inputs[name])
        arrays[f"in_{name}"] = a
        args.append(nc.dram_tensor(f"in_{name}", a.shape, mybir.dt.from_np(a.dtype), kind="ExternalInput").ap())
    out = nc.dram_tensor("out", (N, D), F32, kind="ExternalOutput").ap()
    gnn(nc, *args, out)
    return run_bass_kernel_spmd(nc, [arrays], core_ids=[0]).results[0]["out"]
```

```python
from contextlib import ExitStack

import concourse.bass as bass
from concourse import mybir
from concourse.alu_op_type import AluOpType as ALU

F32 = mybir.dt.float32
F32R = mybir.dt.float32r
BF16 = mybir.dt.bfloat16
I32 = mybir.dt.int32
I16 = mybir.dt.int16
ACT = mybir.ActivationFunctionType
AX = mybir.AxisListType

P = 128
N = 3125
D = 64
E = 103125
S = 9
H0, DH = 4, 16
H1 = 8
O1 = H1 * DH
NP, NJ = 125, 25
Q = 4
ST = Q * P
NST = -(-E // ST)
CH = 16
TC = 51
NT = CH * TC
EP = NT * P
U = TC * P
PAD = N
NTE = -(-E // P)
NTR = NST * Q
BIG = 1.5e38
LN_EPS = BN_EPS = 1e-5
SCALE0, CLIP = 1.0 / 8.0, 5.0
F0 = D + H0
F1 = O1 + H1


def need(eng, sem, n):
    if not isinstance(n, int) or n > 0:
        eng.wait_ge(sem, n)


def pipelined(eng, stages):
    most, least = max(a for _, a in stages), min(a for _, a in stages)

    def step(it, i, b):
        for f, a in stages:
            if not isinstance(i, int) or 0 <= i + a < NST:
                f(it + (b + a) // 2, i + a, (b + a) % 2)

    first = max(1, (2 - least) // 2)
    end = (NST - 1 - max(most, 0)) // 2
    for i in range(-max(most, 0), 2 * first):
        step(i // 2, i, i % 2)
    with eng.Fori(first, end) as it:
        for b in range(2):
            step(it, it * 2 + b, b)
    for i in range(2 * end, NST - least):
        step(i // 2, i, i % 2)


class Chain:

    def __init__(self, eng, sem):
        self.eng, self.sem, self.n = eng, sem, 0

    def __call__(self, ins):
        ins.then_inc(self.sem, 1)
        self.n += 1
        self.eng.wait_ge(self.sem, self.n)


def bcast(ap, axis, n):
    ap = ap.unsqueeze(axis)
    shape = list(ap.shape)
    shape[axis] = n
    return ap.broadcast_to(shape)


def gnn(nc, x, src, dst, ea64, ea9, Wq0, bq0, Wk0, bk0, Wv0, bv0, Wo0, bo0, Wf0, bf0, g0, be0,
        Wq1, Cqk, Cv, kw1, kb1, kw2, kb2, vw1, vb1, vw2, vb2, Wout, Wself, g1, be1, out):
    ctx = ExitStack()

    def sb(name, shape, dt=F32, where=None):
        return (where or ctx).enter_context(nc.sbuf_tensor(name, shape, dt))

    def sem(name):
        return ctx.enter_context(nc.semaphore(name))

    def dram(name, shape, dt=F32):
        return nc.dram_tensor(name, shape, dt, kind="Internal").ap()

    with ctx:
        dst_tab = dram("dst_tab", (NT + 1, P), I32)
        src_tab = dram("src_tab", (NT, P), I32)
        assert PAD + 1 < 2 ** 15
        dst16_tab = dram("dst16_tab", (NT, P), I16)
        kv0_tab = dram("kv0_tab", (N, 2 * D))
        q0_tab = dram("q0_tab", (N + 1, D))
        q0_edge = dram("q0_edge", (NTR * P, D))
        sum0_edge = dram("sum0_edge", (NTR * P, F0))
        carry0_tab = dram("carry0_tab", (NTR, F0))
        h1_tab = dram("h1_tab", (N, D))
        q1_tab = dram("q1_tab", (N + 1, O1))
        dst_s = dram("dst_s", (NTE * P, 1), I32)
        src_s = dram("src_s", (NTE * P, 1), I32)
        ea64_s = dram("ea64_s", (NTE * P, D))
        ea9_s = dram("ea9_s", (NTE * P, S))
        next_tab = dram("next_tab", (N + 1, 1), I32)
        v1_edge = dram("v1_edge", (NST, P, Q * O1))
        sum1_edge = dram("sum1_edge", (NTR * P, F1))
        carry1_tab = dram("carry1_tab", (NTR, F1))

        bank = [ctx.enter_context(nc.psum_tensor(f"bank{k}", [P, 512], F32)) for k in range(8)]

        ident = sb("ident", [P, P])
        W0 = sb("W0", [D + 1, 3 * D])
        WfA = sb("WfA", [D + 1, D])
        WoA = sb("WoA", [D + 1, D])
        Wq1s = sb("Wq1s", [D, O1])
        Wselfs = sb("Wselfs", [D, D])
        Wouts = sb("Wouts", [O1, D])
        W1_hi = sb("W1_hi", [P, O1], F32R)
        W1_lo = sb("W1_lo", [P, O1], F32R)
        b1 = sb("b1", [O1, 1])
        W2_hi = sb("W2_hi", [O1, 2 * O1], F32R)
        W2_lo = sb("W2_lo", [O1, 2 * O1], F32R)
        b2 = sb("b2", [P, 2 * O1])
        C_hi = sb("C_hi", [P, 5, 2 * O1], F32R)
        C_lo = sb("C_lo", [P, 5, 2 * O1], F32R)
        g0b = sb("g0b", [NP, D])
        be0b = sb("be0b", [NP, D])
        g1b = sb("g1b", [NP, D])
        be1b = sb("be1b", [NP, D])
        src_i = sb("src_i", [P, NT], I32)
        dst_i = sb("dst_i", [P, NT], I32)
        dst_e = sb("dst_e", [P, NT])
        cont = sb("cont", [P, NTR])
        last_i = sb("last_i", [NP, NJ], I32)
        tile_i = sb("tile_i", [NP, NJ], I32)
        has = sb("has", [NP, NJ])
        over = sb("over", [NP, NJ])
        unsorted = sb("unsorted", [P, 1], I32)
        xs = sb("xs", [NP, NJ, D])
        hT = sb("hT", [D + 1, NJ * NP])

        W_SEM = sem("weights_loaded")

        def layer_norm(dve, step, src_ap, cen, sq, st, var_ready, std_ready, k):
            step(dve.tensor_reduce(st[:, 0, :], src_ap, AX.X, ALU.add))
            step(dve.tensor_scalar(st[:, 0, :], st[:, 0, :], 1.0 / D, None, ALU.mult))
            step(dve.tensor_tensor(cen, src_ap, bcast(st[:, 0, :], 2, D), ALU.subtract))
            step(dve.tensor_tensor(sq, cen, cen, ALU.mult))
            step(dve.tensor_reduce(st[:, 1, :], sq, AX.X, ALU.add))
            dve.tensor_scalar(st[:, 1, :], st[:, 1, :], 1.0 / D, LN_EPS, ALU.mult, ALU.add)\
               .then_inc(var_ready, 1)
            dve.wait_ge(std_ready, k)
            step(dve.reciprocal(st[:, 3, :], st[:, 2, :]))
            step(dve.tensor_tensor(cen, cen, bcast(st[:, 3, :], 2, D), ALU.mult))

        def roots(act, st, var_ready, std_ready, k):
            act.wait_ge(var_ready, k)
            nc.scalar.activation(st[:, 2, :], st[:, 1, :], ACT.Sqrt).then_inc(std_ready, 1)

        ph = ExitStack()
        with ph:
            def tsb(name, shape, dt=F32):
                return sb(name, shape, dt, ph)

            ones = tsb("ones", [P, P])
            row_l = tsb("row_l", [P, P])
            C = tsb("C", [P, 5, 2 * O1])
            W1 = tsb("W1", [P, O1])
            W2 = tsb("W2", [O1, 2 * O1])
            padi = tsb("padi", [1, EP - E + P], I32)
            zrow = tsb("zrow", [P, 101, D])
            dst_r = tsb("dst_r", [P, 7, P], I32)
            src_r = tsb("src_r", [P, 7, P], I32)
            dst16_r = tsb("dst16_r", [P, 7, P], I16)
            first_i = tsb("first_i", [P, 7], I32)
            qfirst = tsb("qfirst", [P, 7, D])
            rows_f = tsb("rows_f", [P, 2, 7 * P])
            lastrow = tsb("lastrow", [P, NT])
            junk = tsb("junk", [P, NT])
            node_n = tsb("node_n", [NP, NJ + 1])
            tiles_n = tsb("tiles_n", [NP, NJ + 1])
            tiles_i = tsb("tiles_i", [NP, NJ + 1], I32)
            inner_n = tsb("inner_n", [NP, NJ + 1])
            upto = tsb("upto", [NP, NJ + 1])
            tile_rows = tsb("tile_rows", [NP, NJ + 1, P], I32)
            start_n = tsb("start_n", [NP, NJ])
            start_i = tsb("start_i", [NP, NJ], I32)
            tf = tsb("tf", [NP, 3, NJ])
            cen = tsb("cen", [NP, NJ, D])
            sq = tsb("sq", [NP, NJ, D])
            st = tsb("st", [NP, 4, NJ])
            kvq = tsb("kvq", [NP, NJ, 3 * D])
            qn = tsb("qn", [NP, NJ, D])

            x_in, lin, rows_in, pad_set = sem("x_in"), sem("lin"), sem("rows_in"), sem("pad_set")
            consts, poolc, dstep, rows_cast = sem("consts"), sem("poolc"), sem("dstep1"), sem("rows_cast")
            tpose, tpose_out, last_mm = sem("tpose"), sem("tpose_out"), sem("last_mm")
            var1, std1, h_ready, w2z = sem("var1"), sem("std1"), sem("h_ready"), sem("w2z")
            hT_mm, hT_out, proj_mm, proj_out, tabs = (sem("hT_mm"), sem("hT_out"), sem("proj_mm"),
                                                      sem("proj_out"), sem("tabs"))
            filled = [sem(f"filled{k}") for k in range(4)]
            tiles_ready, tiles_got, start_ready = sem("tiles_ready"), sem("tiles_got"), sem("start_ready")
            q_scat, first_set, first_got, first_put = sem("q_scat"), sem("first_set"), sem("first_got"), sem("first_put")
            w0_in = sem("w0_in")
            ranges_ready, dst16_set, dst16_out = sem("ranges_ready"), sem("dst16_set"), sem("dst16_out")
            hT_groups = [(a, min(a + 4, NJ)) for a in range(0, NJ, 4)]
            q0_fill = q0_edge.rearrange("(a p n) d -> a p n d", p=P, n=101)
            FILL_BEFORE = 17
            fill_parts = [(0, 26), (26, 51), (51, 76), (76, 101)]
            fills = [(q0_fill[a][:, lo:hi, :], zrow[:, lo:hi, :]) for a in range(NTR // 101) for lo, hi in fill_parts]
            n_groups = [(a, min(a + 5, NJ + 1)) for a in range(0, NJ + 1, 5)]
            pj_groups = [(a, min(a + 2, NJ)) for a in range(0, NJ, 2)]
            dst_flat = dst_tab.rearrange("t p -> (t p)")
            src_flat = src_tab.rearrange("t p -> (t p)")
            near = tsb("near", [P, 2, NTE], I32)
            down = tsb("down", [P, NTE])
            downs = tsb("downs", [P, 1])
            near_in, down_ready, down_mm, down_steps = sem("near_in"), sem("down_ready"), sem("down_mm"), sem("down_steps")

            loads0 = [(W0[0:D, 0:D], Wk0), (W0[0:D, D:2 * D], Wv0), (W0[0:D, 2 * D:3 * D], Wq0),
                     (W0[D:D + 1, 0:D], bk0.unsqueeze(0)), (W0[D:D + 1, D:2 * D], bv0.unsqueeze(0)),
                     (W0[D:D + 1, 2 * D:3 * D], bq0.unsqueeze(0))]
            loads = [(WfA[0:D, :], Wf0), (WfA[D:D + 1, :], bf0.unsqueeze(0)),
                     (WoA[0:D, :], Wo0), (WoA[D:D + 1, :], bo0.unsqueeze(0)),
                     (Wq1s[:, :], Wq1), (Wselfs[:, :], Wself), (Wouts[:, :], Wout),
                     (W1[D:2 * D, 0:D], kw1), (W1[D:2 * D, D:O1], vw1),
                     (b1[0:D, :], kb1.unsqueeze(1)), (b1[D:O1, :], vb1.unsqueeze(1)),
                     (W2[0:D, 0:O1], kw2), (W2[D:O1, O1:2 * O1], vw2),
                     (b2[:, 0:O1], kb2.unsqueeze(0).broadcast_to([P, O1])),
                     (b2[:, O1:2 * O1], vb2.unsqueeze(0).broadcast_to([P, O1]))]
            for r in range(2):
                loads += [(C[r * D:(r + 1) * D, 0:5 - r, 0:O1], Cqk[:, r::2, :]),
                          (C[r * D:(r + 1) * D, 0:5 - r, O1:2 * O1], Cv[:, r::2, :])]
            for dst_t, v in ((g0b, g0), (be0b, be0), (g1b, g1), (be1b, be1)):
                loads.append((dst_t[:, :], v.unsqueeze(0).broadcast_to([NP, D])))
            n_weights = 16 * len(loads)

            with nc.Block() as block:
                @block.sync
                def _(sp):
                    sp.dma_start(dst_flat[0:E].unsqueeze(0), dst.unsqueeze(0)).then_inc(lin, 16)
                    sp.dma_start(src_flat[0:E].unsqueeze(0), src.unsqueeze(0)).then_inc(lin, 16)
                    sp.dma_start(xs[:, :, :], x.rearrange("(p j) d -> p j d", j=NJ)).then_inc(x_in, 16)
                    sp.wait_ge(pad_set, 3)
                    sp.dma_start(dst_flat[E:EP + P].unsqueeze(0), padi[:, :]).then_inc(lin, 16)
                    sp.dma_start(src_flat[E:EP].unsqueeze(0), zrow[0:1, :, :].bitcast(I32).rearrange(
                        "p a d -> p (a d)")[:, 0:EP - E]).then_inc(lin, 16)
                    sp.wait_ge(lin, 64)
                    for n in range(2):
                        sp.dma_start(near[:, n, :], dst_flat[n:n + P * NTE].rearrange("(p e) -> p e", p=P))\
                          .then_inc(near_in, 16)
                    for k in range(4):
                        sp.dma_start(*fills[k]).then_inc(filled[k], 16)

                @block.scalar
                def _(act):
                    act.wait_ge(w2z, 1)
                    for a, b in loads0:
                        act.dma_start(a, b).then_inc(w0_in, 16)

                @block.gpsimd
                def _(pool):
                    pool.memset(padi[:, 0:EP - E], PAD).then_inc(pad_set, 1)
                    pool.memset(padi[:, EP - E:], PAD + 1).then_inc(pad_set, 1)
                    pool.memset(zrow[:, :, :], 0.0).then_inc(pad_set, 1)
                    pool.memset(W2[:, :], 0.0).then_inc(w2z, 1)
                    pool.memset(ident[:, :], 0.0).then_inc(poolc, 1)
                    pool.memset(row_l[:, :], 0.0).then_inc(poolc, 1)
                    pool.memset(ones[:, :], 1.0).then_inc(poolc, 1)
                    pool.wait_ge(poolc, 3)
                    pool.affine_select(out=ident[:, :], in_=ident[:, :], compare_op=ALU.not_equal, fill=1.0,
                                       base=0, pattern=[[-1, P]], channel_multiplier=1).then_inc(consts, 1)
                    pool.affine_select(out=row_l[:, :], in_=row_l[:, :], compare_op=ALU.not_equal, fill=1.0,
                                       base=1 - P, pattern=[[0, P]], channel_multiplier=1).then_inc(consts, 1)
                    pool.iota(node_n[:, :], [[1, NJ + 1]], base=-1, channel_multiplier=NJ,
                              allow_small_or_imprecise_dtypes=True).then_inc(consts, 1)
                    pool.wait_ge(consts, 3)
                    pool.memset(hT[D:D + 1, :], 1.0).then_inc(consts, 1)
                    pool.wait_ge(consts, 4)

                @block.vector
                def _(dve):
                    step = Chain(dve, down_steps)
                    dve.wait_ge(near_in, 32)
                    step(dve.tensor_tensor(down[:, :], near[:, 0, :], near[:, 1, :], ALU.is_gt))
                    dve.tensor_reduce(downs[:, :], down[:, :], AX.X, ALU.add).then_inc(down_ready, 1)
                    dve.wait_ge(down_mm, 1)
                    step(dve.tensor_copy(unsorted[:, :], bank[0][:, 0:1]))

                @block.tensor
                def _(pe):
                    pe.wait_ge(poolc, 3)
                    pe.wait_ge(down_ready, 1)
                    nc.tensor.matmul(bank[0][:, 0:1], ones[:, :], downs[:, :], start=True, stop=True)\
                             .then_inc(down_mm, 1)

            sort_ph = ExitStack()
            with sort_ph:
                W = 1875
                all_dst = sb("all_dst", [NP, W], I32, sort_ph)
                below = sb("below", [NP, W], F32, sort_ph)
                part = sb("part", [NP, NJ], F32, sort_ph)
                begin = sb("begin", [NP, NJ], F32, sort_ph)
                begin_i = sb("begin_i", [NP, NJ], I32, sort_ph)
                end_i = sb("end_i", [1, 1], I32, sort_ph)
                dcol_i = sb("dcol_i", [P, 1], I32, sort_ph)
                dcol_f = sb("dcol_f", [P, 1], F32, sort_ph)
                scol_i = sb("scol_i", [P, 1], I32, sort_ph)
                drow_i = sb("drow_i", [P, P], I32, sort_ph)
                rows64 = sb("rows64", [P, D], F32, sort_ph)
                rows9 = sb("rows9", [P, S], F32, sort_ph)
                equal = sb("equal", [P, P], F32, sort_ph)
                before = sb("before", [P, P], F32, sort_ph)
                earlier = sb("earlier", [P, P], F32, sort_ph)
                base_i = sb("base_i", [P, 1], I32, sort_ph)
                base_f = sb("base_f", [P, 1], F32, sort_ph)
                rank = sb("rank", [P, 2], F32, sort_ph)
                place = sb("place", [P, 2], F32, sort_ph)
                place_i = sb("place_i", [P, 2], I32, sort_ph)
                sort_sems = []

                def sort_sem(name):
                    sort_sems.append(nc.alloc_semaphore(name=name))
                    return sort_sems[-1]

                chunk_in, chunk_read, begun, begin_put = (sort_sem("chunk_in"), sort_sem("chunk_read"), sort_sem("begun"),
                                                          sort_sem("begin_put"))
                low_set, low_ready = sort_sem("low_set"), sort_sem("low_ready")
                tile_free, tile_in = sort_sem("tile_free"), sort_sem("tile_in")
                base_got, placed, put, sort_turn, back_in = (sort_sem("base_got"), sort_sem("placed"), sort_sem("put"),
                                                             sort_sem("sort_turn"), sort_sem("sorted_back"))
                count_step, place_step = sort_sem("count_step"), sort_sem("place_step")
                assert E % W == 0

                with nc.Block() as block:
                    @block.sync
                    def _(sp):
                        with sp.If(sp.value_load(unsorted[0:1, 0:1]) > 0):
                            with sp.Fori(0, E // W) as c:
                                sp.wait_ge(chunk_read, c + 1)
                                sp.dma_start(all_dst[:, :], dst_flat[bass.ds(c * W, W)].unsqueeze(0).broadcast_to([NP, W]))\
                                  .then_inc(chunk_in, 16)
                            sp.wait_ge(begun, 2)
                            sp.dma_start(next_tab[0:N, :].rearrange("(p j) a -> p (j a)", j=NJ), begin_i[:, :])\
                              .then_inc(begin_put, 16)
                            sp.dma_start(next_tab[N:N + 1, :], end_i[:, :]).then_inc(begin_put, 16)

                            def load(t, n):
                                sp.wait_ge(tile_free, t + 1)
                                of_tile = dst_tab[bass.ds(t, 1), :]
                                sp.dma_start(dcol_i[:, :], of_tile.rearrange("a p -> p a"),
                                             allow_slow_non_contiguous=True).then_inc(tile_in, 16)
                                sp.dma_start(drow_i[:, :], of_tile.broadcast_to([P, P])).then_inc(tile_in, 16)
                                sp.dma_start(scol_i[:, :], src_tab[bass.ds(t, 1), :].rearrange("a p -> p a"),
                                             allow_slow_non_contiguous=True)\
                                  .then_inc(tile_in, 16)
                                sp.dma_start(rows64[0:n, :], ea64[bass.ds(t * P, n), :]).then_inc(tile_in, 16)
                                sp.dma_start(rows9[0:n, :], ea9[bass.ds(t * P, n), :]).then_inc(tile_in, 16)
                            with sp.Fori(0, NTE - 1) as t:
                                load(t, P)
                            load(NTE - 1, E - (NTE - 1) * P)
                            sp.wait_ge(tile_free, NTE + 1)
                            for tab, rows in ((dst_flat, dst_s), (src_flat, src_s)):
                                sp.dma_start(tab[0:E].unsqueeze(0), rows[0:E, :].rearrange("e a -> a e"))\
                                  .then_inc(back_in, 16)
                            sp.wait_ge(back_in, 32)

                    @block.gpsimd
                    def _(pool):
                        with pool.If(pool.value_load(unsorted[0:1, 0:1]) > 0):
                            pool.memset(end_i[:, :], E).then_inc(begun, 1)
                            pool.memset(before[:, :], 1.0).then_inc(low_set, 1)
                            pool.wait_ge(low_set, 1)
                            pool.affine_select(out=before[:, :], in_=before[:, :], compare_op=ALU.is_gt, fill=0.0,
                                               base=0, pattern=[[-1, P]], channel_multiplier=1).then_inc(low_ready, 1)
                            pool.sem_inc(tile_free, 1)
                            pool.wait_ge(begin_put, 32)

                            def place_tile(t):
                                pool.wait_ge(tile_in, 80 * t + 80)
                                pool.sem_inc(sort_turn, 1)
                                pool.indirect_dma_start(
                                    base_i[:, :], None, next_tab,
                                    bass.IndirectOffsetOnAxis(ap=dcol_i[:, 0:1], axis=0)).then_inc(base_got, 16)
                                pool.wait_ge(placed, t + 1)
                                pool.sem_inc(sort_turn, 1)
                                pool.indirect_dma_start(
                                    next_tab, bass.IndirectOffsetOnAxis(ap=dcol_i[:, 0:1], axis=0),
                                    place_i[:, 1:2], None).then_inc(put, 16)
                                for tab, rows in ((dst_s, dcol_i), (src_s, scol_i), (ea64_s, rows64), (ea9_s, rows9)):
                                    pool.indirect_dma_start(
                                        tab, bass.IndirectOffsetOnAxis(ap=place_i[:, 0:1], axis=0),
                                        rows[:, :], None).then_inc(put, 16)
                                pool.wait_ge(put, 80 * t + 80)
                                pool.sem_inc(tile_free, 1)
                            with pool.Fori(0, NTE) as t:
                                place_tile(t)

                    @block.vector
                    def _(dve):
                        with dve.If(dve.value_load(unsorted[0:1, 0:1]) > 0):
                            dve.memset(begin[:, :], 0.0).then_inc(count_step, 1)
                            dve.wait_ge(count_step, 1)
                            dve.sem_inc(chunk_read, 1)
                            with dve.Fori(0, E // W) as c:
                                dve.wait_ge(chunk_in, 16 * c + 16)
                                for j in range(NJ):
                                    dve.tensor_scalar(below[:, :], all_dst[:, :], node_n[:, j:j + 1], 0.0, ALU.is_le,
                                                      ALU.add, accum_out=part[:, j:j + 1]).then_inc(count_step, 1)
                                    dve.wait_ge(count_step, c * (NJ + 1) + j + 2)
                                dve.tensor_tensor(begin[:, :], begin[:, :], part[:, :], ALU.add).then_inc(count_step, 1)
                                dve.wait_ge(count_step, c * (NJ + 1) + NJ + 2)
                                dve.sem_inc(chunk_read, 1)
                            dve.tensor_copy(begin_i[:, :], begin[:, :]).then_inc(begun, 1)
                            dve.wait_ge(low_ready, 1)
                            with dve.Fori(0, NTE) as t:
                                dve.wait_ge(tile_in, 80 * t + 80)
                                ops = 6

                                def done(n):
                                    dve.wait_ge(place_step, t * ops + n)
                                dve.tensor_copy(dcol_f[:, :], dcol_i[:, :]).then_inc(place_step, 1)
                                done(1)
                                dve.tensor_scalar(equal[:, :], drow_i[:, :], dcol_f[:, 0:1], 0.0, ALU.is_equal, ALU.add,
                                                  accum_out=rank[:, 1:2]).then_inc(place_step, 1)
                                done(2)
                                dve.tensor_tensor(earlier[:, :], equal[:, :], before[:, :], ALU.mult)\
                                   .then_inc(place_step, 1)
                                done(3)
                                dve.tensor_reduce(rank[:, 0:1], earlier[:, :], AX.X, ALU.add).then_inc(place_step, 1)
                                done(4)
                                dve.wait_ge(base_got, 16 * t + 16)
                                dve.tensor_copy(base_f[:, :], base_i[:, :]).then_inc(place_step, 1)
                                done(5)
                                dve.tensor_scalar(place[:, :], rank[:, :], base_f[:, 0:1], None, ALU.add)\
                                   .then_inc(place_step, 1)
                                done(6)
                                dve.tensor_copy(place_i[:, :], place[:, :]).then_inc(placed, 1)

            nc.clear_and_free_semaphores(sort_sems)

            with nc.Block() as block:
                @block.sync
                def _(sp):
                    for rows, tab in ((dst_r, dst_tab), (src_r, src_tab)):
                        sp.dma_start(rows[:, 0:6, :], tab[0:6 * P, :].rearrange("(g t) p -> t g p", g=6))\
                          .then_inc(rows_in, 16)
                        sp.dma_start(rows[0:NT - 6 * P, 6, :], tab[6 * P:NT, :]).then_inc(rows_in, 16)
                    for k in range(4, len(fills)):
                        sp.wait_ge(filled[k % 4], 16 * (k // 4))
                        sp.dma_start(*fills[k]).then_inc(filled[k % 4], 16)
                        if k == 7:
                            sp.wait_ge(w2z, 1)
                            for a, b in loads:
                                sp.dma_start(a, b).then_inc(W_SEM, 16)
                            sp.wait_ge(dst16_set, 2)
                            sp.dma_start(dst16_tab[0:6 * P, :].rearrange("(g t) p -> t g p", g=6), dst16_r[:, 0:6, :])\
                              .then_inc(dst16_out, 16)
                            sp.dma_start(dst16_tab[6 * P:NT, :], dst16_r[0:NT - 6 * P, 6, :]).then_inc(dst16_out, 16)
                            sp.dma_start(q0_tab[N:N + 1, :], zrow[0:1, 0, :]).then_inc(tabs, 16)
                            sp.dma_start(q1_tab[N:N + 1, :], zrow[0:1, 0:2, :].rearrange("p a d -> p (a d)"))\
                              .then_inc(tabs, 16)
                        if k == FILL_BEFORE:
                            sp.wait_ge(proj_out, len(pj_groups))
                            sp.dma_start(kv0_tab.rearrange("(p j) d -> p j d", j=NJ), kvq[:, :, 0:2 * D])\
                              .then_inc(tabs, 16)
                            sp.dma_start(q0_tab[0:N, :].rearrange("(p j) d -> p j d", j=NJ),
                                         kvq[:, :, 2 * D:3 * D]).then_inc(tabs, 16)
                    sp.wait_ge(tabs, 64)
                    sp.wait_ge(first_got, 16 * 7)
                    sp.wait_ge(q_scat, 16 * NJ)
                    rows_of = q0_edge.rearrange("(t p) d -> t p d", p=P)
                    for g in range(7):
                        n = P if g < 6 else NTR - 6 * P
                        sp.dma_start(rows_of[g * P:g * P + n, 0, :], qfirst[0:n, g, :]).then_inc(first_put, 16)
                    sp.wait_ge(first_put, 16 * 7)
                    sp.wait_ge(dst16_out, 32)

                @block.scalar
                def _(act):
                    for n in range(2):
                        for half in range(2):
                            act.wait_ge(tpose, 2 * n + half + 1)
                            w = 512 if half == 0 else NT - 512
                            dest = (dst_e, src_i)[n]
                            nc.scalar.activation(dest[:, 512 * half:512 * half + w],
                                                 bank[2 * n + half][:, 0:w], ACT.Copy).then_inc(tpose_out, 1)
                    for half in range(2):
                        act.wait_ge(last_mm, half + 1)
                        w = 512 if half == 0 else NT - 512
                        nc.scalar.activation(lastrow[:, 512 * half:512 * half + w], bank[half][:, 0:w],
                                             ACT.Copy).then_inc(tpose_out, 1)
                    roots(act, st, var1, std1, 1)
                    for g, (a, b) in enumerate(hT_groups):
                        act.wait_ge(hT_mm, g + 1)
                        nc.scalar.activation(hT[0:D, a * NP:b * NP], bank[4 + g % 2][0:D, 0:(b - a) * NP],
                                             ACT.Copy).then_inc(hT_out, 1)
                    for g, (a, b) in enumerate(pj_groups):
                        act.wait_ge(proj_mm, g + 1)
                        nc.scalar.activation(kvq[:, a:b, :].rearrange("p a d -> p (a d)"),
                                             bank[6 + g % 2][0:NP, 0:(b - a) * 3 * D], ACT.Copy).then_inc(proj_out, 1)
                    act.wait_ge(W_SEM, n_weights)

                @block.gpsimd
                def _(pool):
                    for g, (a, b) in enumerate(n_groups):
                        pool.wait_ge(tiles_ready, g + 1)
                        for j in range(a, b):
                            pool.indirect_dma_start(
                                tile_rows[:, j, :], None, dst_tab,
                                bass.IndirectOffsetOnAxis(ap=tiles_i[:, j:j + 1], axis=0)).then_inc(tiles_got, 16)
                    pool.wait_ge(tabs, 64)
                    pool.wait_ge(first_set, 2)
                    for g in range(7):
                        n = P if g < 6 else NTR - 6 * P
                        pool.indirect_dma_start(
                            qfirst[0:n, g, :], None, q0_tab,
                            bass.IndirectOffsetOnAxis(ap=first_i[0:n, g:g + 1], axis=0)).then_inc(first_got, 16)
                    pool.wait_ge(start_ready, 2)
                    for k in range(4):
                        pool.wait_ge(filled[k], 16 * (len(fills) // 4))
                    for j in range(NJ):
                        pool.indirect_dma_start(
                            q0_edge, bass.IndirectOffsetOnAxis(ap=start_i[:, j:j + 1], axis=0), qn[:, j, :], None,
                            bounds_check=NTR * P - 1, oob_is_err=False).then_inc(q_scat, 16)

                @block.vector
                def _(dve):
                    step = Chain(dve, dstep)
                    dve.wait_ge(rows_in, 64)
                    for n, rows in enumerate((dst_r, src_r)):
                        dve.tensor_copy(rows_f[:, n, 0:6 * P], rows[:, 0:6, :].rearrange("t g p -> t (g p)"))\
                           .then_inc(rows_cast, 1)
                        dve.tensor_copy(rows_f[0:NT - 6 * P, n, 6 * P:7 * P], rows[0:NT - 6 * P, 6, :])\
                           .then_inc(rows_cast, 1)
                    dve.tensor_copy(dst16_r[:, 0:6, :], dst_r[:, 0:6, :]).then_inc(dst16_set, 1)
                    dve.tensor_copy(dst16_r[0:NT - 6 * P, 6, :], dst_r[0:NT - 6 * P, 6, :]).then_inc(dst16_set, 1)
                    dve.tensor_copy(first_i[:, 0:6], dst_r[:, 0:6, 0]).then_inc(first_set, 1)
                    dve.tensor_copy(first_i[0:NT - 6 * P, 6:7], dst_r[0:NT - 6 * P, 6, 0:1]).then_inc(first_set, 1)
                    dve.wait_ge(x_in, 16)
                    layer_norm(dve, step, xs[:, :, :], cen[:, :, :], sq[:, :, :], st, var1, std1, 1)
                    dve.tensor_scalar(cen[:, :, :], cen[:, :, :], 0.0, None, ALU.max).then_inc(h_ready, 1)
                    dve.wait_ge(tpose_out, 6)
                    dve.wait_ge(consts, 4)
                    for a, b in n_groups:
                        for j in range(a, b):
                            step(dve.tensor_scalar(junk[0:NP, :], lastrow[0:NP, :], node_n[:, j:j + 1], 0.0, ALU.is_le,
                                                   ALU.add, accum_out=tiles_n[:, j:j + 1]))
                        dve.tensor_copy(tiles_i[:, a:b], tiles_n[:, a:b]).then_inc(tiles_ready, 1)
                    dve.tensor_copy(dst_i[:, :], dst_e[:, :]).then_inc(ranges_ready, 1)
                    step(dve.tensor_scalar(cont[:, 0:1], dst_e[:, 0:1], 0.0, None, ALU.mult))
                    step(dve.tensor_tensor(cont[:, 1:], lastrow[:, 1:NTR], lastrow[:, 0:NTR - 1], ALU.is_equal))
                    dve.wait_ge(tiles_got, 16 * (NJ + 1))
                    for j in range(NJ + 1):
                        step(dve.tensor_scalar(junk[0:NP, 0:P], tile_rows[:, j, :], node_n[:, j:j + 1], 0.0, ALU.is_le,
                                               ALU.add, accum_out=inner_n[:, j:j + 1]))
                    step(dve.scalar_tensor_tensor(upto[:, :], tiles_n[:, :], float(P), inner_n[:, :], ALU.mult,
                                                  ALU.add))
                    lo, hi = upto[:, 0:NJ], upto[:, 1:NJ + 1]
                    step(dve.tensor_tensor(has[:, :], hi, lo, ALU.is_gt))
                    step(dve.tensor_scalar(tf[:, 0, :], has[:, :], -4.0 * E, 4.0 * E, ALU.mult, ALU.add))
                    step(dve.tensor_tensor(start_n[:, :], lo, tf[:, 0, :], ALU.add))
                    dve.tensor_copy(start_i[:, :], start_n[:, :]).then_inc(start_ready, 1)
                    dve.wait_ge(proj_out, len(pj_groups))
                    dve.tensor_copy(qn[:, :, :], kvq[:, :, 2 * D:3 * D]).then_inc(start_ready, 1)
                    step(dve.tensor_scalar(tf[:, 1, :], hi, -1.0, 0.0, ALU.add, ALU.max))
                    step(dve.tensor_copy(last_i[:, :], tf[:, 1, :]))
                    step(dve.tensor_scalar(tf[:, 2, :], inner_n[:, 1:NJ + 1], 0.0, None, ALU.is_equal))
                    step(dve.tensor_tensor(tf[:, 2, :], tiles_n[:, 1:NJ + 1], tf[:, 2, :], ALU.subtract))
                    step(dve.tensor_scalar(tf[:, 2, :], tf[:, 2, :], 0.0, None, ALU.max))
                    step(dve.tensor_copy(tile_i[:, :], tf[:, 2, :]))
                    step(dve.scalar_tensor_tensor(tf[:, 0, :], tf[:, 2, :], float(P), lo, ALU.mult, ALU.is_gt))
                    step(dve.tensor_tensor(over[:, :], tf[:, 0, :], has[:, :], ALU.mult))
                    dve.wait_ge(W_SEM, n_weights)
                    parts = [(C[:, 0:4, :], C_hi[:, 0:4, :], C_lo[:, 0:4, :]),
                             (C[0:D, 4, :], C_hi[0:D, 4, :], C_lo[0:D, 4, :]),
                             (W1[D:2 * D, :], W1_hi[D:2 * D, :], W1_lo[D:2 * D, :]),
                             (W2[:, :], W2_hi[:, :], W2_lo[:, :])]
                    for whole, hi, lo in parts:
                        step(dve.tensor_copy(hi, whole))
                        step(dve.tensor_tensor(lo, whole, hi.bitcast(F32), ALU.subtract))
                    step(dve.tensor_copy(C_hi[D:2 * D, 4, :], C_hi[0:D, 4, :].bitcast(F32)))
                    step(dve.tensor_copy(W1_hi[0:D, :], W1_hi[D:2 * D, :].bitcast(F32)))

                @block.tensor
                def _(pe):
                    pe.wait_ge(consts, 4)
                    for n in range(2):
                        pe.wait_ge(rows_cast, 2 * n + 2)
                        for g in range(7):
                            rows = P if g < 6 else NT - 6 * P
                            b = bank[2 * n + g // 4]
                            ins = nc.tensor.transpose(b[:, (g % 4) * P:(g % 4) * P + rows],
                                                      rows_f[0:rows, n, g * P:(g + 1) * P], ident[0:rows, 0:rows])
                            if g in (3, 6):
                                ins.then_inc(tpose, 1)
                    for half in range(2):
                        pe.wait_ge(tpose_out, half + 1)
                        w = 512 if half == 0 else NT - 512
                        nc.tensor.matmul(bank[half][:, 0:w], row_l[:, :], dst_e[:, 512 * half:512 * half + w],
                                         start=True, stop=True).then_inc(last_mm, 1)
                    pe.wait_ge(h_ready, 1)
                    for g, (a, b) in enumerate(hT_groups):
                        need(pe, hT_out, g - 1)
                        for j in range(a, b):
                            ins = nc.tensor.transpose(bank[4 + g % 2][0:D, (j - a) * NP:(j - a + 1) * NP],
                                                      cen[:, j, :], ident[0:NP, 0:NP])
                        ins.then_inc(hT_mm, 1)
                    pe.wait_ge(hT_out, len(hT_groups))
                    pe.wait_ge(w0_in, 16 * len(loads0))
                    for g, (a, b) in enumerate(pj_groups):
                        need(pe, proj_out, g - 1)
                        for j in range(a, b):
                            ins = nc.tensor.matmul(bank[6 + g % 2][0:NP, (j - a) * 3 * D:(j - a + 1) * 3 * D],
                                                   hT[:, j * NP:(j + 1) * NP], W0[:, :], start=True, stop=True)
                        ins.then_inc(proj_mm, 1)

        def dst_rows(i):
            return dst16_tab[bass.ds(i * Q, Q), :].rearrange("q p -> (q p)").unsqueeze(0).broadcast_to([P, ST])

        ph = ExitStack()
        with ph:
            kv = [sb(f"kv{b}", [P, Q, 2 * D], F32, ph) for b in range(2)]
            idx = [sb(f"idx{b}", [P, Q], I32, ph) for b in range(2)]
            qs = [sb(f"qs{b}", [P, Q, D], F32, ph) for b in range(2)]
            drow = [sb(f"drow{b}", [P, ST], I16, ph) for b in range(2)]
            prod = sb("prod", [P, Q * D], F32, ph)
            sc = sb("sc", [P, Q, H0], F32, ph)
            feat = [sb(f"feat{b}", [P, Q, F0], F32, ph) for b in range(2)]
            same_q = [sb(f"same_q{b}", [P, Q, P], F32, ph) for b in range(2)]
            same = [sb(f"same{b}", [P, Q, P], F32, ph) for b in range(2)]
            rows = [sb(f"rows{b}", [P, Q, F0], F32, ph) for b in range(2)]
            edge_sems = []

            def edge_sem(name):
                edge_sems.append(nc.alloc_semaphore(name=name))
                return edge_sems[-1]

            idx_copied, idx_turn = edge_sem("idx_copied"), edge_sem("idx_turn")
            kv_got = [edge_sem(f"kv_got{b}") for b in range(2)]
            qs_in = [edge_sem(f"qs_in{b}") for b in range(2)]
            drow_in = [edge_sem(f"drow_in{b}") for b in range(2)]
            rows_out = [edge_sem(f"rows_out{b}") for b in range(2)]
            same_copied = edge_sem("same_copied")
            same_ready, qe_mm, prod_ready, red_ready, clip_ready = (
                edge_sem("same_ready"), edge_sem("qe_mm"), edge_sem("prod_ready"), edge_sem("red_ready"), edge_sem("clip_ready"))
            score_ready, exp_done, feat_ready = edge_sem("score_ready"), edge_sem("exp_done"), edge_sem("feat_ready")
            sum_mm, rows_cp = edge_sem("sum_mm"), edge_sem("rows_cp")

            with nc.Block() as block:
                @block.gpsimd
                def _(pool):
                    def gather(it, i, b):
                        need(pool, feat_ready, i - 1)
                        pool.tensor_copy(idx[b][:, :], src_i[:, bass.ds(i * Q, Q)]).then_inc(idx_copied, 1)
                        pool.wait_ge(idx_copied, i + 1)
                        pool.sem_inc(idx_turn, 1)
                        for q in range(Q):
                            pool.indirect_dma_start(
                                kv[b][:, q, :], None, kv0_tab,
                                bass.IndirectOffsetOnAxis(ap=idx[b][:, q:q + 1], axis=0)).then_inc(kv_got[b], 16)
                    pipelined(pool, [(gather, 0)])

                @block.sync
                def _(sp):
                    def load(it, i, b):
                        need(sp, same_ready, i - 1)
                        sp.dma_start(drow[b][:, :], dst_rows(i)).then_inc(drow_in[b], 16)
                        need(sp, qe_mm, i - 1)
                        sp.dma_start(qs[b][:, :, :], q0_edge[bass.ds(i * ST, ST), :].rearrange(
                            "(q p) d -> p q d", p=P)).then_inc(qs_in[b], 16)

                    pipelined(sp, [(load, 3)])

                @block.scalar
                def _(act):
                    def score(it, i, b):
                        act.wait_ge(score_ready, i + 1)
                        need(act, sum_mm, i - 1)
                        nc.scalar.activation(feat[b][:, :, D:F0], sc[:, :, :], ACT.Exp).then_inc(exp_done, 1)

                    def sums(it, i, b):
                        act.wait_ge(sum_mm, i + 1)
                        need(act, rows_out[b], it * 16)
                        nc.scalar.activation(rows[b][:, :, :].rearrange("p q f -> p (q f)"),
                                             bank[2 + b][:, 0:Q * F0], ACT.Copy).then_inc(rows_cp, 1)
                    def copy_same(it, i, b):
                        act.wait_ge(same_ready, i + 1)
                        need(act, sum_mm, i - 1)
                        nc.scalar.activation(same[b][:, :, :], same_q[b][:, :, :], ACT.Copy).then_inc(same_copied, 1)

                    def store(it, i, b):
                        act.wait_ge(rows_cp, i + 1)
                        act.dma_start(sum0_edge[bass.ds(i * ST, ST), :].rearrange("(q p) d -> p q d", p=P),
                                      rows[b][:, :, :]).then_inc(rows_out[b], 16)
                    pipelined(act, [(score, 0), (copy_same, 1), (sums, -1), (store, -1)])
                    for b in range(2):
                        act.wait_ge(rows_out[b], 16 * (NST // 2))

                @block.vector
                def _(dve):
                    def build(it, i, b):
                        dve.wait_ge(drow_in[b], 16 * (it + 1))
                        need(dve, qe_mm, i - 1)
                        need(dve, same_copied, i - 1)
                        dve.tensor_tensor(same_q[b][:, :, :], drow[b][:, :].rearrange("p (q e) -> p q e", q=Q),
                                          bcast(dst_e[:, bass.ds(i * Q, Q)], 2, P), ALU.is_equal)\
                           .then_inc(same_ready, 1)

                    def body(it, i, b):
                        dve.wait_ge(kv_got[b], 16 * Q * (it + 1))
                        dve.wait_ge(qe_mm, i + 1)
                        need(dve, red_ready, i)
                        dve.tensor_tensor(prod[:, :].rearrange("p (q d) -> p q d", q=Q), kv[b][:, :, 0:D],
                                          bank[b][:, 0:Q * D].rearrange("p (q d) -> p q d", q=Q), ALU.mult)\
                           .then_inc(prod_ready, 1)
                        dve.wait_ge(prod_ready, i + 1)
                        need(dve, exp_done, i)
                        dve.tensor_reduce(sc[:, :, :].rearrange("p q h -> p (q h)"),
                                          prod[:, :].rearrange("p (g d) -> p g d", d=DH), AX.X, ALU.add)\
                           .then_inc(red_ready, 1)
                        dve.wait_ge(red_ready, i + 1)
                        dve.tensor_scalar(sc[:, :, :], sc[:, :, :], SCALE0, -CLIP, ALU.mult, ALU.max)\
                           .then_inc(clip_ready, 1)
                        dve.wait_ge(clip_ready, i + 1)
                        dve.tensor_scalar(sc[:, :, :], sc[:, :, :], CLIP, None, ALU.min).then_inc(score_ready, 1)

                    def weigh(it, i, b):
                        dve.wait_ge(exp_done, i + 1)
                        dve.tensor_tensor(
                            feat[b][:, :, 0:D].rearrange("p q (h d) -> p q h d", d=DH),
                            kv[b][:, :, D:2 * D].rearrange("p q (h d) -> p q h d", d=DH),
                            bcast(feat[b][:, :, D:F0], 3, DH), ALU.mult).then_inc(feat_ready, 1)
                    pipelined(dve, [(body, 0), (build, 2), (weigh, 0)])

                @block.tensor
                def _(pe):
                    def spread_q(it, i, b):
                        pe.wait_ge(same_ready, i + 1)
                        pe.wait_ge(qs_in[b], 16 * (it + 1))
                        need(pe, prod_ready, i - 1)
                        for q in range(Q):
                            ins = nc.tensor.matmul(bank[b][:, q * D:(q + 1) * D], same_q[b][:, q, :], qs[b][:, q, :],
                                                   start=True, stop=True)
                        ins.then_inc(qe_mm, 1)

                    def sums(it, i, b):
                        pe.wait_ge(feat_ready, i + 1)
                        pe.wait_ge(same_copied, i + 1)
                        need(pe, rows_cp, i - 1)
                        for q in range(Q):
                            ins = nc.tensor.matmul(bank[2 + b][:, q * F0:(q + 1) * F0], same[b][:, q, :],
                                                   feat[b][:, q, :], start=True, stop=True)
                        ins.then_inc(sum_mm, 1)
                    pipelined(pe, [(spread_q, 2), (sums, 0)])
        nc.clear_and_free_semaphores(edge_sems)
        nc.all_engine_barrier()

        c_groups = [(g * P, min((g + 1) * P, NTR)) for g in range(7)]

        def load_last_rows(sp, lrows, sum_edge, got):
            of_tile = sum_edge.rearrange("(t p) f -> t p f", p=P)
            for g, (a, b) in enumerate(c_groups):
                sp.dma_start(lrows[0:b - a, g, :], of_tile[a:b, P - 1, :]).then_inc(got, 16)

        def feature_parts(F):
            return [(a, min(a + P, F)) for a in range(0, F, P)]

        def transpose_last_rows(pe, lrows, F, got, done):
            pe.wait_ge(got, 16 * len(c_groups))
            for k, (f0, f1) in enumerate(feature_parts(F)):
                for g, (a, b) in enumerate(c_groups):
                    ins = nc.tensor.transpose(bank[6 - 2 * k + g // 4][0:f1 - f0, (g % 4) * P:(g % 4) * P + b - a],
                                              lrows[0:b - a, g, f0:f1], ident[0:b - a, 0:b - a])
                    if g in (3, 6):
                        ins.then_inc(done, 1)

        def copy_last(act, last, F, mm, done):
            for k, (f0, f1) in enumerate(feature_parts(F)):
                for half in range(2):
                    act.wait_ge(mm, 2 * k + half + 1)
                    w = 512 if half == 0 else NTR - 512
                    nc.scalar.activation(last[0:f1 - f0, k, 512 * half:512 * half + w],
                                         bank[6 - 2 * k + half][0:f1 - f0, 0:w], ACT.Copy).then_inc(done, 1)

        def carry_over(dve, step, last, full, cshift, F, last_out):
            for k, (f0, f1) in enumerate(feature_parts(F)):
                dve.wait_ge(last_out, 2 * k + 2)
                f = slice(0, f1 - f0)
                step(dve.tensor_tensor_scan(full[f, k, :], cont[f, :], last[f, k, :], 0.0, ALU.mult, ALU.add))
                step(dve.memset(cshift[f, k, 0:1], 0.0))
                step(dve.tensor_copy(cshift[f, k, 1:], full[f, k, 0:NTR - 1]))

        ph = ExitStack()
        with ph:
            lrows = sb("lrows", [P, 7, F0], F32, ph)
            last = sb("last", [F0, 1, NTR], F32, ph)
            full = sb("full", [F0, 1, NTR], F32, ph)
            cshift = sb("cshift", [F0, 1, NTR], F32, ph)
            crows = sb("crows", [P, 7, F0], F32, ph)
            own = sb("own", [NP, NJ, F0], F32, ph)
            car = sb("car", [NP, NJ, F0], F32, ph)
            zr = sb("zr", [NP, NJ, H0], F32, ph)
            wv = sb("wv", [NP, NJ, D], F32, ph)
            wvT = sb("wvT", [D + 1, NJ * NP], F32, ph)
            hp = sb("hp", [NP, NJ, D], F32, ph)
            cen = sb("cen3", [NP, NJ, D], F32, ph)
            sq = sb("sq3", [NP, NJ, D], F32, ph)
            st = sb("st3", [NP, 4, NJ], F32, ph)
            q1n = sb("q1n", [NP, NJ, O1], F32, ph)
            last_got, last_mm, last_out = sem("last3_got"), sem("last3_mm"), sem("last3_out")
            d3, c_mm, c_out, c_put = sem("dstep3"), sem("c_mm"), sem("c_out"), sem("c_put")
            shift_ready, own_got, car_got, wv_ready = sem("shift_ready"), sem("own_got"), sem("car_got"), sem("wv_ready")
            t_mm, t_out, o_mm, o_out = sem("t3_mm"), sem("t3_out"), sem("o_mm"), sem("o_out")
            var3, std3, h1_ready, u_mm, u_out = sem("var3"), sem("std3"), sem("h1_ready"), sem("u_mm"), sem("u_out")
            q_mm, q_out, tab3, onesw = sem("q_mm"), sem("q_out"), sem("tab3"), sem("onesw")
            groups4 = [(a, min(a + 4, NJ)) for a in range(0, NJ, 4)]

            with nc.Block() as block:
                @block.gpsimd
                def _(pool):
                    pool.memset(wvT[D:D + 1, :], 1.0).then_inc(onesw, 1)
                    for j in range(NJ):
                        pool.indirect_dma_start(
                            own[:, j, :], None, sum0_edge,
                            bass.IndirectOffsetOnAxis(ap=last_i[:, j:j + 1], axis=0)).then_inc(own_got, 16)
                    pool.wait_ge(c_put, 16 * 7)
                    for j in range(NJ):
                        pool.indirect_dma_start(
                            car[:, j, :], None, carry0_tab,
                            bass.IndirectOffsetOnAxis(ap=tile_i[:, j:j + 1], axis=0)).then_inc(car_got, 16)

                @block.sync
                def _(sp):
                    load_last_rows(sp, lrows, sum0_edge, last_got)
                    for g, (a, b) in enumerate(c_groups):
                        sp.wait_ge(c_out, g + 1)
                        sp.dma_start(carry0_tab[a:b, :], crows[0:b - a, g, :]).then_inc(c_put, 16)
                    sp.wait_ge(h1_ready, 1)
                    sp.dma_start(h1_tab.rearrange("(p j) d -> p j d", j=NJ), cen[:, :, :]).then_inc(tab3, 16)
                    sp.wait_ge(q_out, len(groups4))
                    sp.dma_start(q1_tab[0:N, :].rearrange("(p j) d -> p j d", j=NJ), q1n[:, :, :]).then_inc(tab3, 16)
                    sp.wait_ge(tab3, 32)
                    sp.wait_ge(c_put, 16 * 7)

                @block.tensor
                def _(pe):
                    transpose_last_rows(pe, lrows, F0, last_got, last_mm)
                    pe.wait_ge(shift_ready, 1)
                    for g, (a, b) in enumerate(c_groups):
                        need(pe, c_out, g - 1)
                        nc.tensor.transpose(bank[g % 2][0:b - a, 0:F0], cshift[:, 0, a:b], ident[0:F0, 0:F0])\
                                 .then_inc(c_mm, 1)
                    pe.wait_ge(wv_ready, 1)
                    pe.wait_ge(onesw, 1)
                    for g, (a, b) in enumerate(groups4):
                        need(pe, t_out, g - 1)
                        for j in range(a, b):
                            ins = nc.tensor.transpose(bank[2 + g % 2][0:D, (j - a) * NP:(j - a + 1) * NP],
                                                      wv[:, j, :], ident[0:NP, 0:NP])
                        ins.then_inc(t_mm, 1)
                    pe.wait_ge(t_out, len(groups4))
                    for g, (a, b) in enumerate(groups4):
                        if g >= 2:
                            pe.wait_ge(o_out, g - 1)
                        for j in range(a, b):
                            o = bank[4 + g % 2][0:NP, (j - a) * D:(j - a + 1) * D]
                            nc.tensor.matmul(o, hT[:, j * NP:(j + 1) * NP], WfA[:, :], start=True, stop=False)
                            ins = nc.tensor.matmul(o, wvT[:, j * NP:(j + 1) * NP], WoA[:, :], start=False, stop=True)
                        ins.then_inc(o_mm, 1)
                    pe.wait_ge(h1_ready, 1)
                    for g, (a, b) in enumerate(groups4):
                        if g >= 2:
                            pe.wait_ge(u_out, g - 1)
                        for j in range(a, b):
                            ins = nc.tensor.transpose(bank[6 + g % 2][0:D, (j - a) * NP:(j - a + 1) * NP],
                                                      cen[:, j, :], ident[0:NP, 0:NP])
                        ins.then_inc(u_mm, 1)
                    pe.wait_ge(u_out, len(groups4))
                    for g, (a, b) in enumerate(groups4):
                        if g >= 2:
                            pe.wait_ge(q_out, g - 1)
                        for j in range(a, b):
                            ins = nc.tensor.matmul(bank[g % 2][0:NP, (j - a) * O1:(j - a + 1) * O1],
                                                   hT[0:D, j * NP:(j + 1) * NP], Wq1s[:, :], start=True, stop=True)
                        ins.then_inc(q_mm, 1)

                @block.scalar
                def _(act):
                    copy_last(act, last, F0, last_mm, last_out)
                    for g, (a, b) in enumerate(c_groups):
                        act.wait_ge(c_mm, g + 1)
                        nc.scalar.activation(crows[0:b - a, g, :], bank[g % 2][0:b - a, 0:F0], ACT.Copy)\
                                 .then_inc(c_out, 1)
                    for g, (a, b) in enumerate(groups4):
                        act.wait_ge(t_mm, g + 1)
                        nc.scalar.activation(wvT[0:D, a * NP:b * NP], bank[2 + g % 2][0:D, 0:(b - a) * NP],
                                             ACT.Copy).then_inc(t_out, 1)
                    for g, (a, b) in enumerate(groups4):
                        act.wait_ge(o_mm, g + 1)
                        nc.scalar.activation(hp[:, a:b, :].rearrange("p a d -> p (a d)"),
                                             bank[4 + g % 2][0:NP, 0:(b - a) * D], ACT.Copy).then_inc(o_out, 1)
                    roots(act, st, var3, std3, 1)
                    roots(act, st, var3, std3, 2)
                    for g, (a, b) in enumerate(groups4):
                        act.wait_ge(u_mm, g + 1)
                        nc.scalar.activation(hT[0:D, a * NP:b * NP], bank[6 + g % 2][0:D, 0:(b - a) * NP],
                                             ACT.Copy).then_inc(u_out, 1)
                    for g, (a, b) in enumerate(groups4):
                        act.wait_ge(q_mm, g + 1)
                        nc.scalar.activation(q1n[:, a:b, :].rearrange("p a d -> p (a d)"),
                                             bank[g % 2][0:NP, 0:(b - a) * O1], ACT.Copy).then_inc(q_out, 1)

                @block.vector
                def _(dve):
                    step = Chain(dve, d3)
                    carry_over(dve, step, last, full, cshift, F0, last_out)
                    dve.sem_inc(shift_ready, 1)
                    dve.wait_ge(own_got, 16 * NJ)
                    dve.wait_ge(car_got, 16 * NJ)
                    step(dve.tensor_tensor(own[:, :, :], own[:, :, :], bcast(has[:, :], 2, F0), ALU.mult))
                    step(dve.tensor_tensor(car[:, :, :], car[:, :, :], bcast(over[:, :], 2, F0), ALU.mult))
                    step(dve.tensor_tensor(own[:, :, :], own[:, :, :], car[:, :, :], ALU.add))
                    step(dve.tensor_scalar(zr[:, :, :], own[:, :, D:F0], 1.0, None, ALU.add))
                    step(dve.reciprocal(zr[:, :, :], zr[:, :, :]))
                    for h in range(H0):
                        step(dve.tensor_tensor(wv[:, :, h * DH:(h + 1) * DH], own[:, :, h * DH:(h + 1) * DH],
                                               zr[:, :, h:h + 1].broadcast_to([NP, NJ, DH]), ALU.mult))
                    dve.sem_inc(wv_ready, 1)
                    dve.wait_ge(o_out, len(groups4))
                    layer_norm(dve, step, hp[:, :, :], cen[:, :, :], sq[:, :, :], st, var3, std3, 1)
                    step(dve.tensor_tensor(cen[:, :, :], cen[:, :, :], bcast(g0b[:, :], 1, NJ), ALU.mult))
                    step(dve.tensor_tensor(cen[:, :, :], cen[:, :, :], bcast(be0b[:, :], 1, NJ), ALU.add))
                    step(dve.tensor_tensor(hp[:, :, :], hp[:, :, :], cen[:, :, :], ALU.add))
                    step(dve.tensor_tensor(xs[:, :, :], xs[:, :, :], hp[:, :, :], ALU.add))
                    layer_norm(dve, step, xs[:, :, :], cen[:, :, :], sq[:, :, :], st, var3, std3, 2)
                    dve.tensor_scalar(cen[:, :, :], cen[:, :, :], 0.0, None, ALU.max).then_inc(h1_ready, 1)

        attn = sb("attn", [P, NT * H1])
        ph = ExitStack()
        with ph:
            sh = [sb(f"sh{b}", [P, Q, S], F32, ph) for b in range(2)]
            xg = [sb(f"xg{b}", [P, Q, D], F32, ph) for b in range(2)]
            qg = [sb(f"qg{b}", [P, Q, O1], F32, ph) for b in range(2)]
            idx_x = [sb(f"idx_x{b}", [P, Q], I32, ph) for b in range(2)]
            idx_q = [sb(f"idx_q{b}", [P, Q], I32, ph) for b in range(2)]
            z = [sb(f"z{b}", [P, Q, (S + 1) * D], F32, ph) for b in range(2)]
            z_hi = [sb(f"z_hi{b}", [P, 5, Q * P], F32R, ph) for b in range(2)]
            z_lo = [sb(f"z_lo{b}", [P, 5, Q * P], F32R, ph) for b in range(2)]
            hid = sb("hid", [O1, Q * P], F32, ph)
            hid_hi = sb("hid_hi", [O1, Q * P], F32R, ph)
            hid_lo = sb("hid_lo", [O1, Q * P], F32R, ph)
            wsb = sb("wsb", [P, Q, 2 * O1], F32, ph)
            kvs = [sb(f"kvs{b}", [P, Q, 2 * O1], F32, ph) for b in range(2)]
            kq = sb("kq", [P, Q * O1], F32, ph)
            ef_in = [sem(f"ef_in{b}") for b in range(2)]
            sh_in = [sem(f"sh_in{b}") for b in range(2)]
            ef_tail, sh_tail = sem("ef_tail"), sem("sh_tail")
            x_got = [sem(f"x_got{b}") for b in range(2)]
            q_got = [sem(f"q_got{b}") for b in range(2)]
            v_out = [sem(f"v_out{b}") for b in range(2)]
            idx_x_set, idx_q_set, idy_turn = sem("idx_x_set"), sem("idx_q_set"), sem("idy_turn")
            z_ready, hid_mm, hid_out, hid_split = sem("z_ready"), sem("hid_mm"), sem("hid_out"), sem("hid_split")
            zT_mm, hi_out, lo_out, w_mm, w_out = sem("zT_mm"), sem("hi_out"), sem("lo_out"), sem("w_mm"), sem("w_out")
            a_mm, kv_ready, kq_ready, attn_ready = sem("a_mm"), sem("kv_ready"), sem("kq_ready"), sem("attn_ready")
            sp_turn = sem("sp_turn")
            CHUNK = [4, 0, 1, 2, 3]
            ZB = [0, 1, 2, 0, 1]
            ZB_FREE = [-1, 0, -2, 2, 3]
            TAIL = E - (NST - 1) * ST

            def load_rows(sp, i, t, a, got, got_tail):
                if not isinstance(i, int) or i < NST - 1:
                    sp.dma_start(t, a[bass.ds(i * ST, ST), :].rearrange("(q p) d -> p q d", p=P)).then_inc(got, 16)
                    return
                lo, q, n = i * ST, TAIL // P, TAIL % P
                sp.dma_start(t[:, 0:q, :], a[lo:lo + q * P, :].rearrange("(q p) d -> p q d", p=P)).then_inc(got, 16)
                sp.dma_start(t[0:n, q, :], a[lo + q * P:E, :]).then_inc(got_tail, 16)

            def load_either(sp, flag, i, t, given, ordered, got, got_tail):
                sp.sem_inc(sp_turn, 1)
                with sp.If(flag > 0):
                    load_rows(sp, i, t, ordered, got, got_tail)
                with sp.Else():
                    load_rows(sp, i, t, given, got, got_tail)

            with nc.Block() as block:
                @block.sync
                def _(sp):
                    flag = sp.value_load(unsorted[0:1, 0:1])

                    def load_sh(it, i, b):
                        need(sp, z_ready, i * 2 - 2)
                        load_either(sp, flag, i, sh[b][:, :, :], ea9, ea9_s, sh_in[b], sh_tail)

                    def load_ef(it, i, b):
                        need(sp, zT_mm, i * 5 - 9)
                        load_either(sp, flag, i, z[b][:, :, S * D:], ea64, ea64_s, ef_in[b], ef_tail)

                    def store(it, i, b):
                        sp.wait_ge(kv_ready, i * 2 + 2)
                        sp.dma_start(v1_edge[bass.ds(i, 1)].rearrange("a p (q o) -> p (a q) o", q=Q),
                                     kvs[b][:, :, O1:2 * O1]).then_inc(v_out[b], 16)

                    pipelined(sp, [(load_sh, 3), (load_ef, 2), (store, -1)])
                    for b in range(2):
                        sp.wait_ge(v_out[b], 16 * (NST // 2))

                @block.gpsimd
                def _(pool):
                    def gather_x(it, i, b):
                        need(pool, z_ready, i * 2 - 2)
                        pool.tensor_copy(idx_x[b][:, :], src_i[:, bass.ds(i * Q, Q)]).then_inc(idx_x_set, 1)
                        pool.wait_ge(idx_x_set, i + 1)
                        pool.sem_inc(idy_turn, 1)
                        for q in range(Q):
                            pool.indirect_dma_start(
                                xg[b][:, q, :], None, h1_tab,
                                bass.IndirectOffsetOnAxis(ap=idx_x[b][:, q:q + 1], axis=0)).then_inc(x_got[b], 16)

                    def gather_q(it, i, b):
                        need(pool, kq_ready, i - 1)
                        pool.tensor_copy(idx_q[b][:, :], dst_i[:, bass.ds(i * Q, Q)]).then_inc(idx_q_set, 1)
                        pool.wait_ge(idx_q_set, i + 1)
                        pool.sem_inc(idy_turn, 1)
                        for q in range(Q):
                            pool.indirect_dma_start(
                                qg[b][:, q, :], None, q1_tab,
                                bass.IndirectOffsetOnAxis(ap=idx_q[b][:, q:q + 1], axis=0)).then_inc(q_got[b], 16)

                    def times_q(it, i, b):
                        pool.wait_ge(q_got[b], 16 * Q * (it + 1))
                        pool.wait_ge(kv_ready, i * 2 + 2)
                        pool.wait_ge(attn_ready, i + 1)
                        pool.sem_inc(idy_turn, 1)
                        pool.tensor_tensor(kq[:, :].rearrange("p (q o) -> p q o", q=Q), kvs[b][:, :, 0:O1],
                                           qg[b][:, :, :], ALU.mult).then_inc(kq_ready, 1)

                    pipelined(pool, [(times_q, -1), (gather_x, 3), (gather_q, 1)])

                @block.tensor
                def _(pe):
                    def t_z(k):
                        c = CHUNK[k]

                        def stage(it, i, b):
                            if k == 0:
                                pe.wait_ge(z_ready, i * 2 + 2)
                                pe.wait_ge(ef_in[b], 16 * (it + 1))
                                if isinstance(i, int) and i == NST - 1:
                                    pe.wait_ge(ef_tail, 16)
                            need(pe, lo_out, i * 6 + ZB_FREE[k])
                            for q in range(Q):
                                ins = nc.tensor.transpose(bank[ZB[k]][:, q * P:(q + 1) * P],
                                                          z[b][:, q, c * P:(c + 1) * P], ident[:, :])
                            ins.then_inc(zT_mm, 1)
                        return stage

                    def m_hid(it, i, b):
                        pe.wait_ge(lo_out, i * 6 + 2)
                        need(pe, hid_out, i * 2)
                        nc.tensor.matmul(bank[3][:, :], W1_hi[:, :], z_lo[b][:, 4, :], start=True, stop=False)
                        ins = nc.tensor.matmul(bank[3][:, :], W1_lo[D:2 * D, :], z_lo[b][D:2 * D, 4, :],
                                               start=False, stop=True)
                        ins.then_inc(hid_mm, 1)

                    def m_w(half):
                        def stage(it, i, b):
                            pe.wait_ge(hid_split, i + 1)
                            need(pe, w_out, i * 2 + half - 1)
                            parts = [(hid_hi, W2_hi), (hid_hi, W2_lo), (hid_lo, W2_hi)]
                            for r in range(2):
                                q = 2 * half + r
                                for n, (ht, wt) in enumerate(parts):
                                    ins = nc.tensor.matmul(bank[4 + half][:, r * 2 * O1:(r + 1) * 2 * O1],
                                                           ht[:, q * P:(q + 1) * P], wt[:, :],
                                                           start=(n == 0), stop=(n == 2))
                            ins.then_inc(w_mm, 1)
                        return stage

                    def m_acc(q):
                        def stage(it, i, b):
                            pe.wait_ge(lo_out, i * 6 + 6)
                            need(pe, kv_ready, i * 2 + q // 2 - 1)
                            e = slice(q * P, (q + 1) * P)
                            parts = [(z_hi, C_hi, c, P) for c in range(5)] + [(z_hi, C_lo, c, P) for c in range(4)]\
                                + [(z_hi, C_lo, 4, D)] + [(z_lo, C_hi, c, P) for c in range(4)]
                            for n, (zt, ct, c, rows) in enumerate(parts):
                                ins = nc.tensor.matmul(bank[6 + q // 2][:, (q % 2) * 2 * O1:(q % 2 + 1) * 2 * O1],
                                                       zt[b][0:rows, c, e], ct[0:rows, c, :],
                                                       start=(n == 0), stop=(n == len(parts) - 1))
                            if q % 2:
                                ins.then_inc(a_mm, 1)
                        return stage

                    pipelined(pe, [(t_z(0), 1), (m_acc(0), 0), (m_w(0), 0), (t_z(1), 1), (m_acc(1), 0),
                                   (m_w(1), 0), (t_z(2), 1), (m_acc(2), 0), (t_z(3), 1), (m_hid, 1), (t_z(4), 1),
                                   (m_acc(3), 0)])

                @block.scalar
                def _(act):
                    def hi(k):
                        def stage(it, i, b):
                            act.wait_ge(zT_mm, i * 5 + k + 1)
                            need(act, a_mm, i * 2 - 2)
                            if k == 0:
                                nc.scalar.activation(z_lo[b][D:2 * D, 4, :], bank[ZB[0]][D:2 * D, :], ACT.Copy)\
                                         .then_inc(hi_out, 1)
                                nc.scalar.activation(z_hi[b][0:D, 4, :], bank[ZB[0]][0:D, :], ACT.Copy)\
                                         .then_inc(hi_out, 1)
                                return
                            nc.scalar.activation(z_hi[b][:, CHUNK[k], :], bank[ZB[k]][:, :], ACT.Copy).then_inc(hi_out, 1)
                        return stage

                    def hidden(it, i, b):
                        act.wait_ge(hid_mm, i + 1)
                        need(act, hid_split, i)
                        nc.scalar.activation(hid[:, :], bank[3][:, :], ACT.Relu, bias=b1[:, 0:1]).then_inc(hid_out, 1)

                    def hidden_hi(it, i, b):
                        need(act, w_mm, i * 2)
                        nc.scalar.activation(hid_hi[:, :], bank[3][:, :], ACT.Relu, bias=b1[:, 0:1])\
                                 .then_inc(hid_out, 1)
                    pipelined(act, [(hi(0), 1), (hi(1), 1), (hi(2), 1), (hi(3), 1), (hidden, 1), (hi(4), 1),
                                    (hidden_hi, 1)])

                @block.vector
                def _(dve):
                    dve.memset(attn[:, NTR * H1:], 0.0).then_inc(attn_ready, 1)

                    def outer(half):
                        tiles = slice(half * Q // 2, (half + 1) * Q // 2)

                        def stage(it, i, b):
                            if half == 0:
                                dve.wait_ge(x_got[b], 16 * Q * (it + 1))
                                dve.wait_ge(sh_in[b], 16 * (it + 1))
                                if isinstance(i, int) and i == NST - 1:
                                    dve.wait_ge(sh_tail, 16)
                                need(dve, zT_mm, i * 5 - 5)
                            dve.tensor_tensor(z[b][:, tiles, 0:S * D].rearrange("p q (s d) -> p q s d", d=D),
                                              bcast(xg[b][:, tiles, :], 2, S), bcast(sh[b][:, tiles, :], 3, D),
                                              ALU.mult).then_inc(z_ready, 1)
                        return stage

                    def lo(k):
                        def stage(it, i, b):
                            dve.wait_ge(hi_out, i * 6 + (1 if k == 0 else k + 2))
                            need(dve, a_mm, i * 2 - 2)
                            if k == 0:
                                for rows, lo_rows, t in ((slice(D, 2 * D), slice(0, D), z_lo),
                                                         (slice(0, D), slice(D, 2 * D), z_hi)):
                                    if t is z_hi:
                                        dve.wait_ge(hi_out, i * 6 + 2)
                                    dve.tensor_tensor(t[b][lo_rows, 4, :], bank[ZB[0]][rows, :],
                                                      t[b][rows, 4, :].bitcast(F32), ALU.subtract).then_inc(lo_out, 1)
                                return
                            c = CHUNK[k]
                            dve.tensor_tensor(z_lo[b][:, c, :], bank[ZB[k]][:, :], z_hi[b][:, c, :].bitcast(F32),
                                              ALU.subtract).then_inc(lo_out, 1)
                        return stage

                    def hidden_lo(it, i, b):
                        dve.wait_ge(hid_out, i * 2 + 2)
                        need(dve, w_mm, i * 2)
                        dve.tensor_tensor(hid_lo[:, :], hid[:, :], hid_hi[:, :].bitcast(F32), ALU.subtract)\
                           .then_inc(hid_split, 1)

                    def bias(half):
                        def stage(it, i, b):
                            dve.wait_ge(w_mm, i * 2 + half + 1)
                            need(dve, kv_ready, i * 2 + half - 1)
                            dve.tensor_tensor(wsb[:, 2 * half:2 * half + 2, :],
                                              bank[4 + half][:, :].rearrange("p (q o) -> p q o", q=2),
                                              bcast(b2[:, :], 1, 2), ALU.add).then_inc(w_out, 1)
                        return stage

                    def product(half):
                        def stage(it, i, b):
                            need(dve, v_out[b], it * 16)
                            dve.wait_ge(a_mm, i * 2 + half + 1)
                            dve.wait_ge(w_out, i * 2 + half + 1)
                            dve.tensor_tensor(kvs[b][:, 2 * half:2 * half + 2, :], wsb[:, 2 * half:2 * half + 2, :],
                                              bank[6 + half][:, :].rearrange("p (q o) -> p q o", q=2), ALU.mult)\
                               .then_inc(kv_ready, 1)
                        return stage

                    def logits(it, i, b):
                        dve.wait_ge(kq_ready, i + 1)
                        dve.tensor_reduce(attn[:, bass.ds(i * (Q * H1), Q * H1)],
                                          kq[:, :].rearrange("p (g d) -> p g d", d=DH), AX.X, ALU.add)\
                           .then_inc(attn_ready, 1)

                    pipelined(dve, [(product(1), -1), (lo(0), 1), (outer(0), 2), (bias(0), 0), (lo(1), 1),
                                    (logits, -1), (product(0), 0), (bias(1), 0), (lo(2), 1), (outer(1), 2),
                                    (lo(3), 1), (lo(4), 1), (hidden_lo, 1)])

        ph = ExitStack()
        with ph:
            A = sb("A", [P, U], F32, ph)
            Fs = sb("Fs", [P, U], F32, ph)
            X = sb("X", [P, U + 2], F32, ph)
            NE = sb("NE", [P, U + 1], BF16, ph)
            CT = sb("CT", [P, U + 1], BF16, ph)
            sel8 = sb("sel8", [P, H1], F32, ph)
            selT = sb("selT", [H1, P], F32, ph)
            chm = sb("chm", [P, CH], F32, ph)
            sums = sb("sums", [P, 2], F32, ph)
            spread = sb("spread", [P, 2, CH], F32, ph)
            per_head = sb("per_head", [H1, 2, CH], F32, ph)
            run = sb("run", [H1, CH], F32, ph)
            carry = sb("carry", [H1, CH], F32, ph)
            back = sb("back", [P, CH], F32, ph)
            cin = sb("cin", [P, 1], F32, ph)
            starts = sb("starts", [P, 2], F32, ph)
            d5, dst_in, a_tr, a_cp = sem("dstep5"), sem("dst_in"), sem("a_tr"), sem("a_cp")
            sel_ready, selT_mm, spr_ready, head_mm, car_ready, back_mm = (
                sem("sel_ready"), sem("selT_mm"), sem("spr_ready"), sem("head_mm"), sem("car_ready"), sem("back_mm"))
            sub_ready, b_tr, b_cp = sem("sub_ready"), sem("b_tr"), sem("b_cp")
            perm_ready, x0_set = sem("perm_ready"), sem("x0_set")
            groups = [(a, min(a + 4, TC)) for a in range(0, TC, 4)]
            attn_v = attn[:, :].rearrange("p (j c h) -> p c j h", j=CH, h=H1)

            with nc.Block() as block:
                @block.sync
                def _(sp):
                    flat = dst_tab.rearrange("t p -> (t p)")
                    for j in range(CH):
                        lo = 1 if j == 0 else 0
                        sp.dma_start(X[j * H1:(j + 1) * H1, lo:].bitcast(I32),
                                     flat[j * U - 1 + lo:j * U + U + 1].unsqueeze(0).broadcast_to([H1, U + 2 - lo]))\
                          .then_inc(dst_in, 16)
                    sp.wait_ge(dst_in, 16 * CH)

                @block.gpsimd
                def _(pool):
                    pool.memset(X[0:H1, 0:1].bitcast(I32), -1).then_inc(x0_set, 1)

                @block.tensor
                def _(pe):
                    pe.wait_ge(perm_ready, 1)
                    for g, (a, b) in enumerate(groups):
                        need(pe, a_cp, g - 1)
                        for c in range(a, b):
                            ins = nc.tensor.transpose(bank[g % 2][:, (c - a) * P:(c - a + 1) * P],
                                                      Fs[:, c * P:(c + 1) * P], ident[:, :])
                        ins.then_inc(a_tr, 1)
                    pe.wait_ge(sel_ready, 1)
                    nc.tensor.transpose(bank[2][0:H1, 0:P], sel8[:, :], ident[:, :]).then_inc(selT_mm, 1)
                    for k in range(2):
                        pe.wait_ge(spr_ready, k + 1)
                        nc.tensor.matmul(bank[3][0:H1, 0:2 * CH], sel8[:, :],
                                         spread[:, :, :].rearrange("p a c -> p (a c)"), start=True, stop=True)\
                                 .then_inc(head_mm, 1)
                        pe.wait_ge(car_ready, k + 1)
                        nc.tensor.matmul(bank[4][:, 0:CH], selT[:, :], carry[:, :], start=True, stop=True)\
                                 .then_inc(back_mm, 1)
                    pe.wait_ge(sub_ready, 1)
                    for g, (a, b) in enumerate(groups):
                        need(pe, b_cp, g - 1)
                        for c in range(a, b):
                            ins = nc.tensor.transpose(bank[5 + g % 2][:, (c - a) * P:(c - a + 1) * P],
                                                      A[:, c * P:(c + 1) * P], ident[:, :])
                        ins.then_inc(b_tr, 1)

                @block.scalar
                def _(act):
                    nc.scalar.activation(Fs[:, :].rearrange("p (c j h) -> p c j h", c=TC, h=H1), attn_v[:, :],
                                         ACT.Copy).then_inc(perm_ready, 1)
                    for g, (a, b) in enumerate(groups):
                        act.wait_ge(a_tr, g + 1)
                        nc.scalar.activation(A[:, a * P:b * P], bank[g % 2][:, 0:(b - a) * P], ACT.Copy)\
                                 .then_inc(a_cp, 1)
                    for g, (a, b) in enumerate(groups):
                        act.wait_ge(b_tr, g + 1)
                        nc.scalar.activation(attn_v[:, a:b], bank[5 + g % 2][:, 0:(b - a) * P].rearrange(
                            "p (c j h) -> p c j h", c=b - a, h=H1), ACT.Exp).then_inc(b_cp, 1)

                @block.vector
                def _(dve):
                    step = Chain(dve, d5)
                    rev = slice(None, None, -1)
                    carries = [0]

                    def carry_in(last, flag, forward):
                        carries[0] += 1
                        step(dve.tensor_scalar(spread[:, 0, :], chm[:, :], last, None, ALU.mult))
                        step(dve.tensor_scalar(spread[:, 1, :], chm[:, :], flag, None, ALU.mult))
                        dve.sem_inc(spr_ready, 1)
                        dve.wait_ge(head_mm, carries[0])
                        step(dve.tensor_copy(per_head[:, :, :].rearrange("p a c -> p (a c)"),
                                             bank[3][0:H1, 0:2 * CH]))
                        if forward:
                            step(dve.tensor_scalar(per_head[:, 1, :], per_head[:, 1, :], -BIG, None, ALU.mult))
                            step(dve.tensor_tensor_scan(run[:, :], per_head[:, 1, :], per_head[:, 0, :], -BIG,
                                                        ALU.add, ALU.max))
                            step(dve.memset(carry[:, 0:1], -BIG))
                            step(dve.tensor_copy(carry[:, 1:], run[:, 0:CH - 1]))
                        else:
                            step(dve.tensor_scalar(per_head[:, 1, :], per_head[:, 1, :], -1.0, 1.0, ALU.mult, ALU.add))
                            step(dve.tensor_tensor_scan(run[:, rev], per_head[:, 1, rev], per_head[:, 0, rev], 0.0,
                                                        ALU.mult, ALU.add))
                            step(dve.memset(carry[:, CH - 1:], 0.0))
                            step(dve.tensor_copy(carry[:, 0:CH - 1], run[:, 1:]))
                        dve.sem_inc(car_ready, 1)
                        dve.wait_ge(back_mm, carries[0])
                        step(dve.tensor_tensor(back[:, :], bank[4][:, 0:CH], chm[:, :], ALU.mult))
                        step(dve.tensor_reduce(cin[:, :], back[:, :], AX.X, ALU.add))

                    step(dve.tensor_reduce(sel8[:, :], ident[:, :].rearrange("p (j h) -> p h j", h=H1), AX.X, ALU.add))
                    dve.sem_inc(sel_ready, 1)
                    step(dve.tensor_reduce(chm[:, :], ident[:, :].rearrange("p (j h) -> p j h", h=H1), AX.X, ALU.add))
                    dve.wait_ge(selT_mm, 1)
                    step(dve.tensor_copy(selT[:, :], bank[2][0:H1, 0:P]))
                    dve.wait_ge(dst_in, 16 * CH)
                    dve.wait_ge(x0_set, 1)
                    Xi = X[:, :].bitcast(I32)
                    step(dve.tensor_tensor(NE[:, :], Xi[:, 1:], Xi[:, 0:U + 1], ALU.not_equal))
                    step(dve.tensor_scalar(CT[:, :], NE[:, :], -1.0, 1.0, ALU.mult, ALU.add))
                    step(dve.tensor_reduce(starts[:, 0:1], NE[:, 0:U], AX.X, ALU.max))
                    step(dve.tensor_reduce(starts[:, 1:2], NE[:, 1:U + 1], AX.X, ALU.max))
                    step(dve.tensor_scalar(X[:, 0:U], NE[:, 0:U], -BIG, None, ALU.mult))
                    dve.wait_ge(a_cp, len(groups))

                    def scan_max(init):
                        step(dve.tensor_tensor_scan(Fs[:, :], X[:, 0:U], A[:, :], init, ALU.add, ALU.max))
                    scan_max(-BIG)
                    carry_in(Fs[:, U - 1:U], starts[:, 0:1], True)
                    scan_max(cin[:, 0:1])
                    step(dve.tensor_tensor(X[:, 0:U], Fs[:, :], NE[:, 1:U + 1], ALU.mult))

                    def scan_back(init):
                        step(dve.tensor_tensor_scan(Fs[:, rev], CT[:, 1:U + 1][:, rev], X[:, 0:U][:, rev], init,
                                                    ALU.mult, ALU.add))
                    scan_back(0.0)
                    carry_in(Fs[:, 0:1], starts[:, 1:2], False)
                    scan_back(cin[:, 0:1])
                    step(dve.tensor_tensor(A[:, :], A[:, :], Fs[:, :], ALU.subtract))
                    dve.sem_inc(sub_ready, 1)

        ph = ExitStack()
        with ph:
            vin = [sb(f"vin{b}", [P, Q * O1], F32, ph) for b in range(2)]
            va = [sb(f"va{b}", [P, Q, F1], F32, ph) for b in range(2)]
            drow = [sb(f"dsow{b}", [P, ST], I16, ph) for b in range(2)]
            same = [sb(f"samf{b}", [P, Q, P], F32, ph) for b in range(2)]
            rows = [sb(f"rowt{b}", [P, Q, F1], F32, ph) for b in range(2)]
            v_in = [sem(f"v_in{b}") for b in range(2)]
            drow_in = [sem(f"dsow_in{b}") for b in range(2)]
            rows_out = [sem(f"rowt_out{b}") for b in range(2)]
            ex_copied = sem("ex_copied")
            same_ready, va_ready, sum_mm, rows_cp = (sem("samf_ready"), sem("va_ready"), sem("sum1_mm"),
                                                     sem("rowt_cp"))

            with nc.Block() as block:
                @block.sync
                def _(sp):
                    def load(it, i, b):
                        need(sp, same_ready, i - 1)
                        sp.dma_start(drow[b][:, :], dst_rows(i)).then_inc(drow_in[b], 16)
                        need(sp, va_ready, i - 1)
                        sp.dma_start(vin[b][:, :], v1_edge[bass.ds(i, 1)].rearrange("a p o -> p (a o)"))\
                          .then_inc(v_in[b], 16)

                    pipelined(sp, [(load, 3)])

                @block.vector
                def _(dve):
                    def build(it, i, b):
                        dve.wait_ge(drow_in[b], 16 * (it + 1))
                        need(dve, sum_mm, i - 1)
                        dve.tensor_tensor(same[b][:, :, :], drow[b][:, :].rearrange("p (q e) -> p q e", q=Q),
                                          bcast(dst_e[:, bass.ds(i * Q, Q)], 2, P), ALU.is_equal)\
                           .then_inc(same_ready, 1)

                    def weigh(it, i, b):
                        dve.wait_ge(v_in[b], 16 * (it + 1))
                        need(dve, sum_mm, i - 1)
                        dve.wait_ge(ex_copied, i + 1)
                        dve.tensor_tensor(va[b][:, :, 0:O1].rearrange("p q (h d) -> p q h d", d=DH),
                                          vin[b][:, :].rearrange("p (q h d) -> p q h d", q=Q, d=DH),
                                          bcast(va[b][:, :, O1:F1], 3, DH), ALU.mult)\
                           .then_inc(va_ready, 1)
                    pipelined(dve, [(build, 0), (weigh, 0)])

                @block.tensor
                def _(pe):
                    def sums(it, i, b):
                        pe.wait_ge(va_ready, i + 1)
                        pe.wait_ge(same_ready, i + 1)
                        need(pe, rows_cp, i * 2 - 2)
                        for q in range(Q):
                            ins = nc.tensor.matmul(bank[2 * b + q // 2][:, (q % 2) * F1:(q % 2 + 1) * F1],
                                                   same[b][:, q, :], va[b][:, q, :], start=True, stop=True)
                        ins.then_inc(sum_mm, 1)
                    pipelined(pe, [(sums, 0)])

                @block.scalar
                def _(act):
                    def sums(it, i, b):
                        act.wait_ge(sum_mm, i + 1)
                        need(act, rows_out[b], it * 16)
                        for half in range(2):
                            nc.scalar.activation(rows[b][:, 2 * half:2 * half + 2, :].rearrange("p q f -> p (q f)"),
                                                 bank[2 * b + half][:, 0:2 * F1], ACT.Copy).then_inc(rows_cp, 1)

                    def store(it, i, b):
                        act.wait_ge(rows_cp, i * 2 + 2)
                        act.dma_start(sum1_edge[bass.ds(i * ST, ST), :].rearrange("(q p) d -> p q d", p=P),
                                      rows[b][:, :, :]).then_inc(rows_out[b], 16)

                    def weights(it, i, b):
                        need(act, sum_mm, i - 1)
                        nc.scalar.activation(va[b][:, :, O1:F1], attn[:, bass.ds(i * (Q * H1), Q * H1)].rearrange(
                            "p (q h) -> p q h", h=H1), ACT.Copy).then_inc(ex_copied, 1)
                    pipelined(act, [(sums, 0), (weights, 2), (store, 0)])
                    for b in range(2):
                        act.wait_ge(rows_out[b], 16 * (NST // 2))

        ph = ExitStack()
        with ph:
            lrows = sb("lrows7", [P, 7, F1], F32, ph)
            last = sb("last7", [O1, 2, NTR], F32, ph)
            full = sb("full7", [O1, 2, NTR], F32, ph)
            cshift = sb("cshift7", [O1, 2, NTR], F32, ph)
            crows = sb("crows7", [P, 7, F1], F32, ph)
            own = sb("own7", [NP, NJ, F1], F32, ph)
            car = sb("car7", [NP, NJ, F1], F32, ph)
            updT = sb("updT", [O1, NJ * NP], F32, ph)
            o = sb("o", [NP, NJ, D], F32, ph)
            sq = sb("sq7", [NP, NJ, D], F32, ph)
            stat = sb("stat", [NP, 4, D], F32, ph)
            onesn = sb("onesn", [NP, NP], F32, ph)
            last_got, last_mm, last_out = sem("last7_got"), sem("last7_mm"), sem("last7_out")
            d7, c_mm, c_out, c_put = sem("dstep7"), sem("c7_mm"), sem("c7_out"), sem("c7_put")
            shift_ready, own_got, car_got, upd_ready = sem("shift7"), sem("own7_got"), sem("car7_got"), sem("upd_ready")
            t_mm, t_out, o_mm, o_out, ones7, part_ready, part_mm = (
                sem("t7_mm"), sem("t7_out"), sem("o7_mm"), sem("o7_out"), sem("ones7"), sem("part_ready"),
                sem("part_mm"))
            var7, std7, x_ready, out_sem = sem("var7"), sem("std7"), sem("x_ready"), sem("out_sem")
            groups4 = [(a, min(a + 4, NJ)) for a in range(0, NJ, 4)]
            groups8 = [(a, min(a + 8, NJ)) for a in range(0, NJ, 8)]

            with nc.Block() as block:
                @block.gpsimd
                def _(pool):
                    pool.memset(onesn[:, :], 1.0).then_inc(ones7, 1)
                    for j in range(NJ):
                        pool.indirect_dma_start(
                            own[:, j, :], None, sum1_edge,
                            bass.IndirectOffsetOnAxis(ap=last_i[:, j:j + 1], axis=0)).then_inc(own_got, 16)
                    pool.wait_ge(c_put, 16 * 7)
                    for j in range(NJ):
                        pool.indirect_dma_start(
                            car[:, j, :], None, carry1_tab,
                            bass.IndirectOffsetOnAxis(ap=tile_i[:, j:j + 1], axis=0)).then_inc(car_got, 16)

                @block.sync
                def _(sp):
                    load_last_rows(sp, lrows, sum1_edge, last_got)
                    for g, (a, b) in enumerate(c_groups):
                        sp.wait_ge(c_out, g + 1)
                        sp.dma_start(carry1_tab[a:b, :], crows[0:b - a, g, :]).then_inc(c_put, 16)
                    sp.wait_ge(c_put, 16 * 7)
                    sp.wait_ge(x_ready, 1)
                    sp.dma_start(out.rearrange("(p j) d -> p j d", j=NJ), xs[:, :, :]).then_inc(out_sem, 16)
                    sp.wait_ge(out_sem, 16)

                @block.tensor
                def _(pe):
                    transpose_last_rows(pe, lrows, F1, last_got, last_mm)
                    pe.wait_ge(shift_ready, 1)
                    for g, (a, b) in enumerate(c_groups):
                        need(pe, c_out, g - 1)
                        for k, (f0, f1) in enumerate(feature_parts(F1)):
                            f = slice(0, f1 - f0)
                            ins = nc.tensor.transpose(bank[g % 2][0:b - a, f0:f1], cshift[f, k, a:b], ident[f, f])
                        ins.then_inc(c_mm, 1)
                    pe.wait_ge(upd_ready, 1)
                    for g, (a, b) in enumerate(groups4):
                        need(pe, t_out, g - 1)
                        for j in range(a, b):
                            ins = nc.tensor.transpose(bank[2 + g % 2][:, (j - a) * NP:(j - a + 1) * NP],
                                                      own[:, j, 0:O1], ident[0:NP, 0:NP])
                        ins.then_inc(t_mm, 1)
                    pe.wait_ge(t_out, len(groups4))
                    for g, (a, b) in enumerate(groups8):
                        need(pe, o_out, g - 1)
                        for j in range(a, b):
                            r = bank[4 + g % 2][0:NP, (j - a) * D:(j - a + 1) * D]
                            nc.tensor.matmul(r, hT[0:D, j * NP:(j + 1) * NP], Wselfs[:, :], start=True, stop=False)
                            ins = nc.tensor.matmul(r, updT[:, j * NP:(j + 1) * NP], Wouts[:, :], start=False, stop=True)
                        ins.then_inc(o_mm, 1)
                    pe.wait_ge(ones7, 1)
                    for k in range(2):
                        pe.wait_ge(part_ready, k + 1)
                        nc.tensor.matmul(bank[6 + k][0:NP, 0:D], onesn[:, :], stat[:, k, :], start=True, stop=True)\
                                 .then_inc(part_mm, 1)

                @block.scalar
                def _(act):
                    copy_last(act, last, F1, last_mm, last_out)
                    for g, (a, b) in enumerate(c_groups):
                        act.wait_ge(c_mm, g + 1)
                        nc.scalar.activation(crows[0:b - a, g, :], bank[g % 2][0:b - a, 0:F1], ACT.Copy)\
                                 .then_inc(c_out, 1)
                    for g, (a, b) in enumerate(groups4):
                        act.wait_ge(t_mm, g + 1)
                        nc.scalar.activation(updT[:, a * NP:b * NP], bank[2 + g % 2][:, 0:(b - a) * NP],
                                             ACT.Copy).then_inc(t_out, 1)
                    for g, (a, b) in enumerate(groups8):
                        act.wait_ge(o_mm, g + 1)
                        nc.scalar.activation(o[:, a:b, :].rearrange("p a d -> p (a d)"),
                                             bank[4 + g % 2][0:NP, 0:(b - a) * D], ACT.Copy).then_inc(o_out, 1)
                    act.wait_ge(var7, 1)
                    nc.scalar.activation(stat[:, 3, :], stat[:, 2, :], ACT.Sqrt).then_inc(std7, 1)

                @block.vector
                def _(dve):
                    step = Chain(dve, d7)
                    carry_over(dve, step, last, full, cshift, F1, last_out)
                    dve.sem_inc(shift_ready, 1)
                    dve.wait_ge(own_got, 16 * NJ)
                    step(dve.tensor_tensor(own[:, :, :], own[:, :, :], bcast(has[:, :], 2, F1), ALU.mult))
                    dve.wait_ge(car_got, 16 * NJ)
                    step(dve.tensor_tensor(car[:, :, :], car[:, :, :], bcast(over[:, :], 2, F1), ALU.mult))
                    step(dve.tensor_tensor(own[:, :, :], own[:, :, :], car[:, :, :], ALU.add))
                    step(dve.tensor_scalar(own[:, :, O1:F1], own[:, :, O1:F1], 1e-16, None, ALU.add))
                    step(dve.reciprocal(car[:, :, O1:F1], own[:, :, O1:F1]))
                    for h in range(H1):
                        step(dve.tensor_tensor(own[:, :, h * DH:(h + 1) * DH], own[:, :, h * DH:(h + 1) * DH],
                                               car[:, :, O1 + h:O1 + h + 1].broadcast_to([NP, NJ, DH]), ALU.mult))
                    dve.sem_inc(upd_ready, 1)
                    dve.wait_ge(o_out, len(groups8))
                    dve.tensor_reduce(stat[:, 0, :], o[:, :, :].rearrange("p j d -> p d j"), AX.X, ALU.add)\
                       .then_inc(part_ready, 1)
                    dve.wait_ge(part_mm, 1)
                    step(dve.tensor_scalar(stat[:, 2, :], bank[6][0:NP, 0:D], 1.0 / N, None, ALU.mult))
                    step(dve.tensor_tensor(o[:, :, :], o[:, :, :], bcast(stat[:, 2, :], 1, NJ), ALU.subtract))
                    step(dve.tensor_tensor(sq[:, :, :], o[:, :, :], o[:, :, :], ALU.mult))
                    dve.tensor_reduce(stat[:, 1, :], sq[:, :, :].rearrange("p j d -> p d j"), AX.X, ALU.add)\
                       .then_inc(part_ready, 1)
                    dve.wait_ge(part_mm, 2)
                    dve.tensor_scalar(stat[:, 2, :], bank[7][0:NP, 0:D], 1.0 / N, BN_EPS, ALU.mult, ALU.add)\
                       .then_inc(var7, 1)
                    dve.wait_ge(std7, 1)
                    step(dve.reciprocal(stat[:, 2, :], stat[:, 3, :]))
                    step(dve.tensor_tensor(stat[:, 2, :], stat[:, 2, :], g1b[:, :], ALU.mult))
                    step(dve.tensor_tensor(o[:, :, :], o[:, :, :], bcast(stat[:, 2, :], 1, NJ), ALU.mult))
                    step(dve.tensor_tensor(o[:, :, :], o[:, :, :], bcast(be1b[:, :], 1, NJ), ALU.add))
                    dve.tensor_tensor(xs[:, :, :], xs[:, :, :], o[:, :, :], ALU.add).then_inc(x_ready, 1)


_INS = ["x", "src", "dst", "edge_attr_64", "edge_attr_9", "L0_gnn_Wq", "L0_gnn_bq", "L0_gnn_Wk", "L0_gnn_bk",
        "L0_gnn_Wv", "L0_gnn_bv", "L0_gnn_Wo", "L0_gnn_bo", "L0_gnn_Wf", "L0_gnn_bf", "L0_gnn_gamma",
        "L0_gnn_beta", "L1_gnn_Wq", "L1_gnn_Cqk", "L1_gnn_Cv", "L1_gnn_k_w1", "L1_gnn_k_b1", "L1_gnn_k_w2",
        "L1_gnn_k_b2", "L1_gnn_v_w1", "L1_gnn_v_b1", "L1_gnn_v_w2", "L1_gnn_v_b2", "L1_gnn_W_out",
        "L1_gnn_W_self", "L1_gnn_gamma", "L1_gnn_beta"]


def kernel(**inputs):
    import numpy as np
    import concourse.bacc as bacc
    from concourse.bass_utils import run_bass_kernel_spmd

    nc = bacc.Bacc("TRN2", target_bir_lowering=False, num_devices=1)
    arrays, args = {}, []
    for name in _INS:
        a = np.ascontiguousarray(inputs[name])
        arrays[f"in_{name}"] = a
        args.append(nc.dram_tensor(f"in_{name}", a.shape, mybir.dt.from_np(a.dtype), kind="ExternalInput").ap())
    out = nc.dram_tensor("out", (N, D), F32, kind="ExternalOutput").ap()
    gnn(nc, *args, out)
    return run_bass_kernel_spmd(nc, [arrays], core_ids=[0]).results[0]["out"]
```
